# Optimizing a Trainium2 kernel written in Bass

```python
import numpy as np
import jax
import jax.numpy as jnp

def _softmax(x, axis=-1):
    return jax.nn.softmax(x, axis=axis)

def _gelu(x):
    return jax.nn.gelu(x, approximate=True)

def _silu(x):
    return jax.nn.silu(x)

def _sigmoid(x):
    return jax.nn.sigmoid(x)

def _layernorm(x, axis=-1, eps=1e-05):
    m = jnp.mean(x, axis=axis, keepdims=True)
    v = jnp.var(x, axis=axis, keepdims=True)
    return (x - m) / jnp.sqrt(v + eps)

def _scatter_add(tgt, idx, src, axis=0):
    return tgt.at[idx].add(src)

def _segment_sum(src, seg, n):
    return jax.ops.segment_sum(src, seg, n)
kernel_name = 'mk_xattn_ffn_d4_seqx_r8_e36f10'

def setup_inputs(seed: int=0):
    np.random.seed(seed)
    _w = jnp.asarray

    def _rec_inputs():
        import jax
        import jax.numpy as jnp
        _rk = jax.random.key(seed)
        x = -0.0005207 + 1.001 * jax.random.normal(jax.random.fold_in(_rk, 1), (4, 256, 512), jnp.float32)
        _lenS = 256 - jax.random.randint(jax.random.fold_in(_rk, 7), (4,), 0, max(1, 256 // 4) + 1, jnp.int32)
        _lenS2 = 64 - jax.random.randint(jax.random.fold_in(_rk, 8), (4,), 0, max(1, 64 // 4) + 1, jnp.int32)
        _ctx_4096P = jax.random.normal(jax.random.fold_in(_rk, 11), (4, 16, 512), jnp.float32)
        _ctx_4096c = jax.random.dirichlet(jax.random.fold_in(_rk, 511), 0.3 * jnp.ones((16,), jnp.float32), (4, 64))
        _ctx_4096t = jnp.einsum('bsk,bkd->bsd', _ctx_4096c, _ctx_4096P)
        _ctx_4096t = _ctx_4096t * jax.lax.rsqrt(jnp.mean(jnp.square(_ctx_4096t)) + 1e-12) * 0.953939
        ctx_4096 = -0.00010331 + 0.999899 * (_ctx_4096t + 0.3 * jax.random.normal(jax.random.fold_in(_rk, 611), (4, 64, 512), jnp.float32))
        return (x, ctx_4096)
    x, ctx_4096 = _rec_inputs()

    def _L0_xattn_setup():
        import jax, jax.numpy as jnp
        import numpy as np
        B, Q, D = (8, 64, 512)
        CTX = 512
        H, KV, HD = (16, 4, 96)
        G = H // KV
        key = jax.random.key(seed)
        ks = jax.random.split(key, 6)
        s = 0.02
        return {'latents': jax.random.normal(ks[0], (B, Q, D), jnp.float32), 'context': jax.random.normal(ks[1], (B, CTX, D), jnp.float32), 'Wq': jax.random.normal(ks[2], (H * HD, D), jnp.float32) * s, 'Wk': jax.random.normal(ks[3], (KV * HD, D), jnp.float32) * s, 'Wv': jax.random.normal(ks[4], (KV * HD, D), jnp.float32) * s, 'Wo': jax.random.normal(ks[5], (D, H * HD), jnp.float32) * s}
    _L0_xattn_all = _L0_xattn_setup()
    _L0_xattn_in = {k: v for k, v in _L0_xattn_all.items() if k in ('Wq', 'Wk', 'Wv', 'Wo')}
    del _L0_xattn_all

    def _L0_ffn_setup():
        import jax, jax.numpy as jnp
        import numpy as np
        HIDDEN = 512
        INTER = 1376

        def _ternary_quantize(w):
            scale = jnp.mean(jnp.abs(w))
            return jnp.clip(jnp.round(w / scale), -1.0, 1.0) * scale
        key = jax.random.key(seed)
        kx, kg, ku, kd = jax.random.split(key, 4)
        x = jax.random.normal(kx, (2, 256, HIDDEN), dtype=jnp.float32)
        w_gate = _ternary_quantize(jax.random.normal(kg, (INTER, HIDDEN), dtype=jnp.float32) * 0.02)
        w_up = _ternary_quantize(jax.random.normal(ku, (INTER, HIDDEN), dtype=jnp.float32) * 0.02)
        w_down = _ternary_quantize(jax.random.normal(kd, (HIDDEN, INTER), dtype=jnp.float32) * 0.02)
        return {'x': x, 'w_gate': w_gate, 'w_up': w_up, 'w_down': w_down}
    _L0_ffn_all = _L0_ffn_setup()
    _L0_ffn_in = {k: v for k, v in _L0_ffn_all.items() if k in ('w_gate', 'w_up', 'w_down')}
    del _L0_ffn_all

    def _L1_xattn_setup():
        import jax, jax.numpy as jnp
        import numpy as np
        key = jax.random.key(seed)
        k1, k2 = jax.random.split(key)
        B, Lq, Lk, D = (16, 128, 256, 512)
        query = jax.random.normal(k1, (B, Lq, D), dtype=jnp.float32)
        key_t = jax.random.normal(k2, (B, Lk, D), dtype=jnp.float32)
        return {'query': query, 'key': key_t}
    _L1_xattn_all = _L1_xattn_setup()
    _L1_xattn_in = {k: v for k, v in _L1_xattn_all.items() if k in ()}
    del _L1_xattn_all

    def _L1_ffn_setup():
        import jax, jax.numpy as jnp
        import numpy as np
        IN_F = 512
        OUT_F = 512
        RANK = 8
        NUM_EXPERTS = 64
        TOP_K = 16
        ROUTER_DIM = 16
        ALPHA = 32
        SCALING = ALPHA / TOP_K
        BOTTLENECK = NUM_EXPERTS * RANK
        key = jax.random.key(seed)
        ks = jax.random.split(key, 5)
        x = jax.random.normal(ks[0], (4, 512, IN_F), dtype=jnp.float32)
        bound_a = float(np.sqrt(6.0 / IN_F))
        A_w = jax.random.uniform(ks[1], (BOTTLENECK, IN_F), jnp.float32, -bound_a, bound_a)
        B_w = jax.random.normal(ks[2], (OUT_F, BOTTLENECK), dtype=jnp.float32) * 0.02
        Wq_w = jax.random.normal(ks[3], (ROUTER_DIM, IN_F), dtype=jnp.float32) * 0.02
        keys = jax.random.normal(ks[4], (NUM_EXPERTS, ROUTER_DIM), dtype=jnp.float32) * 0.01
        return {'x': x, 'A_w': A_w, 'B_w': B_w, 'Wq_w': Wq_w, 'keys': keys}
    _L1_ffn_all = _L1_ffn_setup()
    _L1_ffn_in = {k: v for k, v in _L1_ffn_all.items() if k in ('A_w', 'B_w', 'Wq_w', 'keys')}
    del _L1_ffn_all

    def _L2_xattn_setup():
        import jax, jax.numpy as jnp
        import numpy as np
        TEXT_DIM = 512
        FEATURE_DIM = 512

        def _xavier_uniform(key, shape):
            fan_in, fan_out = (shape[1], shape[0])
            limit = float(np.sqrt(6.0 / (fan_in + fan_out)))
            return jax.random.uniform(key, shape, jnp.float32, -limit, limit)
        key = jax.random.key(seed)
        k1, k2, k3, k4 = jax.random.split(key, 4)
        text = jax.random.normal(k1, (8, 256, TEXT_DIM), jnp.float32)
        features = jax.random.normal(k2, (8, 72, FEATURE_DIM), jnp.float32)
        Wq = _xavier_uniform(k3, (FEATURE_DIM, TEXT_DIM))
        bq = jnp.zeros((FEATURE_DIM,), jnp.float32)
        Wk = _xavier_uniform(k4, (FEATURE_DIM, FEATURE_DIM))
        bk = jnp.zeros((FEATURE_DIM,), jnp.float32)
        return {'text': text, 'features': features, 'Wq': Wq, 'bq': bq, 'Wk': Wk, 'bk': bk}
    _L2_xattn_all = _L2_xattn_setup()
    _L2_xattn_in = {k: v for k, v in _L2_xattn_all.items() if k in ('Wq', 'bq', 'Wk', 'bk')}
    del _L2_xattn_all

    def _L2_ffn_setup():
        import jax, jax.numpy as jnp
        import numpy as np
        B, S, D = (4, 256, 512)
        NUM_EXPERTS, TOP_K = (3, 2)

        def _expert_outputs(h, w1, b1, w2, b2):
            pre = jnp.einsum('bsd,edf->ebsf', h, w1) + b1[:, None, None, :]
            act = jnp.stack([jnp.tanh(pre[0]), jax.nn.gelu(pre[1], approximate=False), jax.nn.silu(pre[2])])
            return jnp.einsum('ebsf,efd->ebsd', act, w2) + b2[:, None, None, :]
        key = jax.random.key(seed)
        ks = jax.random.split(key, 8)
        scale_in = 1.0 / np.sqrt(D)
        scale_gate = 1.0 / np.sqrt(D + 1)
        return {'h': jax.random.normal(ks[0], (B, S, D), dtype=jnp.float32), 'gate_w': jax.random.uniform(ks[1], (D + 1, NUM_EXPERTS), minval=-scale_gate, maxval=scale_gate, dtype=jnp.float32), 'gate_b': jnp.zeros((NUM_EXPERTS,), dtype=jnp.float32), 'w1': jax.random.uniform(ks[2], (NUM_EXPERTS, D, D), minval=-scale_in, maxval=scale_in, dtype=jnp.float32), 'b1': jnp.zeros((NUM_EXPERTS, D), dtype=jnp.float32), 'w2': jax.random.uniform(ks[3], (NUM_EXPERTS, D, D), minval=-scale_in, maxval=scale_in, dtype=jnp.float32), 'b2': jnp.zeros((NUM_EXPERTS, D), dtype=jnp.float32)}
    _L2_ffn_all = _L2_ffn_setup()
    _L2_ffn_in = {k: v for k, v in _L2_ffn_all.items() if k in ('gate_w', 'gate_b', 'w1', 'b1', 'w2', 'b2')}
    del _L2_ffn_all

    def _L3_xattn_setup():
        import jax, jax.numpy as jnp
        import numpy as np
        HIDDEN = 512
        N_HEADS = 32
        N_KV_HEADS = 8
        HEAD_DIM = HIDDEN // N_HEADS
        N_REP = N_HEADS // N_KV_HEADS
        EPS = 1e-05

        def _rmsnorm(x, w):
            xf = x.astype(jnp.float32)
            var = jnp.mean(xf * xf, axis=-1, keepdims=True)
            return (xf * jax.lax.rsqrt(var + EPS)).astype(x.dtype) * w
        key = jax.random.key(seed)
        ks = jax.random.split(key, 7)
        B, Q, K = (2, 128, 256)
        scale = 0.02
        return {'hidden_states': jax.random.normal(ks[0], (B, Q, HIDDEN), jnp.float32), 'encoder_hidden_states': jax.random.normal(ks[1], (B, K, HIDDEN), jnp.float32), 'wq': jax.random.normal(ks[2], (N_HEADS * HEAD_DIM, HIDDEN), jnp.float32) * scale, 'wk': jax.random.normal(ks[3], (N_KV_HEADS * HEAD_DIM, HIDDEN), jnp.float32) * scale, 'wv': jax.random.normal(ks[4], (N_KV_HEADS * HEAD_DIM, HIDDEN), jnp.float32) * scale, 'wo': jax.random.normal(ks[5], (HIDDEN, N_HEADS * HEAD_DIM), jnp.float32) * scale, 'ln_w': jnp.ones((HIDDEN,), jnp.float32)}
    _L3_xattn_all = _L3_xattn_setup()
    _L3_xattn_in = {k: v for k, v in _L3_xattn_all.items() if k in ('wq', 'wk', 'wv', 'wo', 'ln_w')}
    del _L3_xattn_all

    def _L3_ffn_setup():
        import jax, jax.numpy as jnp
        import numpy as np
        NF4_CODE = jnp.array([-1.0, -0.6961928009986877, -0.5250730514526367, -0.39491748809814453, -0.28444138169288635, -0.18477343022823334, -0.09105003625154495, 0.0, 0.07958029955625534, 0.16093020141124725, 0.24611230194568634, 0.33791524171829224, 0.44070982933044434, 0.5626170039176941, 0.7229568362236023, 1.0], dtype=jnp.float32)
        BLOCKSIZE = 64

        def nf4_quant_dequant(w):
            shape = w.shape
            flat = w.reshape(-1, BLOCKSIZE)
            absmax = jnp.max(jnp.abs(flat), axis=1, keepdims=True)
            normalized = flat / jnp.where(absmax == 0, 1.0, absmax)
            bounds = (NF4_CODE[:-1] + NF4_CODE[1:]) * 0.5
            idx = jnp.searchsorted(bounds, normalized)
            return (NF4_CODE[idx] * absmax).reshape(shape)
        key = jax.random.key(seed)
        k1, k2, k3, kx = jax.random.split(key, 4)
        D, H = (512, 1376)
        scale = 0.02
        w1 = jax.random.normal(k1, (H, D), jnp.float32) * scale
        w2 = jax.random.normal(k2, (H, D), jnp.float32) * scale
        w3 = jax.random.normal(k3, (D, H), jnp.float32) * scale
        x = jax.random.normal(kx, (2, 256, D), jnp.float32)
        return {'x': x, 'w1': w1, 'w2': w2, 'w3': w3}
    _L3_ffn_all = _L3_ffn_setup()
    _L3_ffn_in = {k: v for k, v in _L3_ffn_all.items() if k in ('w1', 'w2', 'w3')}
    del _L3_ffn_all
    return {'x': x, 'ctx_4096': ctx_4096, 'L0_xattn_Wq': _L0_xattn_in['Wq'], 'L0_xattn_Wk': _L0_xattn_in['Wk'], 'L0_xattn_Wv': _L0_xattn_in['Wv'], 'L0_xattn_Wo': _L0_xattn_in['Wo'], 'L0_ffn_w_gate': _L0_ffn_in['w_gate'], 'L0_ffn_w_up': _L0_ffn_in['w_up'], 'L0_ffn_w_down': _L0_ffn_in['w_down'], 'L1_ffn_A_w': _L1_ffn_in['A_w'], 'L1_ffn_B_w': _L1_ffn_in['B_w'], 'L1_ffn_Wq_w': _L1_ffn_in['Wq_w'], 'L1_ffn_keys': _L1_ffn_in['keys'], 'L2_xattn_Wq': _L2_xattn_in['Wq'], 'L2_xattn_bq': _L2_xattn_in['bq'], 'L2_xattn_Wk': _L2_xattn_in['Wk'], 'L2_xattn_bk': _L2_xattn_in['bk'], 'L2_ffn_gate_w': _L2_ffn_in['gate_w'], 'L2_ffn_gate_b': _L2_ffn_in['gate_b'], 'L2_ffn_w1': _L2_ffn_in['w1'], 'L2_ffn_b1': _L2_ffn_in['b1'], 'L2_ffn_w2': _L2_ffn_in['w2'], 'L2_ffn_b2': _L2_ffn_in['b2'], 'L3_xattn_wq': _L3_xattn_in['wq'], 'L3_xattn_wk': _L3_xattn_in['wk'], 'L3_xattn_wv': _L3_xattn_in['wv'], 'L3_xattn_wo': _L3_xattn_in['wo'], 'L3_xattn_ln_w': _L3_xattn_in['ln_w'], 'L3_ffn_w1': _L3_ffn_in['w1'], 'L3_ffn_w2': _L3_ffn_in['w2'], 'L3_ffn_w3': _L3_ffn_in['w3']}

def reference(x, ctx_4096, L0_xattn_Wq, L0_xattn_Wk, L0_xattn_Wv, L0_xattn_Wo, L0_ffn_w_gate, L0_ffn_w_up, L0_ffn_w_down, L1_ffn_A_w, L1_ffn_B_w, L1_ffn_Wq_w, L1_ffn_keys, L2_xattn_Wq, L2_xattn_bq, L2_xattn_Wk, L2_xattn_bk, L2_ffn_gate_w, L2_ffn_gate_b, L2_ffn_w1, L2_ffn_b1, L2_ffn_w2, L2_ffn_b2, L3_xattn_wq, L3_xattn_wk, L3_xattn_wv, L3_xattn_wo, L3_xattn_ln_w, L3_ffn_w1, L3_ffn_w2, L3_ffn_w3):
    import jax
    import jax.numpy as jnp

    def _L0_xattn_ref(latents, context, Wq, Wk, Wv, Wo):
        import jax, jax.numpy as jnp
        import numpy as np
        B, Q, D = (8, 64, 512)
        CTX = 512
        H, KV, HD = (16, 4, 96)
        G = H // KV
        b, q_len, _ = latents.shape
        hidden = jnp.concatenate([context, latents], axis=1)
        s_len = hidden.shape[1]
        q = (latents @ Wq.T).reshape(b, q_len, H, HD)
        k = (hidden @ Wk.T).reshape(b, s_len, KV, HD)
        v = (hidden @ Wv.T).reshape(b, s_len, KV, HD)
        q = q.transpose(0, 2, 1, 3).reshape(b, KV, G, q_len, HD)
        k = k.transpose(0, 2, 1, 3)
        v = v.transpose(0, 2, 1, 3)
        scale = 1.0 / jnp.sqrt(jnp.asarray(HD, q.dtype))
        scores = jnp.einsum('bkgqd,bksd->bkgqs', q, k) * scale
        attn = jax.nn.softmax(scores.astype(jnp.float32), axis=-1).astype(q.dtype)
        out = jnp.einsum('bkgqs,bksd->bkgqd', attn, v)
        out = out.reshape(b, H, q_len, HD).transpose(0, 2, 1, 3).reshape(b, q_len, H * HD)
        return out @ Wo.T

    def _L0_ffn_ref(x, w_gate, w_up, w_down):
        import jax, jax.numpy as jnp
        import numpy as np
        HIDDEN = 512
        INTER = 1376

        def _ternary_quantize(w):
            scale = jnp.mean(jnp.abs(w))
            return jnp.clip(jnp.round(w / scale), -1.0, 1.0) * scale
        xf = x.astype(jnp.float32) / 128.0
        gate = jnp.einsum('bsh,ih->bsi', xf, w_gate)
        up = jnp.einsum('bsh,ih->bsi', xf, w_up)
        inter = jax.nn.silu(gate) * up
        inter_q = jnp.trunc(jnp.clip(inter * 128.0, -128.0, 127.0)).astype(jnp.int8)
        down = jnp.einsum('bsi,hi->bsh', inter_q.astype(jnp.float32), w_down)
        out = jnp.trunc(jnp.clip(down * 128.0, -128.0, 127.0)).astype(jnp.int8)
        return out

    def _L1_xattn_ref(query, key):
        import jax, jax.numpy as jnp
        import numpy as np
        a = jnp.einsum('bqd,bkd->bqk', query, key)
        e = jax.nn.softmax(a, axis=-1)
        c = jnp.einsum('bqk,bkd->bqd', e, key)
        return c

    def _L1_ffn_ref(x, A_w, B_w, Wq_w, keys):
        import jax, jax.numpy as jnp
        import numpy as np
        IN_F = 512
        OUT_F = 512
        RANK = 8
        NUM_EXPERTS = 64
        TOP_K = 16
        ROUTER_DIM = 16
        ALPHA = 32
        SCALING = ALPHA / TOP_K
        BOTTLENECK = NUM_EXPERTS * RANK
        q = jnp.einsum('bsd,rd->bsr', x, Wq_w)
        scores = jnp.einsum('bsr,er->bse', q, keys)
        top_vals, top_idx = jax.lax.top_k(scores, TOP_K)
        top_w = jax.nn.softmax(top_vals, axis=-1)
        gate = jnp.sum(jax.nn.one_hot(top_idx, NUM_EXPERTS, dtype=top_w.dtype) * top_w[..., None], axis=-2)
        z = jnp.einsum('bsd,nd->bsn', x, A_w)
        z = z.reshape(*z.shape[:-1], NUM_EXPERTS, RANK)
        z_gated = (z * gate[..., None]).reshape(*z.shape[:-2], BOTTLENECK)
        out = jnp.einsum('bsn,on->bso', z_gated, B_w) * SCALING
        return out

    def _L2_xattn_ref(text, features, Wq, bq, Wk, bk):
        import jax, jax.numpy as jnp
        import numpy as np
        TEXT_DIM = 512
        FEATURE_DIM = 512

        def _xavier_uniform(key, shape):
            fan_in, fan_out = (shape[1], shape[0])
            limit = float(np.sqrt(6.0 / (fan_in + fan_out)))
            return jax.random.uniform(key, shape, jnp.float32, -limit, limit)
        Q = jnp.einsum('btx,dx->btd', text, Wq) + bq
        K = jnp.einsum('bpx,dx->bpd', features, Wk) + bk
        scale = 1.0 / jnp.sqrt(jnp.asarray(K.shape[-1], K.dtype))
        scores = jnp.einsum('btd,bpd->btp', Q, K) * scale
        attn = jax.nn.softmax(scores, axis=-1)
        attended = jnp.einsum('btp,bpd->btd', attn, features)
        return attended

    def _L2_ffn_ref(h, gate_w, gate_b, w1, b1, w2, b2):
        import jax, jax.numpy as jnp
        import numpy as np
        B, S, D = (4, 256, 512)
        NUM_EXPERTS, TOP_K = (3, 2)

        def _expert_outputs(h, w1, b1, w2, b2):
            pre = jnp.einsum('bsd,edf->ebsf', h, w1) + b1[:, None, None, :]
            act = jnp.stack([jnp.tanh(pre[0]), jax.nn.gelu(pre[1], approximate=False), jax.nn.silu(pre[2])])
            return jnp.einsum('ebsf,efd->ebsd', act, w2) + b2[:, None, None, :]
        b, s, d = h.shape
        vision_len = int(s * 0.3)
        text_strength = jnp.mean(jnp.abs(h[:, vision_len:, :]), axis=(1, 2), keepdims=True)
        vision_strength = jnp.mean(jnp.abs(h[:, :vision_len, :]), axis=(1, 2), keepdims=True)
        modality_ratio = text_strength / (vision_strength + 1e-08)
        modality_ratio = jnp.broadcast_to(modality_ratio, (b, s, 1))
        router_input = jnp.concatenate([h, modality_ratio], axis=-1)
        gate_logits = router_input @ gate_w + gate_b
        gate_scores = jax.nn.softmax(gate_logits, axis=-1)
        top_val, top_idx = jax.lax.top_k(gate_scores, TOP_K)
        top_val = top_val / (jnp.sum(top_val, axis=-1, keepdims=True) + 1e-08)
        expert_out = _expert_outputs(h, w1, b1, w2, b2)
        moe_out = jnp.zeros_like(h)
        batch_idx = jnp.arange(b)
        for i in range(TOP_K):
            j = top_idx[:, 0, i]
            out_i = expert_out[j, batch_idx]
            moe_out = moe_out + top_val[..., i:i + 1] * out_i
        return moe_out

    def _L3_xattn_ref(hidden_states, encoder_hidden_states, wq, wk, wv, wo, ln_w):
        import jax, jax.numpy as jnp
        import numpy as np
        HIDDEN = 512
        N_HEADS = 32
        N_KV_HEADS = 8
        HEAD_DIM = HIDDEN // N_HEADS
        N_REP = N_HEADS // N_KV_HEADS
        EPS = 1e-05

        def _rmsnorm(x, w):
            xf = x.astype(jnp.float32)
            var = jnp.mean(xf * xf, axis=-1, keepdims=True)
            return (xf * jax.lax.rsqrt(var + EPS)).astype(x.dtype) * w
        B, Qlen, _ = hidden_states.shape
        _, Klen, _ = encoder_hidden_states.shape
        x = _rmsnorm(hidden_states, ln_w)
        q = jnp.einsum('bqd,hd->bqh', x, wq).reshape(B, Qlen, N_HEADS, HEAD_DIM)
        k = jnp.einsum('bkd,hd->bkh', encoder_hidden_states, wk).reshape(B, Klen, N_KV_HEADS, HEAD_DIM)
        v = jnp.einsum('bkd,hd->bkh', encoder_hidden_states, wv).reshape(B, Klen, N_KV_HEADS, HEAD_DIM)
        q = q.transpose(0, 2, 1, 3)
        k = k.transpose(0, 2, 1, 3)
        v = v.transpose(0, 2, 1, 3)
        k = jnp.repeat(k, N_REP, axis=1)
        v = jnp.repeat(v, N_REP, axis=1)
        scores = jnp.einsum('bhqd,bhkd->bhqk', q, k) / np.sqrt(HEAD_DIM).astype(np.float32)
        attn = jax.nn.softmax(scores.astype(jnp.float32), axis=-1).astype(q.dtype)
        out = jnp.einsum('bhqk,bhkd->bhqd', attn, v)
        out = out.transpose(0, 2, 1, 3).reshape(B, Qlen, HIDDEN)
        return jnp.einsum('bqh,dh->bqd', out, wo)

    def _L3_ffn_ref(x, w1, w2, w3):
        import jax, jax.numpy as jnp
        import numpy as np
        NF4_CODE = jnp.array([-1.0, -0.6961928009986877, -0.5250730514526367, -0.39491748809814453, -0.28444138169288635, -0.18477343022823334, -0.09105003625154495, 0.0, 0.07958029955625534, 0.16093020141124725, 0.24611230194568634, 0.33791524171829224, 0.44070982933044434, 0.5626170039176941, 0.7229568362236023, 1.0], dtype=jnp.float32)
        BLOCKSIZE = 64

        def nf4_quant_dequant(w):
            shape = w.shape
            flat = w.reshape(-1, BLOCKSIZE)
            absmax = jnp.max(jnp.abs(flat), axis=1, keepdims=True)
            normalized = flat / jnp.where(absmax == 0, 1.0, absmax)
            bounds = (NF4_CODE[:-1] + NF4_CODE[1:]) * 0.5
            idx = jnp.searchsorted(bounds, normalized)
            return (NF4_CODE[idx] * absmax).reshape(shape)
        dq1 = nf4_quant_dequant(w1)
        dq2 = nf4_quant_dequant(w2)
        dq3 = nf4_quant_dequant(w3)
        gate = jnp.einsum('bsd,hd->bsh', x, dq1)
        up = jnp.einsum('bsd,hd->bsh', x, dq2)
        h = jax.nn.silu(gate) * up
        return jnp.einsum('bsh,dh->bsd', h, dq3)
    x = x + _L0_xattn_ref(_layernorm(x, axis=-1), ctx_4096, L0_xattn_Wq, L0_xattn_Wk, L0_xattn_Wv, L0_xattn_Wo)
    x = x + _L0_ffn_ref(_layernorm(x, axis=-1), L0_ffn_w_gate, L0_ffn_w_up, L0_ffn_w_down)
    x = x + _L1_xattn_ref(_layernorm(x, axis=-1), ctx_4096)
    x = x + _L1_ffn_ref(_layernorm(x, axis=-1), L1_ffn_A_w, L1_ffn_B_w, L1_ffn_Wq_w, L1_ffn_keys)
    x = x + _L2_xattn_ref(_layernorm(x, axis=-1), ctx_4096, L2_xattn_Wq, L2_xattn_bq, L2_xattn_Wk, L2_xattn_bk)
    x = x + _L2_ffn_ref(_layernorm(x, axis=-1), L2_ffn_gate_w, L2_ffn_gate_b, L2_ffn_w1, L2_ffn_b1, L2_ffn_w2, L2_ffn_b2)
    x = x + _L3_xattn_ref(_layernorm(x, axis=-1), ctx_4096, L3_xattn_wq, L3_xattn_wk, L3_xattn_wv, L3_xattn_wo, L3_xattn_ln_w)
    x = x + _L3_ffn_ref(_layernorm(x, axis=-1), L3_ffn_w1, L3_ffn_w2, L3_ffn_w3)
    return x

_drawn_inputs = setup_inputs


def setup_inputs(seed=0):
    import zlib

    import numpy as np

    out = dict(_drawn_inputs(seed))
    spreads = {'L2_xattn_bq': (0.0, 0.682),
     'L2_xattn_bk': (0.0, 0.8),
     'L2_ffn_gate_b': (0.0, 0.8),
     'L2_ffn_b1': (0.0, 0.516),
     'L2_ffn_b2': (0.0, 0.1),
     'L3_xattn_ln_w': (1.0, 0.6)}
    factors = {'L0_xattn_Wq': 4.823, 'L0_xattn_Wk': 4.594, 'L3_xattn_wq': 8.0, 'L3_xattn_wk': 8.0}
    for name, (base, spread) in spreads.items():
        noise = np.random.default_rng([zlib.crc32(name.encode()), seed]).standard_normal(out[name].shape)
        drawn = base * np.exp(spread * noise) if base else spread * noise
        out[name] = jnp.asarray(drawn.astype(out[name].dtype))
    for name, factor in factors.items():
        out[name] = (out[name] * factor).astype(out[name].dtype)
    return out
```

```python
import concourse.bass as bass
from concourse import mybir
from contextlib import ExitStack
import numpy as np

FP32 = mybir.dt.float32
F32R = mybir.dt.float32r
INT32 = mybir.dt.int32
ALU = mybir.AluOpType
ACT = mybir.ActivationFunctionType
AX = mybir.AxisListType

P = 128
B, S, D = 4, 256, 512
CTX = 64
TOK = B * S
TILES = TOK // P
KT = D // P
HALF = TOK // 2
TPH = TILES // 2
BPH = B // 2
TPB = S // P
H0, G0, HD0 = 16, 4, 96
HPG = H0 // G0
KEYS0 = S + CTX
F = 1376
FT = (F + P - 1) // P
NE, RANK, TOPK = 64, 8, 16
ROUT = 16
VISION = int(S * 0.3)
MOE = 3
H3, KV3, HD3 = 32, 8, 16
HPC = P // HD3
REP3 = H3 // KV3
PAIRS = HPC // 2
LN_EPS = 1e-5
BLOCK = 64
CODE = np.array([-1.0, -0.6961928009986877, -0.5250730514526367, -0.39491748809814453, -0.28444138169288635,
                 -0.18477343022823334, -0.09105003625154495, 0.0, 0.07958029955625534, 0.16093020141124725,
                 0.24611230194568634, 0.33791524171829224, 0.44070982933044434, 0.5626170039176941,
                 0.7229568362236023, 1.0], dtype=np.float32)
BOUNDS = (CODE[:-1] + CODE[1:]) * np.float32(0.5)
SLOT = 1024
NSLOT = 5
TINY = 1.1754944e-38
ROUND = float(2 ** 23)


def code_steps():
    steps = []
    for low, high in zip(CODE[:-1], CODE[1:]):
        d = np.float32(high - low)
        for c in (d, np.nextafter(d, np.float32(9)), np.nextafter(d, np.float32(-9))):
            if np.float32(low + c) == high:
                d = c
                break
        assert np.float32(low + d) == high
        steps.append(float(d))
    return steps


CODE_STEPS = code_steps()


def fwidth(f):
    return min(P, F - f * P)



def schedule(only=None):
    steps = []

    def layer_norm_0(layer):
        return [("stats", layer, 0)], [("turn", layer, 0), ("stats", layer, 1)], [("turn", layer, 1)]

    a, b, c = layer_norm_0(0)
    steps += a + b + c
    steps += [("v0", t) for t in range(TILES + B)]
    steps += [("k0", 0), ("kc0", 0)] + [("q0", 0, h) for h in range(HPG)]
    units = [(s, bl, h) for s in range(2 * G0) for h in range(HPG) for bl in range(BPH)]
    for n in range(len(units) + 2):
        if n < len(units):
            steps.append(("scores0", n, *units[n]))
        if 1 <= n <= len(units):
            steps.append(("turn0", n - 1, *units[n - 1]))
        if n >= 2:
            steps.append(("pv0", n - 2, *units[n - 2]))
        if n < len(units):
            s, j = n // 8, n % 8
            if s + 1 < 2 * G0:
                if j == 0:
                    steps.append(("k0", s + 1))
                if j == 1:
                    steps.append(("kc0", s + 1))
            if s >= 1 and j in (3, 4):
                steps += [("o0", s - 1, i) for i in (2 * j - 6, 2 * j - 5)]
            if s + 1 < 2 * G0 and j >= 5:
                steps += [("q0", s + 1, h) for h in ((0, 1), (2,), (3,))[j - 5]]
            if s == 2 * G0 - 1 and j == 5:
                steps.append(("stats", 1, 0))
    steps += [("o0", 2 * G0 - 1, i) for i in range(2)] + [("turn", 1, 0)]
    steps += [("o0", 2 * G0 - 1, i) for i in range(2, TPH)] + [("stats", 1, 1)]
    if only == 1:
        return steps
    half_f = (FT + 1) // 2
    steps += [("up0", 0, 0), ("turn", 1, 1), ("up0", 0, 1)]
    steps += [("up0", f, hf) for f in range(1, half_f) for hf in range(2)]
    steps += [("down0", 0, t) for t in range(TILES)]
    steps += [("up0", f, hf) for f in range(half_f, FT) for hf in range(2)]
    steps += [("down0", 1, t) for t in range(TPH)] + [("stats", 2, 0)]
    steps += [("down0", 1, t) for t in range(TPH, TILES)] + [("turn", 2, 0), ("stats", 2, 1)]
    if only == 2:
        return steps
    steps += [("scores1", 1, 0), ("scores1", 1, 1), ("turn", 2, 1), ("pv1", 1, 0), ("scores1", 1, 2),
              ("pv1", 1, 1), ("stats", 3, 0), ("scores1", 1, 3), ("pv1", 1, 2), ("turn", 3, 0), ("pv1", 1, 3),
              ("stats", 3, 1)]
    if only == 3:
        return steps
    steps += [("router1",)] + [("route1", t) for t in range(TPH)] + [("turn", 3, 1)]
    steps += [("z1", 0)] + [("route1", t) for t in range(TPH, TILES)]
    for t in range(TILES):
        if t + 1 < TILES:
            steps.append(("z1", t + 1))
        steps.append(("zt1", t))
        if t >= 1:
            steps.append(("b1", t - 1))
        if t - 1 == TPH - 1:
            steps.append(("stats", 4, 0))
    steps += [("b1", TILES - 1), ("turn", 4, 0), ("stats", 4, 1)]
    if only == 4:
        return steps
    steps += [("k2", c) for c in range(KT)] + [("m2", c) for c in range(KT)] + [("c2",)]
    steps += [("scores1", 2, 0), ("scores1", 2, 1), ("turn", 4, 1), ("pv1", 2, 0), ("scores1", 2, 2),
              ("pv1", 2, 1), ("stats", 5, 0), ("scores1", 2, 3), ("pv1", 2, 2), ("turn", 5, 0), ("pv1", 2, 3),
              ("stats", 5, 1)]
    if only == 5:
        return steps
    steps += [("gate2", t) for t in range(TPH)]
    steps += [("hid2", 0, 0, 0), ("turn", 5, 1), ("hid2", 0, 0, 1)]
    steps += [("gate2", t) for t in range(TPH, TILES)] + [("moe",)]
    steps += [("hid2", 0, c, hf) for c in range(1, KT) for hf in range(2)]
    for e in range(MOE):
        for t in range(TILES):
            if e + 1 < MOE:
                steps.append(("hid2", e + 1, t // 2, t % 2))
            steps.append(("out2", e, t))
            if e == MOE - 1 and t == TPH - 1:
                steps.append(("stats", 6, 0))
    steps += [("turn", 6, 0), ("stats", 6, 1)]
    if only == 6:
        return steps
    steps += [("k3", c) for c in range(KT)] + [("v3", b) for b in range(B)]
    steps += [("q3", 0, 0), ("turn", 6, 1)] + [("q3", c, 0) for c in range(1, KT)] + [("q3", c, 1) for c in range(KT)]
    units = [(b, c) for b in range(B) for c in range(KT)]
    steps.append(("keys3", 0, *units[0]))
    for n in range(len(units) + 2):
        if n < len(units):
            steps.append(("scores3", n, *units[n]))
        if 1 <= n <= len(units):
            steps.append(("turn3", n - 1, *units[n - 1]))
        if n >= 2:
            steps.append(("pv3", n - 2, *units[n - 2]))
            if units[n - 2][1] == 0 and units[n - 2][0] >= 1:
                steps += [("o3", TPB * (units[n - 2][0] - 1) + i) for i in range(TPB)]
            if n - 2 == 3 * KT - 1:
                steps.append(("stats", 7, 0))
        if n + 1 < len(units):
            steps.append(("keys3", n + 1, *units[n + 1]))
        if n < len(units):
            steps.append(("values3", n, *units[n]))
    steps += [("turn", 7, 0)] + [("o3", TILES - 2), ("o3", TILES - 1), ("stats", 7, 1)]
    if only == 7:
        return steps
    steps += [("up3", 0, 0), ("turn", 7, 1), ("up3", 0, 1)]
    steps += [("up3", f, hf) for f in range(1, half_f) for hf in range(2)]
    steps += [("down3", 0, t) for t in range(TILES)]
    steps += [("up3", f, hf) for f in range(half_f, FT) for hf in range(2)]
    steps += [("down3", 1, t) for t in range(TILES)]
    return steps


WEIGHT = {"v0": 1.9, "k0": 2.6, "kc0": .7, "q0": 2.6, "scores0": .9, "turn0": .4, "pv0": 1, "o0": 2.6, "up0": 5.2,
          "down0": 4.8, "scores1": 2, "pv1": 1.6, "route1": 1, "z1": 2.6, "zt1": .5, "b1": 2.6, "k2": 1.3, "m2": 1.3,
          "gate2": 1.2, "hid2": 2.6, "out2": 2.6, "k3": 1.3, "v3": 1, "q3": 2.6, "scores3": 1.3, "turn3": .5,
          "pv3": 1.3, "o3": 2.6, "up3": 5.2, "down3": 4}


def with_background(steps, first, last, jobs):
    a = next(i for i, s in enumerate(steps) if s[0] == first)
    z = max(i for i, s in enumerate(steps) if s[0] == last)
    total = sum(WEIGHT.get(s[0], 0) for s in steps[a:z])
    out, at, spent = list(steps[:a]), 0, 0.0
    for s in steps[a:z]:
        spent += WEIGHT.get(s[0], 0)
        out.append(s)
        while at < len(jobs) and at < len(jobs) * spent / total:
            out.append(jobs[at])
            at += 1
    return out + jobs[at:] + list(steps[z:])


LAYER_STAGES = {"layer0": ("v0", "k0", "kc0", "q0", "scores0", "turn0", "pv0", "o0", "up0", "down0"),
                "layer1": ("scores1", "turn1", "pv1", "router1", "route1", "z1", "zt1", "b1"),
                "layer2": ("k2", "m2", "c2", "gate2", "strength", "choice", "hid2", "out2", "bq"),
                "layer3": ("k3", "v3", "q3", "scores3", "turn3", "pv3", "o3", "up3", "down3")}
SHARED = {f"{stage}_{kind}": f"{layer}_{kind}" for layer, stages in LAYER_STAGES.items() for stage in stages
          for kind in ("product", "high", "low", "added")}
SHARED["h3_low"] = "layer3_low"


class Signals:

    def __init__(self, nc, ctx, known):
        self.nc, self.ctx, self.known = nc, ctx, known
        self.sems, self.count, self.at = {}, {}, {}
        self.bank, self.bank_of, self.user, self.last_step = 0, {}, {}, {}

    def sem(self, name):
        name = SHARED.get(name, name)
        if name not in self.sems:
            self.sems[name] = self.ctx.enter_context(self.nc.semaphore(name))
        return self.sems[name]

    def mark(self, name, key, by=1):
        shared = SHARED.get(name, name)
        self.count[shared] = self.count.get(shared, 0) + by
        self.at[name, key] = self.count[shared]
        return self.sem(name), by

    def when(self, name, key):
        return self.sem(name), self.known.at[name, key] if self.known else 1

    def next_bank(self, key, *freed_by):
        n = self.bank % 8
        self.bank += 1
        ended = self.user.get(n, ())
        self.user[n] = freed_by
        self.bank_of[key] = n
        return n, ended

    def bank_for(self, key):
        return self.known.bank_of[key] if self.known else 0


def build(nc, a, out, known, only=None):
    ctx = ExitStack()
    with ctx:
        sig = Signals(nc, ctx, known)

        def sb(name, shape, dt, scope=ctx):
            return scope.enter_context(nc.sbuf_tensor(name, shape, dt))

        x = sb("x", [P, TILES, D], FP32)
        xn = sb("xn", [P, TPH, D], FP32)
        xT = sb("xT", [P, 2, KT, TOK], F32R)
        ctxT = sb("ctxT", [P, 2, KT, B * CTX], F32R)
        slots = sb("slots", [P, NSLOT, 2, SLOT], F32R)
        staging = sb("staging", [P, 2, SLOT], FP32)
        ident = sb("ident", [P, P], FP32)
        st = sb("st", [P, TILES, 6], FP32)
        mv = sb("mv", [P, TILES, 2], FP32)
        rs = sb("rs", [P, TILES], FP32)
        rt = sb("rt", [P, 4, TILES], FP32)
        mx = sb("mx", [P, 4, 2 * HPC], FP32)
        sm = sb("sm", [P, 4, 2 * HPC], FP32)
        s0 = ExitStack()
        q0 = sb("q0", [HD0, 2, 2, HPG, HALF], F32R, s0)
        k0 = sb("k0", [HD0, 2, 2, BPH, KEYS0], F32R, s0)
        v0 = sb("v0", [P, 2, TILES + B, G0 * HD0], F32R, s0)
        eT0 = sb("eT0", [P, 2, 2, 3, S], F32R, s0)
        e0 = sb("e0", [P, 3, KEYS0], FP32, s0)
        s0.close()
        nfs = ExitStack()
        nf_w = sb("nf_w", [P, D], FP32, nfs)
        nf_a = sb("nf_a", [P, D], FP32, nfs)
        nf_r = sb("nf_r", [P, D], FP32, nfs)
        nf_y = sb("nf_y", [P, 2, D], FP32, nfs)
        nf_acc = sb("nf_acc", [P, D], FP32, nfs)
        nf_m = sb("nf_m", [P, 3, 88], FP32, nfs)
        nf_t = sb("nf_t", [P, 2, P], FP32, nfs)
        l = ExitStack()
        h0 = sb("h0", [P, (FT + 1) // 2, TOK], F32R, l)
        acc0 = sb("acc0", [P, TILES, D], FP32, l)
        g0 = sb("g0", [P, 2, HALF], FP32, l)
        f0 = sb("f0", [P, 5, HALF], FP32, l)
        l.close()
        l = ExitStack()
        ctxN = sb("ctxN", [CTX, 2, B, D], F32R, l)
        e1 = sb("e1", [P, 2, TPB, CTX], FP32, l)
        s1 = sb("s1", [P, 2, TPB, CTX], FP32, l)
        eT1 = sb("eT1", [CTX, 2, 2, S], F32R, l)
        k2 = sb("k2", [P, 2, KT, B * CTX], F32R, l)
        m2 = sb("m2", [P, 2, KT, B * CTX], F32R, l)
        c2 = sb("c2", [P, B * CTX], FP32, l)
        bq = sb("bq", [P, KT], FP32, l)
        bk = sb("bk", [P, KT], FP32, l)
        bqw = sb("bqw", [P, 2, KT, P], F32R, l)
        bqf = sb("bqf", [P, KT, P], FP32, l)
        wq1 = sb("wq1", [ROUT, D], FP32, l)
        keyT = sb("keyT", [ROUT, NE], FP32, l)
        rw = sb("rw", [P, 2, KT, NE], F32R, l)
        r1 = sb("r1", [P, 4, TILES, NE], FP32, l)
        top8 = sb("top8", [P, 2, TILES, 8], FP32, l)
        zg = sb("zg", [P, 2, D], FP32, l)
        zT = sb("zT", [P, 2, 2, KT, P], F32R, l)
        l.close()
        l = ExitStack()
        h2 = sb("h2", [P, 2, 2, KT, TOK], F32R, l)
        hf2 = sb("hf2", [P, 2, HALF], FP32, l)
        y2 = sb("y2", [P, D], FP32, l)
        b1c = sb("b1c", [P, MOE, KT], FP32, l)
        b2b = sb("b2b", [P, MOE, D], FP32, l)
        gwf = sb("gwf", [P, KT, 4], FP32, l)
        gw = sb("gw", [P, 2, KT, 4], F32R, l)
        gwr = sb("gwr", [P, 4], FP32, l)
        gbr = sb("gbr", [P, 4], FP32, l)
        vis = sb("vis", [P, P], FP32, l)
        txt = sb("txt", [P, P], FP32, l)
        one = sb("one", [P, P], FP32, l)
        row0 = sb("row0", [P, P], FP32, l)
        ab = sb("ab", [P, TILES], FP32, l)
        lg = sb("lg", [P, TILES, 4], FP32, l)
        p8 = sb("p8", [P, TILES, 8], FP32, l)
        t8 = sb("t8", [P, TILES, 8], FP32, l)
        gt = sb("gt", [P, 12, TILES], FP32, l)
        fl = sb("fl", [P, 2, MOE, TILES], FP32, l)
        fb = sb("fb", [P, 2, MOE, TILES], FP32, l)
        cf = sb("cf", [P, MOE, TILES], FP32, l)
        ra = sb("ra", [P, 4, TILES], FP32, l)
        l.close()
        l = ExitStack()
        q3 = sb("q3", [P, 2, KT, TOK], F32R, l)
        kd3 = sb("kd3", [P, 2, 2, HPC, CTX], F32R, l)
        vd3 = sb("vd3", [P, 2, 2, PAIRS, P], F32R, l)
        kr3 = sb("kr3", [P, 2, KT, B * CTX], F32R, l)
        v3 = sb("v3", [CTX, 2, B, KV3 * HD3], F32R, l)
        e3 = sb("e3", [P, 2, TPB, HPC * CTX], FP32, l)
        eT3 = sb("eT3", [P, 2, PAIRS, S], F32R, l)
        hm3 = sb("hm3", [P, HPC], FP32, l)
        lnw = sb("lnw", [P, KT], FP32, l)
        l.close()
        nfs.close()
        l = ExitStack()
        h3 = sb("h3", [P, 2, (FT + 1) // 2, TOK], F32R, l)
        g3 = sb("g3", [P, 3, HALF], FP32, l)
        l.close()
        banks = [ctx.enter_context(nc.psum_tensor(f"bank{i}", [P, 512], FP32)) for i in range(8)]

        def psum(key):
            return banks[sig.bank_for(key)]

        def dram(name, shape):
            return nc.dram_tensor(name, shape, FP32, kind="Internal").ap()

        nf_max = [dram(f"nf_max{m}", (88, P)) for m in range(3)]
        nf_rcp = [dram(f"nf_rcp{m}", (88, P)) for m in range(3)]
        nf_out = [dram(f"nf_out{m}", (FT, P, D)) for m in range(3)]

        chunks, chunk_no = [], {}

        def chunk(name, p, dims, loads, dest=None, after=None):
            chunk_no[name] = len(chunks)
            chunks.append((name, p, dims, loads, dest, after))

        def by_k(ap, k0_, k1_):
            return ap.rearrange("(k p) n -> p k n", p=P)[:, k0_:k1_]

        chunk("ctxT", P, (KT, B * CTX), [((slice(None),), by_k(a["ctxT"], 0, KT))], dest=(ctxT[:, 0], ctxT[:, 1]))
        for i in range(2):
            chunk(("v0", i), P, (2, G0 * HD0), [((slice(None),), by_k(a["L0_wvT"], 2 * i, 2 * i + 2))])
        for g in range(G0):
            for i in range(2):
                chunk(("qk0", g, i), P, (2, (HPG + 1) * HD0),
                      [((slice(None),), by_k(a["L0_wqkT"][g], 2 * i, 2 * i + 2))])
            for i in range(2):
                rows = a["L0_woT"][(g * HPG + 2 * i) * HD0:(g * HPG + 2 * i + 2) * HD0]
                chunk(("o0", g, i), HD0, (2, D), [((slice(None),), rows.rearrange("(h p) n -> p h n", p=HD0))])

        def ffn_up(name, gate, up, lo, hi):
            for f in range(lo, hi):
                w = fwidth(f)
                chunk((name, f), P, (2, KT, w), [((0,), gate(f)), ((1,), up(f))], after=after_nf(name, f))

        def ffn_down(name, down, lo, hi):
            for f in range(lo, hi, 2):
                n = min(2, hi - f)
                w = fwidth(f + n - 1)
                if w == P or n == 1:
                    chunk((name, f), w, (n, D), [((i,), down(f + i, w)) for i in range(n)], after=after_nf(name, f))
                else:
                    chunk((name, f), P, (1, D), [((0,), down(f, P))], after=after_nf(name, f))
                    chunk((name, f + 1), w, (1, D), [((0,), down(f + 1, w))], after=after_nf(name, f))

        def after_nf(name, f):
            return ("nf4_stored", FT * 3 - 1) if name in ("up3", "down3") else None

        def cols(ap):
            return lambda f: ap.rearrange("(k p) n -> p k n", p=P)[:, :, f * P:f * P + fwidth(f)]

        half_f = (FT + 1) // 2
        for lo, hi in ((0, half_f), (half_f, FT)):
            ffn_up("up0", cols(a["L0_wgT"]), cols(a["L0_wuT"]), lo, hi)
            ffn_down("down0", lambda f, w: a["L0_wdT"][f * P:f * P + w], lo, hi)
        for i in range(2):
            chunk(("ctxN", i), CTX, (2, D),
                  [((slice(None),), a["ctx"][2 * i:2 * i + 2].rearrange("b s d -> s b d"))],
                  dest=(ctxN[:, 0, 2 * i:2 * i + 2], ctxN[:, 1, 2 * i:2 * i + 2]), after=("down0_product", (1, TILES - 1)))
        for name, ap in (("z1", a["L1_aT"]), ("b1", a["L1_bT"]), ("k2", a["L2_wkT"]), ("m2", a["L2_wq"])):
            for i in range(2):
                chunk((name, i), P, (2, D), [((slice(None),), by_k(ap, 2 * i, 2 * i + 2))])
        for e in range(MOE):
            for name, ap in (("hid2", a["L2_w1"]), ("out2", a["L2_w2"])):
                for i in range(2):
                    chunk((name, e, i), P, (2, D), [((slice(None),), by_k(ap[e], 2 * i, 2 * i + 2))])
        order = []
        tail = chunks[-4 * MOE:]
        del chunks[-4 * MOE:]
        names = {c[0]: c for c in tail}
        order = [("hid2", 0, 0), ("hid2", 0, 1)]
        for e in range(MOE):
            order += [("out2", e, 0), ("out2", e, 1)] + [("hid2", e + 1, i) for i in range(2) if e + 1 < MOE]
        for n in order:
            chunk(*names[n])
        for i in range(2):
            chunk(("k3", i), P, (2, D), [((slice(None),), by_k(a["L3_wkT"], 2 * i, 2 * i + 2))])
        chunk(("v3", 0), P, (KT, KV3 * HD3), [((slice(None),), by_k(a["L3_wvT"], 0, KT))])
        for i in range(2):
            chunk(("q3", i), P, (2, D), [((slice(None),), by_k(a["L3_wqT"], 2 * i, 2 * i + 2))])
        for i in range(2):
            chunk(("o3", i), P, (2, D), [((slice(None),), by_k(a["L3_woT"], 2 * i, 2 * i + 2))])

        def nf_cols(m):
            return lambda f: nf_out[m][f][:, 0:KT * fwidth(f)].rearrange("p (k n) -> p k n", k=KT)

        for lo, hi in ((0, half_f), (half_f, FT)):
            ffn_up("up3", nf_cols(0), nf_cols(1), lo, hi)
            ffn_down("down3", lambda f, w: nf_out[2][f][0:w], lo, hi)

        base = schedule(only)
        if only is None or only == 7:
            jobs = [("nf_max", m, f) for m in range(3) for f in range(FT)] + [("nf_turn", m) for m in range(3)]
            jobs += [("nf", 3 * f + m, m, f, j) for f in range(FT) for m in range(3) for j in range(len(BOUNDS) + 1)]
            base = with_background(base, "up0", "q3", jobs)
        steps = []
        if known:
            last = known.last_step
            free_after = {}
            slot_of, n = {}, 0
            for c_ in chunks:
                if c_[4] is None:
                    slot_of[c_[0]] = n
                    n += 1
            ring = sorted(slot_of, key=slot_of.get)
            for i, c_ in enumerate(chunks):
                at = -1
                if c_[4] is None and slot_of[c_[0]] >= NSLOT:
                    prev = ring[slot_of[c_[0]] - NSLOT]
                    if prev not in last:
                        break
                    at = last[prev]
                if c_[5] is not None and c_[5][0] == "down0_product":
                    at = max(i2 for i2, s in enumerate(base) if s[0] == "down0") if "down0" in {s[0] for s in base} else None
                    if at is None:
                        break
                if c_[5] is not None and c_[5][0] == "nf4_stored":
                    at = max([at] + [i2 for i2, s in enumerate(base) if s[0] == "nf"])
                at = max(at, max(free_after, default=-1))
                free_after.setdefault(at, []).append(i)
            n_chunks = sum(len(v) for v in free_after.values())
            steps += [("split", i) for i in free_after.get(-1, [])]
            for i, s in enumerate(base):
                steps.append(s)
                steps += [("split", j) for j in free_after.get(i, [])]
        else:
            steps = [("split", i) for i in range(len(chunks))] + base
            n_chunks = len(chunks)

        slot_no, n = {}, 0
        for c_ in chunks:
            if c_[4] is None:
                slot_no[c_[0]] = n
                n += 1
        ring_names = sorted(slot_no, key=slot_no.get)

        def flat(ap, dims):
            if len(dims) == 1:
                return ap
            if len(dims) == 2:
                return ap.rearrange("p (a b) -> p a b", a=dims[0])
            return ap.rearrange("p (a b c) -> p a b c", a=dims[0], b=dims[1])

        def weight(name, part):
            _, p, dims, _, dest, _ = chunks[chunk_no[name]]
            if dest is not None:
                return dest[part]
            size = int(np.prod(dims))
            return flat(slots[0:p, slot_no[name] % NSLOT, part, 0:size], dims)

        chunk_no.clear()
        chunk_no.update({c_[0]: i for i, c_ in enumerate(chunks)})
        block = ctx.enter_context(nc.Block())

        @block.sync
        def _(sp):
            sp.dma_start(x[:, 0:TPH], a["x"][:, 0:TPH]).then_inc(*sig.mark("x_loaded0", 0, 16))
            sp.dma_start(x[:, TPH:], a["x"][:, TPH:]).then_inc(*sig.mark("x_loaded1", 0, 16))
            for i in range(n_chunks):
                name, p, dims, loads, dest, after = chunks[i]
                if i >= 2:
                    sp.wait_ge(*sig.when("weight_low", i - 2))
                if after is not None and after[0] == "nf4_stored":
                    for q in range(2):
                        sp.wait_ge(*sig.when(f"nf4_stored{q}", 3 * FT - 1 - q))
                size = int(np.prod(dims))
                view = flat(staging[0:p, i % 2, 0:size], dims)
                for n, (ix, src) in enumerate(loads):
                    dst = view if ix == (slice(None),) else view[:, ix[0]]
                    sp.dma_start(dst, src).then_inc(*sig.mark(f"weight_staged{i % 2}", i, 16))

        def split_source(i):
            _, p, dims, *_ = chunks[i]
            return flat(staging[0:p, i % 2, 0:int(np.prod(dims))], dims)

        @block.gpsimd
        def _(pool):
            g = nc.gpsimd
            g.memset(ident[:], 0.0).then_inc(*sig.mark("pool_const", "a"))
            pool.wait_ge(*sig.when("pool_const", "a"))
            g.affine_select(out=ident[:], in_=ident[:], compare_op=ALU.not_equal, fill=1.0, base=0,
                            pattern=[[-1, P]], channel_multiplier=1).then_inc(*sig.mark("ident_ready", 0))

            def small_loads(when, pairs):
                for w in when:
                    pool.wait_ge(*sig.when(*w))
                for name, dst, src in pairs:
                    pool.dma_start(dst, src).then_inc(*sig.mark(f"loaded_{name}", 0, 16))

            def split(i):
                pool.wait_ge(*sig.when("weight_high", i))
                _, p, dims, *_ = chunks[i]
                hi, lo = weight(chunks[i][0], 0), weight(chunks[i][0], 1)
                g.tensor_tensor(lo, split_source(i), hi.bitcast(FP32), ALU.subtract).then_inc(*sig.mark("weight_low", i))

            nf_src = (a["L3_w1"], a["L3_w2"])

            def nf_max_load(m, f):
                w = fwidth(f) if m < 2 else P
                n = D if m < 2 or f < 10 else 6 * BLOCK
                if (m, f) == (0, 0):
                    pool.wait_ge(*sig.when("pv0_product", 63))
                    pool.wait_ge(*sig.when("o0_product", (2 * G0 - 1, TPH - 1)))
                    pool.wait_ge(*sig.when("x_done", (1, 1)))
                else:
                    prev = (m, f - 1) if f else (m - 1, FT - 1)
                    pool.wait_ge(*sig.when("nf4_max", prev))
                src = nf_src[m][f * P:f * P + w] if m < 2 else a["L3_w3"][:, f * D:f * D + n]
                pool.dma_start(nf_w[0:w, 0:n], src).then_inc(*sig.mark("nf4_rows", (m, f), 16))

            def nf_turned(m):
                for i, dst in enumerate((nf_max[m], nf_rcp[m])):
                    pool.wait_ge(*sig.when("nf4_turned", (m, i)))
                    pool.dma_start(dst, nf_t[0:88, i]).then_inc(*sig.mark(f"nf4_maxima_stored{i}", m, 16))

            def broadcast_rows(dst_tile, src, m, f):
                w = fwidth(f)
                pairs = []
                if m < 2:
                    for ph in range(2):
                        rows = src[f * 8:f * 8 + 8, 0:w].rearrange("(k two) n -> two k n", two=2)[ph]
                        dst = dst_tile[64 * ph:64 * ph + 64, 0:KT * w].rearrange("p (k n) -> p k n", k=KT)
                        pairs.append((dst, rows.partition_broadcast(64)))
                else:
                    for dr in range(4):
                        row, p = None, 0
                        while p < w:
                            hh = (f * P + p) // 32
                            c = (dr * 43 + hh) // 2
                            q = p
                            while q < w and (dr * 43 + (f * P + q) // 32) // 2 == c:
                                q += 32
                            pairs.append((dst_tile[p:q, dr * P:(dr + 1) * P], src[c].partition_broadcast(q - p)))
                            p = q
                return pairs

            turned_src = (a["L3_w1T"], a["L3_w2T"])

            def nf(n, m, f, j):
                w = fwidth(f)
                rows, size = (P, KT * w) if m < 2 else (w, D)
                if j == 0:
                    for i in range(2):
                        pool.wait_ge(*sig.when(f"nf4_maxima_stored{i}", 2))
                    if n:
                        pool.wait_ge(*sig.when("nf4_dequantised", n - 1))
                        pool.wait_ge(*sig.when("nf4_step", (n - 1, len(BOUNDS))))
                    src = turned_src[m].rearrange("(k p) n -> p k n", p=P)[:, :, f * P:f * P + w] if m < 2 \
                        else a["L3_w3T"][f * P:f * P + w]
                    dst = nf_w[0:rows, 0:size].rearrange("p (k n) -> p k n", k=KT) if m < 2 else nf_w[0:rows, 0:size]
                    pool.dma_start(dst, src).then_inc(*sig.mark("nf4_weights", n, 16))
                    for dst, src in broadcast_rows(nf_a, nf_max[m], m, f) + broadcast_rows(nf_r, nf_rcp[m], m, f):
                        pool.dma_start(dst, src).then_inc(*sig.mark("nf4_weights", n, 16))
                elif j >= 2:
                    acc = nf_acc[0:rows, 0:size]
                    pool.wait_ge(*sig.when("nf4_step", (n, j)))
                    if j == 2:
                        pool.wait_ge(*sig.when("nf4_step", (n, 1)))
                    else:
                        pool.wait_ge(*sig.when("nf4_added", (n, j - 1)))
                    g.tensor_tensor(acc, acc, nf_y[0:rows, j % 2, 0:size], ALU.add).then_inc(*sig.mark("nf4_added", (n, j)))
                    if j == len(BOUNDS):
                        pool.wait_ge(*sig.when("nf4_added", (n, j)))
                        if n:
                            pool.wait_ge(*sig.when(f"nf4_stored{(n - 1) % 2}", n - 1))
                        o = nf_r[0:rows, 0:size] if m < 2 else nf_r[0:rows, 0:size].rearrange("p (q r) -> p r q", r=4)
                        i0 = acc if m < 2 else acc.rearrange("p (r q) -> p r q", r=4)
                        i1 = nf_a[0:rows, 0:size] if m < 2 else nf_a[0:rows, 0:size].rearrange("p (r q) -> p r q", r=4)
                        g.tensor_tensor(o, i0, i1, ALU.mult).then_inc(*sig.mark("nf4_dequantised", n))
                        pool.wait_ge(*sig.when("nf4_dequantised", n))
                        pool.dma_start(nf_out[m][f][0:rows, 0:size], nf_r[0:rows, 0:size])\
                            .then_inc(*sig.mark(f"nf4_stored{n % 2}", n, 16))
                        pool.wait_ge(*sig.when(f"nf4_stored{n % 2}", n))

            def hid2(e, c, hf):
                pool.wait_ge(*sig.when("h2_high", (e, c, hf)))
                i = (e * KT + c) * 2 + hf
                cs = slice(hf * HALF, (hf + 1) * HALF)
                g.tensor_tensor(h2[:, e % 2, 1, c, cs], hf2[:, i % 2], h2[:, e % 2, 0, c, cs].bitcast(FP32),
                                ALU.subtract).then_inc(*sig.mark("h2_low", (e, c, hf)))

            for s in steps:
                kind, args = s[0], s[1:]
                if kind == "split":
                    split(*args)
                elif kind == "nf_max":
                    nf_max_load(*args)
                elif kind == "nf_turn":
                    nf_turned(*args)
                elif kind == "nf":
                    nf(*args)
                elif kind == "hid2":
                    hid2(*args)
                elif kind == "scores1" and args == (1, 0):
                    small_loads([("down0_product", (1, TILES - 1)), ("x_done", (2, 1))],
                                [("wq1", wq1[:], a["L1_wq"]), ("keyT", keyT[:], a["L1_keysT"]),
                                 ("bq", bq[:], a["L2_bq"]), ("bk", bk[:], a["L2_bk"])])
                elif kind == "stats" and args == (5, 1):
                    pool.wait_ge(*sig.when("pv1_product", (2, B - 1, 1)))
                    pool.wait_ge(*sig.when("x_done", (5, 1)))
                    small_loads([], [("b1c", b1c[:], a["L2_b1"]),
                                     ("b2b", b2b[:], a["L2_b2"].partition_broadcast(P)),
                                     ("gwf", gwf[:, :, 0:MOE], a["L2_gw"][0:D].rearrange("(k p) n -> p k n", p=P)),
                                     ("gwr", gwr[:, 0:MOE], a["L2_gw"][D].partition_broadcast(P)),
                                     ("gbr", gbr[:, 0:MOE], a["L2_gb"].partition_broadcast(P))])
                    g.memset(gwf[:, :, MOE:4], 0.0).then_inc(*sig.mark("pool_gate", "pad"))
                    for n, t in (("vis", vis), ("txt", txt), ("one", one), ("row0", row0)):
                        g.memset(t[:], 1.0).then_inc(*sig.mark("pool_gate", n))
                    g.memset(p8[:], -1.0).then_inc(*sig.mark("pool_gate", "p8"))
                    pool.wait_ge(*sig.when("pool_gate", "row0"))
                    for n, t, base_, mult in (("visf", vis, VISION - 1, -1), ("txtf", txt, -VISION, 1), ("row0f", row0, 0, -1)):
                        g.affine_select(out=t[:], in_=t[:], compare_op=ALU.is_ge, fill=0.0, base=base_,
                                        pattern=[[0, P]], channel_multiplier=mult).then_inc(*sig.mark("pool_gate", n))
                elif kind == "stats" and args == (6, 1):
                    pool.wait_ge(*sig.when("out2_product", (MOE - 1, TILES - 1)))
                    pool.wait_ge(*sig.when("x_done", (6, 1)))
                    small_loads([], [("lnw", lnw[:], a["L3_lnw"])])
                    g.memset(hm3[:], 1.0).then_inc(*sig.mark("pool_head", "a"))
                    pool.wait_ge(*sig.when("pool_head", "a"))
                    g.affine_select(out=hm3[:], in_=hm3[:], compare_op=ALU.is_ge, fill=0.0, base=0,
                                    pattern=[[-HD3, HPC]], channel_multiplier=1).then_inc(*sig.mark("pool_head", "b"))
                    pool.wait_ge(*sig.when("pool_head", "b"))
                    g.affine_select(out=hm3[:], in_=hm3[:], compare_op=ALU.is_ge, fill=0.0, base=HD3 - 1,
                                    pattern=[[HD3, HPC]], channel_multiplier=-1).then_inc(*sig.mark("head_mask", 0))
                    g.memset(vd3[:].bitcast(FP32), 0.0).then_inc(*sig.mark("vd3_clear", 0))

        @block.scalar
        def _(act):
            sc = nc.scalar

            def high(stage, key, dst, src, product=None, func=ACT.Copy, **kw):
                act.wait_ge(*sig.when(*(product or (f"{stage}_product", key))))
                sc.activation(dst, src, func, **kw).then_inc(*sig.mark(f"{stage}_high", key))

            def split(i):
                name, p, dims, loads, dest, after = chunks[i]
                act.wait_ge(*sig.when(f"weight_staged{i % 2}", i))
                if dest is None and slot_no[name] >= NSLOT and known:
                    act.wait_ge(*sig.when(*known.user[("chunk", ring_names[slot_no[name] - NSLOT])]))
                if after is not None and after[0] == "down0_product":
                    act.wait_ge(*sig.when(*after))
                sc.activation(weight(name, 0), split_source(i), ACT.Copy).then_inc(*sig.mark("weight_high", i))

            def turn(layer, hf):
                for c in range(KT):
                    key = (layer, hf, c)
                    dst = xT[:, 0, c, hf * HALF:(hf + 1) * HALF]
                    if layer == 6:
                        act.wait_ge(*sig.when("loaded_lnw", 0))
                        high("turn", key, dst, psum(("turn", *key))[:], func=ACT.Identity, scale=lnw[:, c:c + 1])
                    else:
                        high("turn", key, dst, psum(("turn", *key))[:])

            def v0_(t):
                p = P if t < TILES else CTX
                high("v0", t, v0[0:p, 0, t], psum(("v0", t))[0:p, 0:G0 * HD0])

            def k0_(s):
                high("k0", s, k0[:, s % 2, 0, :, 0:S], psum(("k0", s))[0:HD0].rearrange("p (b n) -> p b n", b=BPH))

            def kc0_(s):
                high("kc0", s, k0[:, s % 2, 0, :, S:], psum(("kc0", s))[0:HD0, 0:BPH * CTX].rearrange("p (b n) -> p b n", b=BPH))

            def q0_(s, h):
                high("q0", (s, h), q0[:, s % 2, 0, h], psum(("q0", s, h))[0:HD0])

            def scores0(n, s, bl, h):
                act.wait_ge(*sig.when("max0", n))
                for i in range(TPB):
                    if 2 * n + i >= 3:
                        act.wait_ge(*sig.when("turn0_product", (2 * n + i - 3) // 2))
                    sc.activation(e0[:, (2 * n + i) % 3], psum(("scores0", n, i))[:, 0:KEYS0], ACT.Exp, scale=HD0 ** -0.5,
                                  bias=mx[:, n % 4, 2 + i:3 + i], accum_out=sm[:, n % 4, i:i + 1])\
                        .then_inc(*sig.mark("exp0", (n, i)))

            def turn0(n, s, bl, h):
                act.wait_ge(*sig.when("turn0_product", n))
                if n >= 2:
                    act.wait_ge(*sig.when("pv0_product", n - 2))
                sc.activation(eT0[:, n % 2, 0, 0:2], psum(("turn0", n, 0))[:].rearrange("p (k n) -> p k n", k=2),
                              ACT.Copy).then_inc(*sig.mark("turn0_high", (n, 0)))
                sc.activation(eT0[0:CTX, n % 2, 0, 2], psum(("turn0", n, 1))[0:CTX, 0:S],
                              ACT.Copy).then_inc(*sig.mark("turn0_high", (n, 1)))

            def pv0(n, s, bl, h):
                high("pv0", n, q0[:, s % 2, 0, h, bl * S:(bl + 1) * S], psum(("pv0", n))[0:HD0, 0:S])

            def up0(f, hf):
                w, n = fwidth(f), 2 * f + hf
                act.wait_ge(*sig.when("up0_product", (f, hf, 0)))
                if n == 0:
                    act.wait_ge(*sig.when("pv0_low", 63))
                if n >= 2:
                    act.wait_ge(*sig.when("inter0", n - 2))
                sc.activation(g0[0:w, n % 2], psum(("up0", f, hf, 0))[0:w], ACT.Silu, scale=1 / 128)\
                    .then_inc(*sig.mark("silu0", n))
                act.wait_ge(*sig.when("inter0", n))
                if n >= 1:
                    act.wait_ge(*sig.when("h0_done", n - 1))
                sc.activation(f0[0:w, 1], f0[0:w, 0], ACT.Abs).then_inc(*sig.mark("abs0", n))
                sc.activation(f0[0:w, 2], f0[0:w, 0], ACT.Sign, scale=-1.0).then_inc(*sig.mark("sign0", n))

            def down0(part, t):
                if part == 0:
                    act.wait_ge(*sig.when("down0_product", (part, t)))
                    sc.activation(acc0[:, t], psum(("down0", part, t))[:], ACT.Copy).then_inc(*sig.mark("down0_part", t))
                else:
                    act.wait_ge(*sig.when("down0_sum", t))
                    sc.activation(f0[:, 1], f0[:, 0], ACT.Abs, scale=128.0).then_inc(*sig.mark("dabs0", t))
                    sc.activation(f0[:, 2], f0[:, 0], ACT.Sign, scale=-1.0).then_inc(*sig.mark("dsign0", t))

            def scores1(layer, b):
                n = (layer, b)
                act.wait_ge(*sig.when("max1", n))
                if b >= 2 or layer == 2:
                    prev = (layer, b - 2) if b >= 2 else (1, B - 2 + b)
                    act.wait_ge(*sig.when("turn1_product", prev))
                for i in range(TPB):
                    src = psum(("scores1", layer, b))[:, i * CTX:(i + 1) * CTX] if layer == 1 else s1[:, b % 2, i]
                    sc.activation(e1[:, b % 2, i], src, ACT.Exp, scale=1.0 if layer == 1 else D ** -0.5,
                                  bias=mx[:, b % 4, 2 + i:3 + i], accum_out=sm[:, b % 4, i:i + 1])\
                        .then_inc(*sig.mark("exp1", (layer, b, i)))

            def pv1(layer, b):
                if b >= 2 or layer == 2:
                    prev = (layer, b - 2, 1) if b >= 2 else (1, B - 2 + b, 1)
                    act.wait_ge(*sig.when("pv1_product", prev))
                if (layer, b) == (1, 0):
                    act.wait_ge(*sig.when("down0_product", (1, TILES - 1)))
                high("turn1", (layer, b), eT1[:, b % 2, 0], psum(("turn1", layer, b))[0:CTX, 0:S])

            def route1(t):
                act.wait_ge(*sig.when("route1_rep", t))
                for i, src in ((2, r1[:, 0, t]), (3, r1[:, 1, t])):
                    sc.activation(r1[:, i, t], src, ACT.Exp, bias=rs[:, t:t + 1]).then_inc(*sig.mark("route1_exp", (t, i)))

            def router1():
                high("router1", 0, rw[:, 0], psum(("router1",))[:, 0:KT * NE].rearrange("p (k n) -> p k n", k=KT))

            def zt1(t):
                if t >= 2:
                    act.wait_ge(*sig.when("b1_product", t - 2))
                high("zt1", t, zT[:, t % 2, 0], psum(("zt1", t))[:].rearrange("p (k n) -> p k n", k=KT))

            def k2_(c):
                act.wait_ge(*sig.when("loaded_bk", 0))
                high("k2", c, k2[:, 0, c], psum(("k2", c))[:, 0:B * CTX], func=ACT.Identity, bias=bk[:, c:c + 1])

            def m2_(c):
                high("m2", c, m2[:, 0, c], psum(("m2", c))[:, 0:B * CTX])

            def c2_():
                act.wait_ge(*sig.when("c2_product", 0))
                sc.activation(c2[:], psum(("c2",))[:, 0:B * CTX], ACT.Copy).then_inc(*sig.mark("c2_ready", 0))

            def k2_prep():
                act.wait_ge(*sig.when("bq_wide", 0))
                sc.activation(bqw[:, 0], bqf[:], ACT.Copy).then_inc(*sig.mark("bq_high", 0))

            def gate2(t):
                if t == 0:
                    act.wait_ge(*sig.when("pool_gate", "pad"))
                    act.wait_ge(*sig.when("loaded_gwf", 0))
                    sc.activation(gw[:, 0], gwf[:], ACT.Copy).then_inc(*sig.mark("gw_high", 0))

            def moe():
                act.wait_ge(*sig.when("moe_shift", 0))
                sc.activation(lg[:, :, 0:MOE], lg[:, :, 0:MOE], ACT.Exp).then_inc(*sig.mark("moe_exp", 0))

            def hid2(e, c, hf):
                i = (e * KT + c) * 2 + hf
                act.wait_ge(*sig.when("hid2_product", (e, c, hf)))
                act.wait_ge(*sig.when("loaded_b1c", 0))
                if i >= 2:
                    e_, r_ = divmod(i - 2, 2 * KT)
                    act.wait_ge(*sig.when("h2_low", (e_, r_ // 2, r_ % 2)))
                func = (ACT.Tanh, ACT.Gelu, ACT.Silu)[e]
                sc.activation(hf2[:, i % 2], psum(("hid2", e, c, hf))[:], func, bias=b1c[:, e, c:c + 1])\
                    .then_inc(*sig.mark("hid2_value", (e, c, hf)))

            def k3_(c):
                high("k3", c, kr3[:, 0, c], psum(("k3", c))[:, 0:B * CTX])

            def v3_(b):
                high("v3", b, v3[:, 0, b], psum(("v3", b))[0:CTX, 0:KV3 * HD3])

            def q3_(c, hf):
                high("q3", (c, hf), q3[:, 0, c, hf * HALF:(hf + 1) * HALF], psum(("q3", c, hf))[:])

            def scores3(n, b, c):
                for i in range(TPB):
                    act.wait_ge(*sig.when("shift3", (n, i)))
                    sc.activation(e3[:, n % 2, i], e3[:, n % 2, i], ACT.Exp, scale=HD3 ** -0.5)\
                        .then_inc(*sig.mark("exp3", (n, i)))

            def turn3(n, b, c):
                for i in range(2):
                    act.wait_ge(*sig.when("turn3_product", (n, i)))
                    if n >= 1:
                        act.wait_ge(*sig.when("pv3_product", n - 1))
                    sc.activation(eT3[:, 0, 2 * i:2 * i + 2], psum(("turn3", n, i))[:].rearrange("p (k n) -> p k n", k=2),
                                  ACT.Copy).then_inc(*sig.mark("turn3_high", (n, i)))

            def pv3(n, b, c):
                high("pv3", n, q3[:, 0, c, b * S:(b + 1) * S], psum(("pv3", n))[:, 0:S])

            def up3(f, hf):
                w, n = fwidth(f), 2 * f + hf
                act.wait_ge(*sig.when("up3_product", (f, hf, 0)))
                if n == 0:
                    act.wait_ge(*sig.when("pv3_low", 15))
                    act.wait_ge(*sig.when("nf4_stored0", 3 * FT - 1))
                if n >= 3:
                    act.wait_ge(*sig.when("h3_low", n - 3))
                sc.activation(g3[0:w, n % 3], psum(("up3", f, hf, 0))[0:w], ACT.Silu).then_inc(*sig.mark("silu3", n))

            def nf_turn(m):
                for i in range(2):
                    act.wait_ge(*sig.when("nf4_turn_product", m))
                    if m:
                        act.wait_ge(*sig.when(f"nf4_maxima_stored{i}", m - 1))
                    elif i == 0:
                        act.wait_ge(*sig.when("nf4_max", (0, 0)))
                    sc.activation(nf_t[0:88, i], psum(("nf_turn", m))[0:88, i * P:(i + 1) * P], ACT.Copy)\
                        .then_inc(*sig.mark("nf4_turned", (m, i)))

            handlers = {"split": split, "turn": turn, "v0": v0_, "k0": k0_, "kc0": kc0_, "q0": q0_, "scores0": scores0,
                        "turn0": turn0, "pv0": pv0, "up0": up0, "down0": down0, "scores1": scores1, "pv1": pv1,
                        "route1": route1, "router1": router1, "zt1": zt1, "k2": k2_, "m2": m2_, "c2": c2_,
                        "gate2": gate2, "moe": moe, "hid2": hid2, "k3": k3_, "v3": v3_, "q3": q3_,
                        "scores3": scores3, "turn3": turn3, "pv3": pv3, "up3": up3, "nf_turn": nf_turn}
            for s in steps:
                if s[0] == "c2":
                    k2_prep()
                if s[0] in handlers:
                    handlers[s[0]](*s[1:])

        @block.vector
        def _(dve):
            v = nc.vector
            links = [0]

            def link(ins):
                links[0] += 1
                ins.then_inc(sig.sem("vector_chain"), 1)
                dve.wait_ge(sig.sem("vector_chain"), links[0])

            def low(stage, key, dst, src, hi):
                dve.wait_ge(*sig.when(f"{stage}_high", key))
                v.tensor_tensor(dst, src, hi.bitcast(FP32), ALU.subtract).then_inc(*sig.mark(f"{stage}_low", key))

            def rsqrt(y, t, tmp, scale=None):
                ib = y.bitcast(INT32)
                link(v.tensor_scalar(ib, t.bitcast(INT32), 1, None, ALU.logical_shift_right))
                link(v.tensor_scalar(ib, ib, -1.0, 1597463007.0, ALU.mult, ALU.add))
                link(v.tensor_scalar(tmp[0], t, -0.5, None, ALU.mult))
                for _ in range(4):
                    link(v.tensor_tensor(tmp[1], y, y, ALU.mult))
                    link(v.tensor_tensor(tmp[1], tmp[1], tmp[0], ALU.mult))
                    link(v.scalar_tensor_tensor(y, tmp[1], 1.5, y, ALU.add, ALU.mult))

            def stats(layer, hf):
                ts = range(hf * TPH, (hf + 1) * TPH)
                sl = slice(hf * TPH, (hf + 1) * TPH)
                if layer == 0:
                    dve.wait_ge(*sig.when(f"x_loaded{hf}", 0))
                else:
                    dve.wait_ge(*sig.when("x_done", (layer, hf)))
                for t in ts:
                    ins = v.bn_stats(st[:, t], x[:, t])
                link(ins)
                for t in ts:
                    ins = v.bn_aggr(mv[:, t], st[:, t])
                link(ins)
                link(v.tensor_scalar(rt[:, 0, sl], mv[:, sl, 1], LN_EPS, None, ALU.add))
                rsqrt(rs[:, sl], rt[:, 0, sl], (rt[:, 1, sl], rt[:, 2, sl]))
                if layer == 6:
                    link(v.tensor_tensor(rt[:, 0, sl], rs[:, sl], rs[:, sl], ALU.mult))
                    link(v.tensor_tensor(rt[:, 0, sl], rt[:, 0, sl], mv[:, sl, 1], ALU.mult))
                    link(v.tensor_scalar(rt[:, 0, sl], rt[:, 0, sl], LN_EPS, None, ALU.add))
                    rsqrt(rt[:, 3, sl], rt[:, 0, sl], (rt[:, 1, sl], rt[:, 2, sl]))
                    link(v.tensor_tensor(rs[:, sl], rs[:, sl], rt[:, 3, sl], ALU.mult))
                if layer or hf:
                    prev = (layer, 0, KT - 1) if hf else (layer - 1, 1, KT - 1)
                    dve.wait_ge(*sig.when("turn_product", prev))
                for t in ts:
                    v.tensor_scalar(xn[:, t % TPH], x[:, t], mv[:, t, 0:1], rs[:, t:t + 1], ALU.subtract, ALU.mult)\
                        .then_inc(*sig.mark("normalised", (layer, t)))
                if layer == 5:
                    dve.wait_ge(*sig.when("normalised", (layer, ts[-1])))
                    v.tensor_reduce(ab[:, sl], xn[:], AX.X, ALU.add, apply_absolute_value=True)\
                        .then_inc(*sig.mark("strength", hf))

            def turn(layer, hf):
                for c in range(KT):
                    key = (layer, hf, c)
                    cs = slice(hf * HALF, (hf + 1) * HALF)
                    if layer == 6:
                        dve.wait_ge(*sig.when("turn_high", key))
                        v.scalar_tensor_tensor(xT[:, 1, c, cs], psum(("turn", *key))[:], lnw[:, c:c + 1],
                                               xT[:, 0, c, cs].bitcast(FP32), ALU.mult, ALU.subtract)\
                            .then_inc(*sig.mark("turn_low", key))
                    else:
                        low("turn", key, xT[:, 1, c, cs], psum(("turn", *key))[:], xT[:, 0, c, cs])

            def v0_(t):
                p = P if t < TILES else CTX
                low("v0", t, v0[0:p, 1, t], psum(("v0", t))[0:p, 0:G0 * HD0], v0[0:p, 0, t])

            def k0_(s):
                low("k0", s, k0[:, s % 2, 1, :, 0:S], psum(("k0", s))[0:HD0].rearrange("p (b n) -> p b n", b=BPH),
                    k0[:, s % 2, 0, :, 0:S])

            def kc0_(s):
                low("kc0", s, k0[:, s % 2, 1, :, S:],
                    psum(("kc0", s))[0:HD0, 0:BPH * CTX].rearrange("p (b n) -> p b n", b=BPH), k0[:, s % 2, 0, :, S:])

            def q0_(s, h):
                low("q0", (s, h), q0[:, s % 2, 1, h], psum(("q0", s, h))[0:HD0], q0[:, s % 2, 0, h])

            def scores0(n, s, bl, h):
                for i in range(TPB):
                    dve.wait_ge(*sig.when("scores0_product", (n, i)))
                    ins = v.tensor_reduce(mx[:, n % 4, i:i + 1], psum(("scores0", n, i))[:, 0:KEYS0], AX.X, ALU.max,
                                          negate=True)
                link(ins)
                v.tensor_scalar(mx[:, n % 4, 2:4], mx[:, n % 4, 0:2], HD0 ** -0.5, None, ALU.mult)\
                    .then_inc(*sig.mark("max0", n))

            def turn0_scale(n):
                dve.wait_ge(*sig.when("exp0", (n, TPB - 1)))
                link(v.reciprocal(sm[:, n % 4, 2:4], sm[:, n % 4, 0:2]))
                for i in range(TPB):
                    v.tensor_scalar(e0[:, (2 * n + i) % 3], e0[:, (2 * n + i) % 3], sm[:, n % 4, 2 + i:3 + i], None, ALU.mult)\
                        .then_inc(*sig.mark("probs0", (n, i)))

            def turn0(n, s, bl, h):
                turn0_scale(n)
                dve.wait_ge(*sig.when("turn0_high", (n, 0)))
                v.tensor_tensor(eT0[:, n % 2, 1, 0:2], psum(("turn0", n, 0))[:].rearrange("p (k n) -> p k n", k=2),
                                eT0[:, n % 2, 0, 0:2].bitcast(FP32), ALU.subtract).then_inc(*sig.mark("turn0_low", (n, 0)))
                dve.wait_ge(*sig.when("turn0_high", (n, 1)))
                v.tensor_tensor(eT0[0:CTX, n % 2, 1, 2], psum(("turn0", n, 1))[0:CTX, 0:S],
                                eT0[0:CTX, n % 2, 0, 2].bitcast(FP32), ALU.subtract).then_inc(*sig.mark("turn0_low", (n, 1)))

            def pv0(n, s, bl, h):
                cs = slice(bl * S, (bl + 1) * S)
                low("pv0", n, q0[:, s % 2, 1, h, cs], psum(("pv0", n))[0:HD0, 0:S], q0[:, s % 2, 0, h, cs])

            def add_to_x(stage, key, t, src, name=None, mark=None, scale=None):
                dve.wait_ge(*sig.when(f"{stage}_product", key))
                if mark is None:
                    mark = (f"{stage}_added", key)
                if scale is None:
                    v.tensor_tensor(x[:, t], src, x[:, t], ALU.add).then_inc(*sig.mark(*mark))
                else:
                    v.scalar_tensor_tensor(x[:, t], src, scale, x[:, t], ALU.mult, ALU.add).then_inc(*sig.mark(*mark))

            def o0(s, i):
                t = (s % 2) * TPH + i
                if s >= 2:
                    dve.wait_ge(*sig.when("o0_added", (s - 2, i)))
                add_to_x("o0", (s, i), t, psum(("o0", s, i))[:])
                if s >= 2 * G0 - 2 and i == TPH - 1:
                    done(1, s % 2, "o0_added", (s, i))

            def done(layer, hf, name, key):
                dve.wait_ge(*sig.when(name, key))
                v.tensor_copy(rt[0:1, 3, 0:1], x[0:1, hf * TPH, 0:1]).then_inc(*sig.mark("x_done", (layer, hf)))

            def cut(n, p, out_ap, mark):
                link(v.tensor_scalar(f0[0:p, 3], f0[0:p, 1], ROUND, ROUND, ALU.add, ALU.subtract))
                link(v.tensor_tensor(f0[0:p, 4], f0[0:p, 1], f0[0:p, 3], ALU.subtract))
                link(v.scalar_tensor_tensor(f0[0:p, 4], f0[0:p, 4], 0.0, f0[0:p, 3], ALU.is_lt, ALU.subtract))
                link(v.tensor_tensor(f0[0:p, 3], f0[0:p, 4], f0[0:p, 2], ALU.mult))
                ins = v.tensor_scalar(out_ap, f0[0:p, 3], -128.0, 127.0, ALU.max, ALU.min)
                if mark:
                    ins.then_inc(*mark)
                else:
                    link(ins)

            def up0(f, hf):
                w, n = fwidth(f), 2 * f + hf
                dve.wait_ge(*sig.when("silu0", n))
                dve.wait_ge(*sig.when("up0_product", (f, hf, 1)))
                if n >= 1:
                    dve.wait_ge(*sig.when("sign0", n - 1))
                if n == 0:
                    dve.wait_ge(*sig.when("pv0_product", 63))
                v.tensor_tensor(f0[0:w, 0], psum(("up0", f, hf, 1))[0:w], g0[0:w, n % 2], ALU.mult)\
                    .then_inc(*sig.mark("inter0", n))
                dve.wait_ge(*sig.when("sign0", n))
                dve.wait_ge(*sig.when("abs0", n))
                if f >= half_f:
                    dve.wait_ge(*sig.when("down0_product", (0, TILES - 1)))
                cut(n, w, h0[0:w, f % half_f, hf * HALF:(hf + 1) * HALF], sig.mark("h0_done", n))

            def down0(part, t):
                if part == 0:
                    return
                dve.wait_ge(*sig.when("down0_product", (part, t)))
                dve.wait_ge(*sig.when("down0_part", t))
                if t:
                    dve.wait_ge(*sig.when("x_done0", t - 1))
                    dve.wait_ge(*sig.when("dsign0", t - 1))
                else:
                    dve.wait_ge(*sig.when("h0_done", 2 * FT - 1))
                    dve.wait_ge(*sig.when("sign0", 2 * FT - 1))
                v.tensor_tensor(f0[:, 0], psum(("down0", part, t))[:], acc0[:, t], ALU.add)\
                    .then_inc(*sig.mark("down0_sum", t))
                dve.wait_ge(*sig.when("dsign0", t))
                cut(t, P, f0[:, 0], None)
                v.tensor_tensor(x[:, t], x[:, t], f0[:, 0], ALU.add).then_inc(*sig.mark("x_done0", t))
                if t % TPH == TPH - 1:
                    done(2, t // TPH, "x_done0", t)

            def scores1(layer, b):
                dve.wait_ge(*sig.when("scores1_product", (layer, b)))
                src = psum(("scores1", layer, b))[:, 0:TPB * CTX].rearrange("p (i n) -> p i n", i=TPB)
                if layer == 2:
                    dve.wait_ge(*sig.when("c2_ready", 0))
                    if b >= 2:
                        dve.wait_ge(*sig.when("exp1", (layer, b - 2, TPB - 1)))
                    for i in range(TPB):
                        ins = v.tensor_tensor(s1[:, b % 2, i], src[:, i], c2[:, b * CTX:(b + 1) * CTX], ALU.add)
                    ins.then_inc(*sig.mark("biased2", b))
                    dve.wait_ge(*sig.when("biased2", b))
                    src = s1[:, b % 2]
                link(v.tensor_reduce(mx[:, b % 4, 0:2], src, AX.X, ALU.max, negate=True))
                v.tensor_scalar(mx[:, b % 4, 2:4], mx[:, b % 4, 0:2], 1.0 if layer == 1 else D ** -0.5, None, ALU.mult)\
                    .then_inc(*sig.mark("max1", (layer, b)))
                dve.wait_ge(*sig.when("exp1", (layer, b, TPB - 1)))
                link(v.reciprocal(sm[:, b % 4, 2:4], sm[:, b % 4, 0:2]))
                for i in range(TPB):
                    v.tensor_scalar(e1[:, b % 2, i], e1[:, b % 2, i], sm[:, b % 4, 2 + i:3 + i], None, ALU.mult)\
                        .then_inc(*sig.mark("probs1", (layer, b, i)))

            def pv1(layer, b):
                low("turn1", (layer, b), eT1[:, b % 2, 1], psum(("turn1", layer, b))[0:CTX, 0:S], eT1[:, b % 2, 0])
                for i in range(TPB):
                    add_to_x("pv1", (layer, b, i), TPB * b + i, psum(("pv1", layer, b, i))[:])
                if b % BPH == BPH - 1:
                    done(3 if layer == 1 else 5, b // BPH, "pv1_added", (layer, b, 1))

            def router1():
                low("router1", 0, rw[:, 1], psum(("router1",))[:, 0:KT * NE].rearrange("p (k n) -> p k n", k=KT), rw[:, 0])

            def route1(t):
                dve.wait_ge(*sig.when("route1_product", t))
                ss = r1[:, 0, t]
                link(v.tensor_copy(ss, psum(("route1", t))[:, 0:NE]))
                link(v.max(top8[:, 0, t], ss))
                link(v.match_replace(r1[:, 1, t], top8[:, 0, t], ss, -1e30))
                link(v.max(top8[:, 1, t], r1[:, 1, t]))
                link(v.match_replace(r1[:, 1, t], top8[:, 1, t], r1[:, 1, t], -1e30))
                v.tensor_scalar(rs[:, t:t + 1], top8[:, 0, t, 0:1], -1.0, None, ALU.mult)\
                    .then_inc(*sig.mark("route1_rep", t))
                dve.wait_ge(*sig.when("route1_exp", (t, 3)))
                link(v.tensor_tensor(r1[:, 0, t], r1[:, 2, t], r1[:, 3, t], ALU.subtract))
                link(v.tensor_reduce(rt[:, 1, t:t + 1], r1[:, 0, t], AX.X, ALU.add))
                link(v.reciprocal(rt[:, 2, t:t + 1], rt[:, 1, t:t + 1]))
                v.tensor_scalar(r1[:, 1, t], r1[:, 0, t], rt[:, 2, t:t + 1], None, ALU.mult)\
                    .then_inc(*sig.mark("gate1", t))

            def z1(t):
                pass

            def zt1(t):
                dve.wait_ge(*sig.when("z1_product", t))
                dve.wait_ge(*sig.when("gate1", t))
                if t >= 2:
                    dve.wait_ge(*sig.when("zt1_product", t - 2))
                v.tensor_tensor(zg[:, t % 2].rearrange("p (e r) -> p e r", e=NE),
                                psum(("z1", t))[:].rearrange("p (e r) -> p e r", e=NE),
                                r1[:, 1, t].unsqueeze(2).broadcast_to((P, NE, RANK)), ALU.mult)\
                    .then_inc(*sig.mark("gated1", t))
                low("zt1", t, zT[:, t % 2, 1], psum(("zt1", t))[:].rearrange("p (k n) -> p k n", k=KT), zT[:, t % 2, 0])

            def b1(t):
                add_to_x("b1", t, t, psum(("b1", t))[:], scale=2.0)
                if t % TPH == TPH - 1:
                    done(4, t // TPH, "b1_added", t)

            def k2_(c):
                dve.wait_ge(*sig.when("k2_high", c))
                v.scalar_tensor_tensor(k2[:, 1, c], psum(("k2", c))[:, 0:B * CTX], bk[:, c:c + 1],
                                       k2[:, 0, c].bitcast(FP32), ALU.add, ALU.subtract).then_inc(*sig.mark("k2_low", c))

            def m2_(c):
                low("m2", c, m2[:, 1, c], psum(("m2", c))[:, 0:B * CTX], m2[:, 0, c])

            def c2_():
                dve.wait_ge(*sig.when("loaded_bq", 0))
                dve.wait_ge(*sig.when("ones_ready", 0))
                for c in range(KT):
                    ins = v.tensor_scalar(bqf[:, c], bqf[:, c], bq[:, c:c + 1], None, ALU.mult)
                ins.then_inc(*sig.mark("bq_wide", 0))
                dve.wait_ge(*sig.when("bq_high", 0))
                v.tensor_tensor(bqw[:, 1], bqf[:], bqw[:, 0].bitcast(FP32), ALU.subtract).then_inc(*sig.mark("bq_low", 0))

            def gate2(t):
                if t == 0:
                    dve.wait_ge(*sig.when("gw_high", 0))
                    v.tensor_tensor(gw[:, 1], gwf[:], gw[:, 0].bitcast(FP32), ALU.subtract).then_inc(*sig.mark("gw_low", 0))
                dve.wait_ge(*sig.when("gate2_product", t))
                v.tensor_copy(lg[:, t, 0:MOE], psum(("gate2", t))[:, 0:MOE]).then_inc(*sig.mark("logits2", t))

            def moe():
                dve.wait_ge(*sig.when("strength_product", 0))
                pb = psum(("strength",))
                dve.wait_ge(*sig.when("logits2", TILES - 1))
                link(v.tensor_copy(ra[:, 0, 0:3 * B], pb[:, 0:3 * B]) if False else
                     v.tensor_copy(gt[:, 0:3, 0:B], pb[:, 0:3 * B].rearrange("p (a b) -> p a b", a=3)))
                link(v.tensor_tensor(ra[:, 0, 0:B], gt[:, 1, 0:B], gt[:, 2, 0:B], ALU.add))
                link(v.tensor_scalar(ra[:, 0, 0:B], ra[:, 0, 0:B], 1.0 / ((S - VISION) * D), None, ALU.mult))
                link(v.tensor_scalar(ra[:, 1, 0:B], gt[:, 0, 0:B], 1.0 / (VISION * D), 1e-8, ALU.mult, ALU.add))
                link(v.reciprocal(ra[:, 2, 0:B], ra[:, 1, 0:B]))
                ratio = ra[:, 3, :].rearrange("p (b i) -> p b i", i=TPB)
                for i in range(TPB):
                    ins = v.tensor_tensor(ratio[:, :, i], ra[:, 0, 0:B], ra[:, 2, 0:B], ALU.mult)
                link(ins)
                dve.wait_ge(*sig.when("loaded_gwr", 0))
                dve.wait_ge(*sig.when("loaded_gbr", 0))
                for e in range(MOE):
                    link(v.scalar_tensor_tensor(lg[:, :, e], ra[:, 3], gwr[:, e:e + 1], lg[:, :, e], ALU.mult, ALU.add))
                    link(v.tensor_scalar(lg[:, :, e], lg[:, :, e], gbr[:, e:e + 1], None, ALU.add))
                link(v.tensor_reduce(gt[:, 0], lg[:, :, 0:MOE], AX.X, ALU.max))
                v.tensor_tensor(lg[:, :, 0:MOE], lg[:, :, 0:MOE], gt[:, 0].unsqueeze(2).broadcast_to((P, TILES, MOE)),
                                ALU.subtract).then_inc(*sig.mark("moe_shift", 0))
                dve.wait_ge(*sig.when("moe_exp", 0))
                link(v.tensor_reduce(gt[:, 1], lg[:, :, 0:MOE], AX.X, ALU.add))
                link(v.reciprocal(gt[:, 2], gt[:, 1]))
                dve.wait_ge(*sig.when("pool_gate", "p8"))
                link(v.tensor_tensor(p8[:, :, 0:MOE], lg[:, :, 0:MOE], gt[:, 2].unsqueeze(2).broadcast_to((P, TILES, MOE)),
                                     ALU.mult))
                for t in range(TILES):
                    ins = v.max(t8[:, t], p8[:, t])
                link(ins)
                link(v.tensor_tensor(gt[:, 3], t8[:, :, 0], t8[:, :, 1], ALU.add))
                link(v.tensor_scalar(gt[:, 3], gt[:, 3], 1e-8, None, ALU.add))
                link(v.reciprocal(gt[:, 4], gt[:, 3]))
                link(v.tensor_tensor(gt[:, 5], t8[:, :, 0], gt[:, 4], ALU.mult))
                link(v.tensor_tensor(gt[:, 6], t8[:, :, 1], gt[:, 4], ALU.mult))
                A_, B_, C_ = (p8[:, :, e] for e in range(MOE))
                link(v.tensor_tensor(gt[:, 7], A_, B_, ALU.is_ge))
                link(v.tensor_tensor(gt[:, 8], A_, C_, ALU.is_ge))
                link(v.tensor_tensor(gt[:, 9], B_, C_, ALU.is_ge))
                link(v.tensor_scalar(gt[:, 10], gt[:, 7], -1.0, 1.0, ALU.mult, ALU.add))
                link(v.tensor_scalar(gt[:, 11], gt[:, 9], -1.0, 1.0, ALU.mult, ALU.add))
                link(v.tensor_scalar(gt[:, 4], gt[:, 8], -1.0, 1.0, ALU.mult, ALU.add))
                for i, e, p_, q_ in ((0, 0, 7, 8), (0, 1, 10, 9), (0, 2, 4, 11), (1, 2, 8, 9), (1, 1, 7, 11), (1, 0, 10, 4)):
                    link(v.tensor_tensor(fl[:, i, e], gt[:, p_], gt[:, q_], ALU.mult))
                link(v.tensor_tensor(fl[:, 1], fl[:, 0], fl[:, 1], ALU.add))
                v.tensor_scalar(fl[:, 1], fl[:, 1], -1.0, 1.0, ALU.mult, ALU.add).then_inc(*sig.mark("choice2", 0))
                dve.wait_ge(*sig.when("choice_product", 0))
                src = psum(("choice",))[:, 0:2 * MOE * TILES].rearrange("p (a b i) -> p a b i", a=2 * MOE, i=TPB)
                fbv = fb[:].rearrange("p c e t -> p (c e) t").rearrange("p a (b i) -> p a b i", i=TPB)
                for i in range(TPB):
                    ins = v.tensor_copy(fbv[:, :, :, i], src[:, :, :, 0])
                link(ins)
                for e in range(MOE):
                    link(v.tensor_tensor(cf[:, e], fb[:, 0, e], gt[:, 5], ALU.mult))
                    link(v.tensor_tensor(gt[:, 3], fb[:, 1, e], gt[:, 6], ALU.mult))
                    link(v.tensor_tensor(cf[:, e], cf[:, e], gt[:, 3], ALU.add))

            def hid2(e, c, hf):
                i = (e * KT + c) * 2 + hf
                dve.wait_ge(*sig.when("hid2_value", (e, c, hf)))
                if e >= 2:
                    dve.wait_ge(*sig.when("out2_product", (e - 2, TILES - 1)))
                v.tensor_copy(h2[:, e % 2, 0, c, hf * HALF:(hf + 1) * HALF], hf2[:, i % 2])\
                    .then_inc(*sig.mark("h2_high", (e, c, hf)))

            def out2(e, t):
                dve.wait_ge(*sig.when("out2_product", (e, t)))
                dve.wait_ge(*sig.when("loaded_b2b", 0))
                if (e, t) != (0, 0):
                    dve.wait_ge(*sig.when("out2_added", (e, t - 1) if t else (e - 1, TILES - 1)))
                link(v.tensor_tensor(y2[:], psum(("out2", e, t))[:], b2b[:, e], ALU.add))
                v.scalar_tensor_tensor(x[:, t], y2[:], cf[:, e, t:t + 1], x[:, t], ALU.mult, ALU.add)\
                    .then_inc(*sig.mark("out2_added", (e, t)))
                if e == MOE - 1 and t % TPH == TPH - 1:
                    done(6, t // TPH, "out2_added", (e, t))

            def k3_(c):
                low("k3", c, kr3[:, 1, c], psum(("k3", c))[:, 0:B * CTX], kr3[:, 0, c])

            def v3_(b):
                low("v3", b, v3[:, 1, b], psum(("v3", b))[0:CTX, 0:KV3 * HD3], v3[:, 0, b])

            def q3_(c, hf):
                cs = slice(hf * HALF, (hf + 1) * HALF)
                low("q3", (c, hf), q3[:, 1, c, cs], psum(("q3", c, hf))[:], q3[:, 0, c, cs])

            def keys3(n, b, c):
                dve.wait_ge(*sig.when("head_mask", 0))
                dve.wait_ge(*sig.when("k3_low", c))
                if n >= 2:
                    dve.wait_ge(*sig.when("scores3_product", (n - 2, TPB - 1)))
                for part in range(2):
                    ins = v.tensor_tensor(kd3[:, n % 2, part],
                                          kr3[:, part, c, b * CTX:(b + 1) * CTX].bitcast(FP32).unsqueeze(1).broadcast_to((P, HPC, CTX)),
                                          hm3[:].unsqueeze(2).broadcast_to((P, HPC, CTX)), ALU.mult)
                ins.then_inc(*sig.mark("keys3", n))

            def values3(n, b, c):
                if n >= 2:
                    dve.wait_ge(*sig.when("pv3_product", n - 2))
                dve.wait_ge(*sig.when("vd3_clear", 0))
                dve.wait_ge(*sig.when("v3_low", b))
                for part in range(2):
                    for p in range(PAIRS):
                        kv = (c * HPC + 2 * p) // REP3
                        for j in range(2):
                            r = slice(CTX * j, CTX * (j + 1))
                            col = (2 * p + j) * HD3
                            ins = v.tensor_copy(vd3[r, n % 2, part, p, col:col + HD3],
                                                v3[:, part, b, kv * HD3:(kv + 1) * HD3].bitcast(FP32))
                ins.then_inc(*sig.mark("values3", n))

            def scores3(n, b, c):
                for i in range(TPB):
                    dve.wait_ge(*sig.when("scores3_product", (n, i)))
                    src = psum(("scores3", n, i))[:].rearrange("p (h k) -> p h k", h=HPC)
                    link(v.tensor_reduce(mx[:, n % 4, i * HPC:(i + 1) * HPC], src, AX.X, ALU.max))
                    if n >= 2:
                        dve.wait_ge(*sig.when("turn3_product", (n - 2, 1)))
                    v.tensor_tensor(e3[:, n % 2, i].rearrange("p (h k) -> p h k", h=HPC), src,
                                    mx[:, n % 4, i * HPC:(i + 1) * HPC].unsqueeze(2).broadcast_to((P, HPC, CTX)),
                                    ALU.subtract).then_inc(*sig.mark("shift3", (n, i)))

            def turn3(n, b, c):
                for i in range(TPB):
                    dve.wait_ge(*sig.when("exp3", (n, i)))
                    e = e3[:, n % 2, i].rearrange("p (h k) -> p h k", h=HPC)
                    hs = slice(i * HPC, (i + 1) * HPC)
                    link(v.tensor_reduce(sm[:, n % 4, hs], e, AX.X, ALU.add))
                    link(v.reciprocal(mx[:, n % 4, hs], sm[:, n % 4, hs]))
                    v.tensor_tensor(e, e, mx[:, n % 4, hs].unsqueeze(2).broadcast_to((P, HPC, CTX)), ALU.mult)\
                        .then_inc(*sig.mark("probs3", (n, i)))
                for i in range(2):
                    dve.wait_ge(*sig.when("turn3_high", (n, i)))
                    v.tensor_tensor(eT3[:, 1, 2 * i:2 * i + 2], psum(("turn3", n, i))[:].rearrange("p (k n) -> p k n", k=2),
                                    eT3[:, 0, 2 * i:2 * i + 2].bitcast(FP32), ALU.subtract)\
                        .then_inc(*sig.mark("turn3_low", (n, i)))

            def pv3(n, b, c):
                cs = slice(b * S, (b + 1) * S)
                low("pv3", n, q3[:, 1, c, cs], psum(("pv3", n))[:, 0:S], q3[:, 0, c, cs])

            def o3(t):
                add_to_x("o3", t, t, psum(("o3", t))[:])
                if t % TPH == TPH - 1:
                    done(7, t // TPH, "o3_added", t)

            def up3(f, hf):
                w, n = fwidth(f), 2 * f + hf
                cs = slice(hf * HALF, (hf + 1) * HALF)
                fi = f % half_f
                dve.wait_ge(*sig.when("silu3", n))
                dve.wait_ge(*sig.when("up3_product", (f, hf, 1)))
                if f >= half_f:
                    dve.wait_ge(*sig.when("down3_product", (0, TILES - 1)))
                if n == 0:
                    dve.wait_ge(*sig.when("o3_product", TILES - 1))
                link(v.tensor_tensor(g3[0:w, n % 3], psum(("up3", f, hf, 1))[0:w], g3[0:w, n % 3], ALU.mult))
                link(v.tensor_copy(h3[0:w, 0, fi, cs], g3[0:w, n % 3]))
                v.tensor_tensor(h3[0:w, 1, fi, cs], g3[0:w, n % 3], h3[0:w, 0, fi, cs].bitcast(FP32), ALU.subtract)\
                    .then_inc(*sig.mark("h3_low", n))

            def down3(part, t):
                if part:
                    dve.wait_ge(*sig.when("down3_added", (0, t)))
                add_to_x("down3", (part, t), t, psum(("down3", part, t))[:])

            def nf_max_(m, f):
                w = fwidth(f) if m < 2 else P
                n = D if m < 2 or f < 10 else 6 * BLOCK
                dve.wait_ge(*sig.when("nf4_rows", (m, f)))
                if (m, f) == (0, 0):
                    link(v.memset(nf_m[:], 0.0))
                v.tensor_reduce(nf_m[0:w, 0, f * 8:f * 8 + n // BLOCK], nf_w[0:w, 0:n].rearrange("p (b k) -> p b k", k=BLOCK),
                                AX.X, ALU.max, apply_absolute_value=True).then_inc(*sig.mark("nf4_max", (m, f)))
                if f == FT - 1:
                    dve.wait_ge(*sig.when("nf4_max", (m, f)))
                    c = 88 if m < 2 else 86
                    if m:
                        dve.wait_ge(*sig.when("nf4_turn_product", m - 1))
                    link(v.tensor_copy(nf_m[:, 1, 0:88], nf_m[:, 0, 0:88]))
                    link(v.tensor_scalar(nf_m[:, 2, 0:88], nf_m[:, 1, 0:88], TINY, None, ALU.max))
                    v.reciprocal(nf_m[:, 2, 0:88], nf_m[:, 2, 0:88]).then_inc(*sig.mark("nf4_rcp", m))

            def nf(n, m, f, j):
                w = fwidth(f)
                rows, size = (P, KT * w) if m < 2 else (w, D)
                if j == 0:
                    return
                if j == 1:
                    dve.wait_ge(*sig.when("nf4_weights", n))
                    v.tensor_tensor(nf_w[0:rows, 0:size], nf_w[0:rows, 0:size], nf_r[0:rows, 0:size], ALU.mult)\
                        .then_inc(*sig.mark("nf4_scaled", n))
                    dve.wait_ge(*sig.when("nf4_scaled", n))
                    if n:
                        dve.wait_ge(*sig.when("nf4_dequantised", n - 1))
                    link(v.tensor_scalar(nf_acc[0:rows, 0:size], nf_w[0:rows, 0:size], float(BOUNDS[0]), CODE_STEPS[0],
                                         ALU.is_gt, ALU.mult))
                    v.tensor_scalar(nf_acc[0:rows, 0:size], nf_acc[0:rows, 0:size], float(CODE[0]), None, ALU.add)\
                        .then_inc(*sig.mark("nf4_step", (n, 1)))
                else:
                    if j >= 4:
                        dve.wait_ge(*sig.when("nf4_added", (n, j - 2)))
                    elif n:
                        dve.wait_ge(*sig.when("nf4_added", (n - 1, len(BOUNDS))))
                    v.tensor_scalar(nf_y[0:rows, j % 2, 0:size], nf_w[0:rows, 0:size], float(BOUNDS[j - 1]),
                                    CODE_STEPS[j - 1], ALU.is_gt, ALU.mult).then_inc(*sig.mark("nf4_step", (n, j)))

            handlers = {"stats": stats, "turn": turn, "v0": v0_, "k0": k0_, "kc0": kc0_, "q0": q0_, "scores0": scores0,
                        "turn0": turn0, "pv0": pv0, "o0": o0, "up0": up0, "down0": down0, "scores1": scores1,
                        "pv1": pv1, "router1": router1, "route1": route1, "z1": z1, "zt1": zt1, "b1": b1, "k2": k2_,
                        "m2": m2_, "c2": c2_, "gate2": gate2, "moe": moe, "hid2": hid2, "out2": out2, "k3": k3_,
                        "v3": v3_, "q3": q3_, "keys3": keys3, "values3": values3, "scores3": scores3, "turn3": turn3,
                        "pv3": pv3, "o3": o3, "up3": up3,
                        "down3": down3, "nf_max": nf_max_, "nf": nf}
            for s in steps:
                if s[0] == "k2" and s[1] == 0:
                    dve.wait_ge(*sig.when("pv1_product", (1, B - 1, 1)))
                    v.memset(bqf[:], 1.0).then_inc(*sig.mark("ones_ready", 0))
                if s[0] in handlers:
                    handlers[s[0]](*s[1:])

        @block.tensor
        def _(pe):
            mm = nc.tensor.matmul
            here = [0]

            def claim(key, *freed_by):
                n, ended = sig.next_bank(key, *freed_by)
                for event in ended:
                    pe.wait_ge(*sig.when(*event))
                return banks[n]

            def need(name, user):
                if known:
                    pe.wait_ge(*sig.when("weight_low", chunk_no[name]))
                sig.user["chunk", name] = user
                sig.last_step[name] = here[0]
                return weight(name, 0), weight(name, 1)

            def product(dst, pairs):
                passes = []
                for l_, r_ in pairs:
                    if len(r_) == 1:
                        passes += [(l_[1], r_[0]), (l_[0], r_[0])]
                    elif len(l_) == 1:
                        passes += [(l_[0], r_[1]), (l_[0], r_[0])]
                    else:
                        passes += [(l_[1], r_[0]), (l_[0], r_[1]), (l_[0], r_[0])]
                for i, (l_, r_) in enumerate(passes):
                    ins = mm(dst, l_, r_, start=i == 0, stop=i == len(passes) - 1)
                return ins

            def cols(parts, *ix):
                return [p[ix] for p in parts]

            def xt(k, c0, c1):
                return [xT[:, p, k, c0:c1] for p in range(2)]

            ALL = slice(None)

            def xt_ready(hf):
                pe.wait_ge(*sig.when("turn_low", (layer_of[hf], hf, KT - 1)))

            layer_of = {}

            def turn(layer, hf):
                layer_of[hf] = layer
                pe.wait_ge(*sig.when("ident_ready", 0))
                for c in range(KT):
                    key = (layer, hf, c)
                    bank = claim(("turn", *key), ("turn_low", key))
                    for i in range(TPH):
                        pe.wait_ge(*sig.when("normalised", (layer, hf * TPH + i)))
                        ins = nc.tensor.transpose(bank[:, i * P:(i + 1) * P], xn[:, i, c * P:(c + 1) * P], ident[:])
                    ins.then_inc(*sig.mark("turn_product", key))

            def v0_(t):
                user = ("v0_product", t)
                w = [need(("v0", i), user) for i in range(2)]
                p = P if t < TILES else CTX
                if t < TILES:
                    xt_ready(t // TPH)
                bank = claim(("v0", t), ("v0_low", t))
                pairs = []
                for k in range(KT):
                    l_ = xt(k, t * P, (t + 1) * P) if t < TILES else \
                        [ctxT[:, q, k, (t - TILES) * CTX:(t - TILES + 1) * CTX] for q in range(2)]
                    pairs.append((l_, [w[k // 2][q][:, k % 2] for q in range(2)]))
                product(bank[0:p, 0:G0 * HD0], pairs).then_inc(*sig.mark(*user))

            def qk(s, user, c0, c1, moving, dst):
                g = s // 2
                w = [need(("qk0", g, i), user) for i in range(2)]
                pairs = [([w[k // 2][q][:, k % 2, c0:c1] for q in range(2)], moving(k)) for k in range(KT)]
                product(dst, pairs).then_inc(*sig.mark(*user))

            def k0_(s):
                hf = s % 2
                xt_ready(hf)
                bank = claim(("k0", s), ("k0_low", s))
                qk(s, ("k0_product", s), HPG * HD0, (HPG + 1) * HD0, lambda k: xt(k, hf * HALF, (hf + 1) * HALF), bank[0:HD0])

            def kc0_(s):
                hf = s % 2
                bank = claim(("kc0", s), ("kc0_low", s))
                n = BPH * CTX
                qk(s, ("kc0_product", s), HPG * HD0, (HPG + 1) * HD0,
                   lambda k: [ctxT[:, q, k, hf * n:(hf + 1) * n] for q in range(2)], bank[0:HD0, 0:n])

            def q0_(s, h):
                hf = s % 2
                bank = claim(("q0", s, h), ("q0_low", (s, h)))
                qk(s, ("q0_product", (s, h)), h * HD0, (h + 1) * HD0, lambda k: xt(k, hf * HALF, (hf + 1) * HALF), bank[0:HD0])

            def scores0(n, s, bl, h):
                pe.wait_ge(*sig.when("q0_low", (s, h)))
                pe.wait_ge(*sig.when("k0_low", s))
                pe.wait_ge(*sig.when("kc0_low", s))
                for i in range(TPB):
                    bank = claim(("scores0", n, i), ("exp0", (n, i)))
                    l_ = [q0[:, s % 2, p, h, bl * S + i * P:bl * S + (i + 1) * P] for p in range(2)]
                    product(bank[:, 0:KEYS0], [(l_, [k0[:, s % 2, p, bl] for p in range(2)])])\
                        .then_inc(*sig.mark("scores0_product", (n, i)))

            def turn0(n, s, bl, h):
                b0 = claim(("turn0", n, 0), ("turn0_low", (n, 0)))
                b1_ = claim(("turn0", n, 1), ("turn0_low", (n, 1)))
                for i in range(TPB):
                    pe.wait_ge(*sig.when("probs0", (n, i)))
                    for k in range(2):
                        nc.tensor.transpose(b0[:, (2 * k + i) * P:(2 * k + i + 1) * P], e0[:, (2 * n + i) % 3, k * P:(k + 1) * P], ident[:])
                    ins = nc.tensor.transpose(b1_[0:CTX, i * P:(i + 1) * P], e0[:, (2 * n + i) % 3, S:KEYS0], ident[:])
                ins.then_inc(*sig.mark("turn0_product", n))

            def pv0(n, s, bl, h):
                g, b = s // 2, (s % 2) * BPH + bl
                pe.wait_ge(*sig.when("v0_low", TILES + B - 1))
                pe.wait_ge(*sig.when("turn0_low", (n, 1)))
                bank = claim(("pv0", n), ("pv0_low", n))
                pairs = []
                for k, (t, p) in enumerate(((TPB * b, P), (TPB * b + 1, P), (TILES + b, CTX))):
                    pairs.append(([v0[0:p, q, t, g * HD0:(g + 1) * HD0] for q in range(2)],
                                  [eT0[0:p, n % 2, q, k] for q in range(2)]))
                product(bank[0:HD0, 0:S], pairs).then_inc(*sig.mark("pv0_product", n))

            def o0(s, i):
                user = ("o0_product", (s, i))
                w = [need(("o0", s // 2, j), user) for j in range(2)]
                pe.wait_ge(*sig.when("pv0_low", 8 * s + 7))
                bank = claim(("o0", s, i), ("o0_added", (s, i)))
                pairs = [([q0[:, s % 2, p, h, i * P:(i + 1) * P] for p in range(2)], [w[h // 2][p][:, h % 2] for p in range(2)])
                         for h in range(HPG)]
                product(bank[:], pairs).then_inc(*sig.mark(*user))

            def up(stage, f, hf, freed_by):
                w = fwidth(f)
                xt_ready(hf)
                for m in range(2):
                    user = (f"{stage}_product", (f, hf, m))
                    parts = need((stage, f), user)
                    bank = claim((stage, f, hf, m), freed_by[m])
                    pairs = [([q[:, m, k] for q in parts], xt(k, hf * HALF, (hf + 1) * HALF)) for k in range(KT)]
                    product(bank[0:w], pairs).then_inc(*sig.mark(*user))

            def down_chunk(stage, f, lo, user):
                first = lo + (f - lo) // 2 * 2
                if (stage, first) in chunk_no and f != first and (stage, f) not in chunk_no:
                    parts = need((stage, first), user)
                    return [q[0:fwidth(f), 1] for q in parts]
                parts = need((stage, f), user)
                return [q[0:fwidth(f), 0] for q in parts]

            def down0(part, t):
                user = ("down0_product", (part, t))
                lo, hi = (0, half_f) if part == 0 else (half_f, FT)
                pe.wait_ge(*sig.when("h0_done", 2 * hi - 1))
                bank = claim(("down0", part, t), ("down0_sum" if part else "down0_part", t))
                pairs = [([h0[0:fwidth(f), f % half_f, t * P:(t + 1) * P]], down_chunk("down0", f, lo, user))
                         for f in range(lo, hi)]
                product(bank[:], pairs).then_inc(*sig.mark(*user))

            def scores1(layer, b):
                if layer == 1:
                    keys = ctxT
                else:
                    keys = m2
                    pe.wait_ge(*sig.when("m2_low", KT - 1))
                xt_ready(b // BPH)
                reader = ("exp1", (layer, b, TPB - 1)) if layer == 1 else ("biased2", b)
                bank = claim(("scores1", layer, b), reader)
                for i in range(TPB):
                    t = TPB * b + i
                    pairs = [(xt(k, t * P, (t + 1) * P), [keys[:, q, k, b * CTX:(b + 1) * CTX] for q in range(2)])
                             for k in range(KT)]
                    ins = product(bank[:, i * CTX:(i + 1) * CTX], pairs)
                ins.then_inc(*sig.mark("scores1_product", (layer, b)))

            def pv1(layer, b):
                bank = claim(("turn1", layer, b), ("turn1_low", (layer, b)))
                for i in range(TPB):
                    pe.wait_ge(*sig.when("probs1", (layer, b, i)))
                    ins = nc.tensor.transpose(bank[0:CTX, i * P:(i + 1) * P], e1[:, b % 2, i], ident[:])
                ins.then_inc(*sig.mark("turn1_product", (layer, b)))
                pe.wait_ge(*sig.when("turn1_low", (layer, b)))
                if known:
                    pe.wait_ge(*sig.when("weight_low", chunk_no["ctxN", 1]))
                for i in range(TPB):
                    bank = claim(("pv1", layer, b, i), ("pv1_added", (layer, b, i)))
                    product(bank[:], [([eT1[:, b % 2, q, i * P:(i + 1) * P] for q in range(2)],
                                       [ctxN[:, q, b] for q in range(2)])])\
                        .then_inc(*sig.mark("pv1_product", (layer, b, i)))

            def router1():
                pe.wait_ge(*sig.when("loaded_wq1", 0))
                pe.wait_ge(*sig.when("loaded_keyT", 0))
                bank = claim(("router1",), ("router1_low", 0))
                for k in range(KT):
                    ins = mm(bank[:, k * NE:(k + 1) * NE], wq1[:, k * P:(k + 1) * P], keyT[:], start=True, stop=True)
                ins.then_inc(*sig.mark("router1_product", 0))

            def route1(t):
                pe.wait_ge(*sig.when("router1_low", 0))
                xt_ready(t // TPH)
                bank = claim(("route1", t), ("route1_rep", t))
                pairs = [(xt(k, t * P, (t + 1) * P), [rw[:, q, k] for q in range(2)]) for k in range(KT)]
                product(bank[:, 0:NE], pairs).then_inc(*sig.mark("route1_product", t))

            def z1(t):
                user = ("z1_product", t)
                w = [need(("z1", i), user) for i in range(2)]
                xt_ready(t // TPH)
                bank = claim(("z1", t), ("gated1", t))
                pairs = [(xt(k, t * P, (t + 1) * P), [w[k // 2][q][:, k % 2] for q in range(2)]) for k in range(KT)]
                product(bank[:], pairs).then_inc(*sig.mark(*user))

            def zt1(t):
                pe.wait_ge(*sig.when("gated1", t))
                bank = claim(("zt1", t), ("zt1_low", t))
                for c in range(KT):
                    ins = nc.tensor.transpose(bank[:, c * P:(c + 1) * P], zg[:, t % 2, c * P:(c + 1) * P], ident[:])
                ins.then_inc(*sig.mark("zt1_product", t))

            def b1(t):
                user = ("b1_product", t)
                w = [need(("b1", i), user) for i in range(2)]
                pe.wait_ge(*sig.when("zt1_low", t))
                bank = claim(("b1", t), ("b1_added", t))
                pairs = [([zT[:, t % 2, q, k] for q in range(2)], [w[k // 2][q][:, k % 2] for q in range(2)]) for k in range(KT)]
                product(bank[:], pairs).then_inc(*sig.mark(*user))

            def ctx_product(stage, c, moving, freed_by):
                user = (f"{stage}_product", c)
                w = [need((stage, i), user) for i in range(2)]
                if stage == "m2":
                    pe.wait_ge(*sig.when("k2_low", KT - 1))
                bank = claim((stage, c), freed_by)
                pairs = [([w[k // 2][q][:, k % 2, c * P:(c + 1) * P] for q in range(2)], [moving[:, q, k] for q in range(2)])
                         for k in range(KT)]
                product(bank[:, 0:B * CTX], pairs).then_inc(*sig.mark(*user))

            def c2_():
                pe.wait_ge(*sig.when("bq_low", 0))
                bank = claim(("c2",), ("c2_ready", 0))
                pairs = [([bqw[:, q, k] for q in range(2)], [k2[:, q, k] for q in range(2)]) for k in range(KT)]
                product(bank[:, 0:B * CTX], pairs).then_inc(*sig.mark("c2_product", 0))

            def gate2(t):
                pe.wait_ge(*sig.when("gw_low", 0))
                xt_ready(t // TPH)
                bank = claim(("gate2", t), ("logits2", t))
                pairs = [(xt(k, t * P, (t + 1) * P), [gw[:, q, k] for q in range(2)]) for k in range(KT)]
                product(bank[:, 0:4], pairs).then_inc(*sig.mark("gate2_product", t))

            def moe():
                pe.wait_ge(*sig.when("strength", 1))
                pe.wait_ge(*sig.when("pool_gate", "row0f"))
                bank = claim(("strength",), ("moe_shift", 0))
                even = ab[:].rearrange("p (b i) -> p i b", i=TPB)
                for i, (mask, src) in enumerate(((vis, even[:, 0]), (txt, even[:, 0]), (one, even[:, 1]))):
                    ins = mm(bank[:, i * B:(i + 1) * B], mask[:], src, start=True, stop=True)
                ins.then_inc(*sig.mark("strength_product", 0))
                choice_pending.append(1)

            choice_pending = []

            def choice():
                pe.wait_ge(*sig.when("choice2", 0))
                bank = claim(("choice",), ("out2_added", (0, 0)))
                mm(bank[:, 0:2 * MOE * TILES], row0[:], fl[:].rearrange("p c e t -> p (c e t)"), start=True, stop=True)\
                    .then_inc(*sig.mark("choice_product", 0))

            def hid2(e, c, hf):
                user = ("hid2_product", (e, c, hf))
                w = [need(("hid2", e, i), user) for i in range(2)]
                xt_ready(hf)
                bank = claim(("hid2", e, c, hf), ("hid2_value", (e, c, hf)))
                pairs = [([w[k // 2][q][:, k % 2, c * P:(c + 1) * P] for q in range(2)], xt(k, hf * HALF, (hf + 1) * HALF))
                         for k in range(KT)]
                product(bank[:], pairs).then_inc(*sig.mark(*user))

            def out2(e, t):
                user = ("out2_product", (e, t))
                w = [need(("out2", e, i), user) for i in range(2)]
                pe.wait_ge(*sig.when("h2_low", (e, KT - 1, t // TPH)))
                bank = claim(("out2", e, t), ("out2_added", (e, t)))
                pairs = [([h2[:, e % 2, q, k, t * P:(t + 1) * P] for q in range(2)], [w[k // 2][q][:, k % 2] for q in range(2)])
                         for k in range(KT)]
                product(bank[:], pairs).then_inc(*sig.mark(*user))

            def v3_(b):
                user = ("v3_product", b)
                w = need(("v3", 0), user)
                bank = claim(("v3", b), ("v3_low", b))
                pairs = []
                for k in range(KT):
                    pairs.append(([ctxT[:, q, k, b * CTX:(b + 1) * CTX] for q in range(2)], [w[q][:, k] for q in range(2)]))
                product(bank[0:CTX, 0:KV3 * HD3], pairs).then_inc(*sig.mark(*user))

            def q3_(c, hf):
                user = ("q3_product", (c, hf))
                w = [need(("q3", i), user) for i in range(2)]
                xt_ready(hf)
                bank = claim(("q3", c, hf), ("q3_low", (c, hf)))
                pairs = [([w[k // 2][q][:, k % 2, c * P:(c + 1) * P] for q in range(2)], xt(k, hf * HALF, (hf + 1) * HALF))
                         for k in range(KT)]
                product(bank[:], pairs).then_inc(*sig.mark(*user))

            def scores3(n, b, c):
                pe.wait_ge(*sig.when("q3_low", (c, b // BPH)))
                pe.wait_ge(*sig.when("keys3", n))
                for i in range(TPB):
                    t = TPB * b + i
                    bank = claim(("scores3", n, i), ("shift3", (n, i)))
                    product(bank[:], [([q3[:, q, c, t * P:(t + 1) * P] for q in range(2)],
                                       [kd3[:, n % 2, q].rearrange("p h k -> p (h k)") for q in range(2)])])\
                        .then_inc(*sig.mark("scores3_product", (n, i)))

            def turn3(n, b, c):
                for j in range(2):
                    bank = claim(("turn3", n, j), ("turn3_low", (n, j)))
                    for i in range(TPB):
                        pe.wait_ge(*sig.when("probs3", (n, i)))
                        for p in range(2):
                            ins = nc.tensor.transpose(bank[:, (2 * p + i) * P:(2 * p + i + 1) * P],
                                                      e3[:, n % 2, i, (2 * j + p) * P:(2 * j + p + 1) * P], ident[:])
                    ins.then_inc(*sig.mark("turn3_product", (n, j)))

            def pv3(n, b, c):
                pe.wait_ge(*sig.when("turn3_low", (n, 1)))
                pe.wait_ge(*sig.when("values3", n))
                bank = claim(("pv3", n), ("pv3_low", n))
                pairs = [([vd3[:, n % 2, q, p] for q in range(2)], [eT3[:, q, p] for q in range(2)]) for p in range(PAIRS)]
                product(bank[:, 0:S], pairs).then_inc(*sig.mark("pv3_product", n))

            def o3(t):
                user = ("o3_product", t)
                w = [need(("o3", i), user) for i in range(2)]
                pe.wait_ge(*sig.when("pv3_low", (t // TPB) * KT + KT - 1))
                bank = claim(("o3", t), ("o3_added", t))
                pairs = [([q3[:, q, k, t * P:(t + 1) * P] for q in range(2)], [w[k // 2][q][:, k % 2] for q in range(2)])
                         for k in range(KT)]
                product(bank[:], pairs).then_inc(*sig.mark(*user))

            def down3(part, t):
                user = ("down3_product", (part, t))
                lo, hi = (0, half_f) if part == 0 else (half_f, FT)
                pe.wait_ge(*sig.when("h3_low", 2 * hi - 1))
                bank = claim(("down3", part, t), ("down3_added", (part, t)))
                pairs = [([h3[0:fwidth(f), q, f % half_f, t * P:(t + 1) * P] for q in range(2)], down_chunk("down3", f, lo, user))
                         for f in range(lo, hi)]
                product(bank[:], pairs).then_inc(*sig.mark(*user))

            def nf_turn(m):
                pe.wait_ge(*sig.when("nf4_rcp", m))
                bank = claim(("nf_turn", m), ("nf4_turned", (m, 1)))
                for i in range(2):
                    ins = nc.tensor.transpose(bank[0:88, i * P:(i + 1) * P], nf_m[:, 1 + i], ident[:])
                ins.then_inc(*sig.mark("nf4_turn_product", m))

            handlers = {"turn": turn, "v0": v0_, "k0": k0_, "kc0": kc0_, "q0": q0_, "scores0": scores0, "turn0": turn0,
                        "pv0": pv0, "o0": o0, "down0": down0, "scores1": scores1, "pv1": pv1, "router1": router1,
                        "route1": route1, "z1": z1, "zt1": zt1, "b1": b1, "c2": c2_, "gate2": gate2, "moe": moe,
                        "hid2": hid2, "out2": out2, "v3": v3_, "q3": q3_, "scores3": scores3, "turn3": turn3,
                        "pv3": pv3, "o3": o3, "down3": down3, "nf_turn": nf_turn,
                        "up0": lambda f, hf: up("up0", f, hf, (("silu0", 2 * f + hf), ("inter0", 2 * f + hf))),
                        "up3": lambda f, hf: up("up3", f, hf, (("silu3", 2 * f + hf), ("h3_low", 2 * f + hf))),
                        "k2": lambda c: ctx_product("k2", c, ctxT, ("k2_low", c)),
                        "m2": lambda c: ctx_product("m2", c, k2, ("m2_low", c)),
                        "k3": lambda c: ctx_product("k3", c, ctxT, ("k3_low", c))}
            if known:
                pe.wait_ge(*sig.when("weight_low", chunk_no["ctxT"]))
            base_at = -1
            for s in steps:
                if s[0] == "split":
                    continue
                base_at += 1
                here[0] = base_at
                if choice_pending and s[0] in ("hid2", "out2"):
                    choice_pending.pop()
                    handlers[s[0]](*s[1:])
                    choice()
                elif s[0] in handlers:
                    handlers[s[0]](*s[1:])

        @block.sync
        def _(sp):
            layer = {None: 8}.get(only, only)
            for hf in range(2):
                if layer == 8:
                    sp.wait_ge(*sig.when("down3_added", (1, (hf + 1) * TPH - 1)))
                else:
                    sp.wait_ge(*sig.when("x_done", (layer, hf)))
                sp.dma_start(out[:, hf * TPH:(hf + 1) * TPH], x[:, hf * TPH:(hf + 1) * TPH]).then_inc(*sig.mark("stored", hf, 16))
            sp.wait_ge(sig.sem("stored"), 32)
        return sig


def lay_out(i):
    t = np.ascontiguousarray
    d = {k: np.asarray(v) for k, v in i.items()}
    wq, wk = d["L0_xattn_Wq"], d["L0_xattn_Wk"]
    rows = [((c * HPC + h) // REP3) * HD3 + j for c in range(KT) for h in range(HPC) for j in range(HD3)]
    return {
        "x": d["x"].reshape(TILES, P, D),
        "ctx": d["ctx_4096"],
        "ctxT": t(d["ctx_4096"].reshape(B * CTX, D).T),
        "L0_wqkT": t(np.stack([np.concatenate([wq[g * HPG * HD0:(g + 1) * HPG * HD0], wk[g * HD0:(g + 1) * HD0]]).T
                               for g in range(G0)])),
        "L0_wvT": t(d["L0_xattn_Wv"].T),
        "L0_woT": t(d["L0_xattn_Wo"].T),
        "L0_wgT": t(d["L0_ffn_w_gate"].T), "L0_wuT": t(d["L0_ffn_w_up"].T), "L0_wdT": t(d["L0_ffn_w_down"].T),
        "L1_aT": t(d["L1_ffn_A_w"].T), "L1_bT": t(d["L1_ffn_B_w"].T),
        "L1_wq": d["L1_ffn_Wq_w"], "L1_keysT": t(d["L1_ffn_keys"].T),
        "L2_wkT": t(d["L2_xattn_Wk"].T), "L2_wq": d["L2_xattn_Wq"],
        "L2_bq": t(d["L2_xattn_bq"].reshape(KT, P).T), "L2_bk": t(d["L2_xattn_bk"].reshape(KT, P).T),
        "L2_gw": d["L2_ffn_gate_w"], "L2_gb": d["L2_ffn_gate_b"],
        "L2_w1": d["L2_ffn_w1"], "L2_w2": d["L2_ffn_w2"],
        "L2_b1": t(d["L2_ffn_b1"].reshape(MOE, KT, P).transpose(2, 0, 1)), "L2_b2": d["L2_ffn_b2"],
        "L3_wqT": t(d["L3_xattn_wq"].T), "L3_wkT": t(d["L3_xattn_wk"][rows].T), "L3_wvT": t(d["L3_xattn_wv"].T),
        "L3_woT": t(d["L3_xattn_wo"].T), "L3_lnw": t(d["L3_xattn_ln_w"].reshape(KT, P).T),
        "L3_w1": d["L3_ffn_w1"], "L3_w2": d["L3_ffn_w2"], "L3_w3": d["L3_ffn_w3"].reshape(P, F * D // P),
        "L3_w1T": t(d["L3_ffn_w1"].T), "L3_w2T": t(d["L3_ffn_w2"].T),
        "L3_w3T": t(d["L3_ffn_w3"].reshape(P, 4, F).transpose(2, 1, 0).reshape(F, D)),
    }


def write_program(nc, shapes, known, only=None):
    aps = {n: nc.dram_tensor(f"in_{n}", shape, FP32, kind="ExternalInput").ap() for n, shape in shapes.items()}
    aps["x"] = aps["x"].rearrange("t p d -> p t d")
    out = nc.dram_tensor("out_x", (TILES, P, D), FP32, kind="ExternalOutput").ap()
    return build(nc, aps, out.rearrange("t p d -> p t d"), known, only)


def kernel(**inputs):
    import concourse.bacc as _bacc
    from concourse.bass_utils import run_bass_kernel_spmd as _run

    arrays = lay_out(inputs)
    shapes = {n: v.shape for n, v in arrays.items()}
    counts = None
    for _ in range(2):
        nc = _bacc.Bacc("TRN2", target_bir_lowering=False, num_devices=1)
        counts = write_program(nc, shapes, counts)
    r = _run(nc, [{f"in_{n}": v for n, v in arrays.items()}], core_ids=[0])
    return np.asarray(r.results[0]["out_x"]).reshape(B, S, D)
```

```python
import concourse.bass as bass
from concourse import mybir
from contextlib import ExitStack
import numpy as np

FP32 = mybir.dt.float32
F32R = mybir.dt.float32r
INT32 = mybir.dt.int32
ALU = mybir.AluOpType
ACT = mybir.ActivationFunctionType
AX = mybir.AxisListType

P = 128
B, S, D = 4, 256, 512
CTX = 64
TOK = B * S
TILES = TOK // P
KT = D // P
HALF = TOK // 2
TPH = TILES // 2
BPH = B // 2
TPB = S // P
H0, G0, HD0 = 16, 4, 96
HPG = H0 // G0
KEYS0 = S + CTX
F = 1376
FT = (F + P - 1) // P
NE, RANK, TOPK = 64, 8, 16
ROUT = 16
VISION = int(S * 0.3)
MOE = 3
H3, KV3, HD3 = 32, 8, 16
HPC = P // HD3
REP3 = H3 // KV3
PAIRS = HPC // 2
LN_EPS = 1e-5
BLOCK = 64
TURN_LAG, PV_LAG = 2, 3
E0_RING = 5
BACKGROUND_END = "q3"
MAX_PRICE = 0.4
L0_ROOM = 1.2
CODE = np.array([-1.0, -0.6961928009986877, -0.5250730514526367, -0.39491748809814453, -0.28444138169288635,
                 -0.18477343022823334, -0.09105003625154495, 0.0, 0.07958029955625534, 0.16093020141124725,
                 0.24611230194568634, 0.33791524171829224, 0.44070982933044434, 0.5626170039176941,
                 0.7229568362236023, 1.0], dtype=np.float32)
BOUNDS = (CODE[:-1] + CODE[1:]) * np.float32(0.5)
SLOT = 1024
NSLOT = 5
SPLIT_GAP, SPLIT_LEAD = 5.0, 12.0
TINY = 1.1754944e-38
ROUND = float(2 ** 23)


def neighbours(v, count):
    out = [np.float32(v)]
    up = down = out[0]
    for _ in range(count):
        up, down = np.nextafter(up, np.float32(9)), np.nextafter(down, np.float32(-9))
        out += [up, down]
    return out


def code_part(at, width):
    low = CODE[at]
    for step in neighbours(CODE[at + 1] - low, 8):
        if low + step == CODE[at + 1]:
            if width == 1:
                return (float(step),)
            for ratio in neighbours((CODE[at + 2] - low) / step - np.float32(1), 40):
                if low + (np.float32(1) + ratio) * step == CODE[at + 2]:
                    return float(step), float(ratio)


PAIRED = (1, 3, 9, 11)
PARTS = [(at, code_part(at, 2 if at in PAIRED else 1)) for at in range(len(BOUNDS)) if at - 1 not in PAIRED]
assert all(numbers is not None for _, numbers in PARTS)
NPART = len(PARTS)


def fwidth(f):
    return min(P, F - f * P)



def schedule(only=None):
    steps = []

    steps += [("stats", 0, 0), ("turn", 0, 0)]
    steps += [("v0", 0, i) for i in range(TPH + BPH)]
    steps += [("k0", 0), ("kc0", 0)] + [("q0", 0, h) for h in range(HPG)]
    units = [(s, bl, h) for s in range(2 * G0) for h in range(HPG) for bl in range(BPH)]
    per, last_stage = HPG * BPH, 2 * G0 - 1
    for n in range(len(units) + PV_LAG):
        if n < len(units):
            steps.append(("scores0", n, *units[n]))
        if 1 <= n <= len(units):
            steps.append(("scale0", n - 1))
        if TURN_LAG <= n < len(units) + TURN_LAG:
            steps.append(("turn0", n - TURN_LAG, *units[n - TURN_LAG]))
        if n >= PV_LAG:
            steps.append(("pv0", n - PV_LAG, *units[n - PV_LAG]))
            if n - PV_LAG == G0 * per - 1:
                steps += [("v0", 1, i) for i in range(TPH + BPH)]
        if n < len(units):
            s, j = n // per, n % per
            if s < last_stage:
                late = 4 if s == G0 else 2
                if j == late:
                    steps.append(("k0", s + 1))
                if j == late + 1:
                    steps.append(("kc0", s + 1))
            if s >= 1 and j in (3, 4):
                steps += [("o0", s - 1, i) for i in (2 * j - 6, 2 * j - 5)]
            if s < last_stage and j >= 5:
                steps += [("q0", s + 1, h) for h in ((0, 1), (2,), (3,))[j - 5]]
            if (s, j) == (0, 3):
                steps.append(("stats", 0, 1))
            if (s, j) == (1, 2):
                steps.append(("turn", 0, 1))
            if (s, j) == (G0, 6):
                steps.append(("stats", 1, 0))
            if (s, j) == (G0 + 1, 6):
                steps.append(("turn", 1, 0))
    steps += [("o0", last_stage, i) for i in range(TPH)] + [("stats", 1, 1)]
    if only == 1:
        return steps
    half_f = (FT + 1) // 2
    steps += [("up0", 0, 0), ("turn", 1, 1), ("up0", 0, 1)]
    steps += [("up0", f, hf) for f in range(1, half_f) for hf in range(2)]
    steps += [("down0", 0, t) for t in range(TILES)]
    steps += [("up0", f, hf) for f in range(half_f, FT) for hf in range(2)]
    steps += [("down0", 1, t) for t in range(TPH)] + [("stats", 2, 0)]
    steps += [("down0", 1, t) for t in range(TPH, TILES)] + [("turn", 2, 0), ("stats", 2, 1)]
    if only == 2:
        return steps
    steps += [("scores1", 1, 0), ("scores1", 1, 1), ("turn", 2, 1), ("pv1", 1, 0), ("scores1", 1, 2),
              ("pv1", 1, 1), ("stats", 3, 0), ("scores1", 1, 3), ("pv1", 1, 2), ("turn", 3, 0), ("pv1", 1, 3),
              ("stats", 3, 1)]
    if only == 3:
        return steps
    steps += [("router1",)] + [("route1", t) for t in range(TPH)] + [("turn", 3, 1)]
    steps += [("z1", 0), ("bias2",)] + [("route1", t) for t in range(TPH, TILES)]
    for t in range(TILES):
        if t + 1 < TILES:
            steps.append(("z1", t + 1))
        steps.append(("zt1", t))
        if t >= 1:
            steps.append(("b1", t - 1))
        if t - 1 == TPH - 1:
            steps.append(("stats", 4, 0))
    steps += [("b1", TILES - 1)] + [("k2", c) for c in range(KT)] + [("turn", 4, 0), ("stats", 4, 1)]
    if only == 4:
        return steps
    steps += [("m2", c) for c in range(KT)] + [("c2",)]
    steps += [("scores1", 2, 0), ("scores1", 2, 1), ("turn", 4, 1), ("pv1", 2, 0), ("scores1", 2, 2),
              ("pv1", 2, 1), ("stats", 5, 0), ("scores1", 2, 3), ("pv1", 2, 2), ("turn", 5, 0), ("pv1", 2, 3),
              ("stats", 5, 1)]
    if only == 5:
        return steps
    steps += [("gate2", t) for t in range(TPH)]
    steps += [("hid2", 0, 0, 0), ("turn", 5, 1), ("hid2", 0, 0, 1)]
    steps += [("gate2", t) for t in range(TPH, TILES)]
    for i in range(2 * (KT - 1)):
        steps += [("moe", i)] * (i < 4) + [("hid2", 0, 1 + i // 2, i % 2)]
    steps += [("hid2", 1, c, hf) for c in range(KT) for hf in range(2)]
    for e in range(MOE):
        steps += [("out2", e, t) for t in range(TPH)]
        if e == MOE - 1:
            steps.append(("stats", 6, 0))
        steps += [("out2", e, t) for t in range(TPH, TILES)]
        if e + 2 < MOE:
            steps += [("hid2", e + 2, c, hf) for c in range(KT) for hf in range(2)]
    if only != 6:
        steps += [("k3", c) for c in range(KT)] + [("v3", b) for b in range(B)]
    steps += [("turn", 6, 0), ("stats", 6, 1)]
    if only == 6:
        return steps
    steps += [("q3", 0, 0), ("turn", 6, 1)] + [("q3", c, 0) for c in range(1, KT)] + [("q3", c, 1) for c in range(KT)]
    units = [(b, c) for b in range(B) for c in range(KT)]
    steps.append(("keys3", 0, *units[0]))
    for n in range(len(units) + 2):
        if n < len(units):
            steps.append(("scores3", n, *units[n]))
        if 1 <= n <= len(units):
            steps.append(("scale3", n - 1))
        if n >= 2:
            steps.append(("pv3", n - 2, *units[n - 2]))
        if n < len(units):
            steps.append(("values3", n, *units[n]))
        if 1 <= n <= len(units):
            steps.append(("turn3", n - 1, *units[n - 1]))
        if n >= 2:
            if units[n - 2][1] == 0 and units[n - 2][0] >= 1:
                steps += [("o3", TPB * (units[n - 2][0] - 1) + i) for i in range(TPB)]
            if n - 2 == 3 * KT - 1:
                steps.append(("stats", 7, 0))
        if n + 1 < len(units):
            steps.append(("keys3", n + 1, *units[n + 1]))
    steps += [("turn", 7, 0)] + [("o3", TILES - 2), ("o3", TILES - 1), ("stats", 7, 1)]
    if only == 7:
        return steps
    steps += [("up3", 0, 0), ("turn", 7, 1), ("up3", 0, 1)]
    steps += [("up3", f, hf) for f in range(1, half_f) for hf in range(2)]
    steps += [("down3", 0, t) for t in range(TILES)]
    steps += [("up3", f, hf) for f in range(half_f, FT) for hf in range(2)]
    steps += [("down3", 1, t) for t in range(TILES)]
    return steps


WEIGHT = {"v0": 1.9, "k0": 2.6, "kc0": .7, "q0": 2.6, "scores0": .9, "turn0": .4, "pv0": 1, "o0": 2.6, "up0": 2.6,
          "down0": 4.8, "scores1": 2, "pv1": 1.6, "route1": 1, "z1": 2.6, "zt1": .5, "b1": 2.6, "k2": 1.3, "m2": 1.3,
          "gate2": 1.2, "hid2": 2.6, "out2": 2.6, "k3": 1.3, "v3": 1, "q3": 2.6, "scores3": 1.3, "turn3": .5,
          "pv3": 1.3, "o3": 2.6, "up3": 2.6, "down3": 4}


def room(step):
    if step[0] in ("scores0", "turn0", "pv0", "q0", "k0", "kc0", "o0"):
        return WEIGHT[step[0]] * L0_ROOM
    return {("up0",): 1.5, ("down0", 0): 6, ("down0", 1): 1}.get(step[:2] if step[0] == "down0" else step[:1],
                                                                WEIGHT.get(step[0], 0))


def with_background(steps, first, last, jobs):
    a = next(i for i, s in enumerate(steps) if s[0] == first)
    z = max(i for i, s in enumerate(steps) if s[0] == last)
    total = sum(room(s) for s in steps[a:z])
    price = [{"nf_max": MAX_PRICE, "nf": 1}.get(job[0], 0) for job in jobs]
    out, at, spent, paid, bill = list(steps[:a]), 0, 0.0, 0.0, sum(price)
    for s in steps[a:z]:
        spent += room(s)
        out.append(s)
        while at < len(jobs) and paid < bill * spent / total:
            out.append(jobs[at])
            paid += price[at]
            at += 1
    return out + jobs[at:] + list(steps[z:])


def spread_splits(base, earliest, first_use):
    times, t = [], 0.0
    for s in base:
        t += WEIGHT.get(s[0], 0.5 if s[0] != "nf" else 0)
        times.append(t)
    count = len(earliest)
    latest, bound = [0] * count, len(base) - 1
    for i in reversed(range(count)):
        at = min(bound, first_use[i] - 1)
        while at > -1 and times[at] > times[max(first_use[i] - 1, 0)] - SPLIT_LEAD:
            at -= 1
        latest[i] = bound = at
    placed, at = {}, -1
    for i in range(count):
        after = times[at] + SPLIT_GAP if at >= 0 and i > NSLOT else 0
        want = max(earliest[i], at)
        while want < latest[i] and (times[want] if want >= 0 else 0) < after:
            want += 1
        at = want
        placed.setdefault(at, []).append(i)
    return placed


LAYER_STAGES = {"layer0": ("v0", "k0", "kc0", "q0", "scores0", "turn0", "pv0", "o0", "up0", "down0"),
                "layer1": ("scores1", "turn1", "pv1", "router1", "route1", "z1", "zt1", "b1"),
                "layer2": ("k2", "m2", "c2", "gate2", "strength", "choice", "hid2", "out2", "bq"),
                "layer3": ("k3", "v3", "q3", "scores3", "turn3", "pv3", "o3", "up3", "down3")}
SHARED = {f"{stage}_{kind}": f"{layer}_{kind}" for layer, stages in LAYER_STAGES.items() for stage in stages
          for kind in ("product", "high", "low", "added")}
SHARED["h3_low"] = "layer3_low"


class Signals:

    def __init__(self, nc, ctx, known):
        self.nc, self.ctx, self.known = nc, ctx, known
        self.sems, self.count, self.at = {}, {}, {}
        self.bank, self.bank_of, self.user = 0, {}, {}
        self.first_step, self.last_step = {}, {}

    def sem(self, name):
        name = SHARED.get(name, name)
        if name not in self.sems:
            self.sems[name] = self.ctx.enter_context(self.nc.semaphore(name))
        return self.sems[name]

    def mark(self, name, key, by=1):
        shared = SHARED.get(name, name)
        self.count[shared] = self.count.get(shared, 0) + by
        self.at[name, key] = self.count[shared]
        return self.sem(name), by

    def when(self, name, key):
        return self.sem(name), self.known.at[name, key] if self.known else 1

    def next_bank(self, key, *freed_by):
        n = self.bank % 8
        self.bank += 1
        ended = self.user.get(n, ())
        self.user[n] = freed_by
        self.bank_of[key] = n
        return n, ended

    def bank_for(self, key):
        return self.known.bank_of[key] if self.known else 0


def build(nc, a, out, known, only=None):
    ctx = ExitStack()
    with ctx:
        sig = Signals(nc, ctx, known)

        def sb(name, shape, dt, scope=ctx):
            return scope.enter_context(nc.sbuf_tensor(name, shape, dt))

        x = sb("x", [P, TILES, D], FP32)
        xn = sb("xn", [P, TPH, D], FP32)
        xT = sb("xT", [P, 2, KT, TOK], F32R)
        ctxT = sb("ctxT", [P, 2, KT, B * CTX], F32R)
        slots = sb("slots", [P, NSLOT, 2, SLOT], F32R)
        staging = sb("staging", [P, 2, SLOT], FP32)
        ident = sb("ident", [P, P], FP32)
        st = sb("st", [P, TILES, 6], FP32)
        mv = sb("mv", [P, TILES, 2], FP32)
        rs = sb("rs", [P, TILES], FP32)
        rt = sb("rt", [P, 4, TILES], FP32)
        mx = sb("mx", [P, 4, 2 * HPC], FP32)
        sm = sb("sm", [P, 4, 2 * HPC], FP32)
        nfs = ExitStack()
        nf_w = sb("nf_w", [P, 2, D], FP32, nfs)
        nf_a = sb("nf_a", [P, 2, D], FP32, nfs)
        nf_r = sb("nf_r", [P, D], FP32, nfs)
        l = ExitStack()
        nf_m = sb("nf_m", [P, 3, 88], FP32, l)
        nf_t = sb("nf_t", [P, 2, P], FP32, l)
        l.close()
        nf_y = sb("nf_y", [P, 3, D], FP32, nfs)
        s0 = ExitStack()
        q0 = sb("q0", [HD0, 2, 2, HPG, HALF], F32R, s0)
        k0 = sb("k0", [HD0, 2, 2, BPH, KEYS0], F32R, s0)
        v0 = sb("v0", [P, 2, TPH + BPH, G0 * HD0], F32R, s0)
        eT0 = sb("eT0", [P, 2, 2, 3, S], F32R, s0)
        e0 = sb("e0", [P, E0_RING, KEYS0], FP32, s0)
        s0.close()
        l = ExitStack()
        h0 = sb("h0", [P, (FT + 1) // 2, TOK], F32R, l)
        acc0 = sb("acc0", [P, TILES, D], FP32, l)
        g0 = sb("g0", [P, 2, HALF], FP32, l)
        f0 = sb("f0", [P, 2, 5, HALF], FP32, l)
        l.close()
        l = ExitStack()
        ctxN = sb("ctxN", [CTX, 2, B, D], F32R, l)
        e1 = sb("e1", [P, 2, TPB, CTX], FP32, l)
        s1 = sb("s1", [P, 2, TPB, CTX], FP32, l)
        eT1 = sb("eT1", [CTX, 2, 2, S], F32R, l)
        k2 = sb("k2", [P, 2, KT, B * CTX], F32R, l)
        m2 = sb("m2", [P, 2, KT, B * CTX], F32R, l)
        c2 = sb("c2", [P, B * CTX], FP32, l)
        bq = sb("bq", [P, KT], FP32, l)
        bk = sb("bk", [P, KT], FP32, l)
        bqw = sb("bqw", [P, 2, KT, P], F32R, l)
        bqf = sb("bqf", [P, KT, P], FP32, l)
        wq1 = sb("wq1", [ROUT, D], FP32, l)
        keyT = sb("keyT", [ROUT, NE], FP32, l)
        rw = sb("rw", [P, 2, KT, NE], F32R, l)
        r1 = sb("r1", [P, 4, TILES, NE], FP32, l)
        top8 = sb("top8", [P, 2, TILES, 8], FP32, l)
        zg = sb("zg", [P, 2, D], FP32, l)
        zT = sb("zT", [P, 2, 2, KT, P], F32R, l)
        l.close()
        l = ExitStack()
        h2 = sb("h2", [P, 2, 2, KT, TOK], F32R, l)
        hf2 = sb("hf2", [P, 2, HALF], FP32, l)
        y2 = sb("y2", [P, D], FP32, l)
        b1c = sb("b1c", [P, MOE, KT], FP32, l)
        b2b = sb("b2b", [P, 2, D], FP32, l)
        gwf = sb("gwf", [P, KT, 4], FP32, l)
        gw = sb("gw", [P, 2, KT, 4], F32R, l)
        gwr = sb("gwr", [P, 4], FP32, l)
        gbr = sb("gbr", [P, 4], FP32, l)
        vis = sb("vis", [P, P], FP32, l)
        txt = sb("txt", [P, P], FP32, l)
        one = sb("one", [P, P], FP32, l)
        row0 = sb("row0", [P, P], FP32, l)
        ab = sb("ab", [P, TILES], FP32, l)
        lg = sb("lg", [P, TILES, 4], FP32, l)
        p8 = sb("p8", [P, TILES, 8], FP32, l)
        t8 = sb("t8", [P, TILES, 8], FP32, l)
        gt = sb("gt", [P, 12, TILES], FP32, l)
        fl = sb("fl", [P, 2, MOE, TILES], FP32, l)
        fb = sb("fb", [P, 2, MOE, TILES], FP32, l)
        cf = sb("cf", [P, MOE, TILES], FP32, l)
        ra = sb("ra", [P, 4, TILES], FP32, l)
        l.close()
        l = ExitStack()
        q3 = sb("q3", [P, 2, KT, TOK], F32R, l)
        kd3 = sb("kd3", [P, 2, 2, HPC, CTX], F32R, l)
        vd3 = sb("vd3", [P, 2, 2, PAIRS, P], F32R, l)
        kr3 = sb("kr3", [P, 2, KT, B * CTX], F32R, l)
        v3 = sb("v3", [CTX, 2, B, KV3 * HD3], F32R, l)
        e3 = sb("e3", [P, 2, TPB, HPC * CTX], FP32, l)
        eT3 = sb("eT3", [P, 2, PAIRS, S], F32R, l)
        hm3 = sb("hm3", [P, HPC], FP32, l)
        lnw = sb("lnw", [P, KT], FP32, l)
        l.close()
        nfs.close()
        l = ExitStack()
        h3 = sb("h3", [P, 2, (FT + 1) // 2, TOK], F32R, l)
        g3 = sb("g3", [P, 3, HALF], FP32, l)
        l.close()
        banks = [ctx.enter_context(nc.psum_tensor(f"bank{i}", [P, 512], FP32)) for i in range(8)]

        def psum(key):
            return banks[sig.bank_for(key)]

        def dram(name, shape):
            return nc.dram_tensor(name, shape, FP32, kind="Internal").ap()

        nf_max = [dram(f"nf_max{m}", (88, P)) for m in range(3)]
        nf_rcp = [dram(f"nf_rcp{m}", (88, P)) for m in range(3)]
        nf_out = [dram(f"nf_out{m}", (FT, P, D)) for m in range(3)]

        chunks, chunk_no = [], {}

        def chunk(name, p, dims, loads, dest=None, after=None):
            chunk_no[name] = len(chunks)
            chunks.append((name, p, dims, loads, dest, after))

        def by_k(ap, k0_, k1_):
            return ap.rearrange("(k p) n -> p k n", p=P)[:, k0_:k1_]


        def v0_chunks(hf):
            for i in range(2):
                chunk(("v0", hf, i), P, (2, G0 * HD0), [((slice(None),), by_k(a["L0_wvT"], 2 * i, 2 * i + 2))])

        def qk0_chunks(s):
            for i in range(2):
                chunk(("qk0", s, i), P, (2, (HPG + 1) * HD0),
                      [((slice(None),), by_k(a["L0_wqkT"][s % G0], 2 * i, 2 * i + 2))])

        def o0_chunks(s):
            for i in range(2):
                rows = a["L0_woT"][(s % G0 * HPG + 2 * i) * HD0:(s % G0 * HPG + 2 * i + 2) * HD0]
                chunk(("o0", s, i), HD0, (2, D), [((slice(None),), rows.rearrange("(h p) n -> p h n", p=HD0))])

        v0_chunks(0)
        chunk("ctxT", P, (KT, B * CTX), [((slice(None),), by_k(a["ctxT"], 0, KT))], dest=(ctxT[:, 0], ctxT[:, 1]))
        qk0_chunks(0)
        for s in range(2 * G0):
            if s + 1 < 2 * G0:
                qk0_chunks(s + 1)
            if s == G0 - 1:
                v0_chunks(1)
            o0_chunks(s)

        def ffn_up(name, gate, up, lo, hi):
            for f in range(lo, hi):
                w = fwidth(f)
                chunk((name, f), P, (2, KT, w), [((0,), gate(f)), ((1,), up(f))], after=after_nf(name, 3 * f + 1))

        def ffn_down(name, down, lo, hi):
            for f in range(lo, hi, 2):
                n = min(2, hi - f)
                w = fwidth(f + n - 1)
                if w == P or n == 1:
                    chunk((name, f), w, (n, D), [((i,), down(f + i, w)) for i in range(n)],
                          after=after_nf(name, 3 * (f + n - 1) + 2))
                else:
                    chunk((name, f), P, (1, D), [((0,), down(f, P))], after=after_nf(name, 3 * f + 2))
                    chunk((name, f + 1), w, (1, D), [((0,), down(f + 1, w))], after=after_nf(name, 3 * f + 5))

        def after_nf(name, item):
            return ("nf4_stored", item) if name in ("up3", "down3") else None

        def cols(ap):
            return lambda f: ap.rearrange("(k p) n -> p k n", p=P)[:, :, f * P:f * P + fwidth(f)]

        half_f = (FT + 1) // 2
        for lo, hi in ((0, half_f), (half_f, FT)):
            ffn_up("up0", cols(a["L0_wgT"]), cols(a["L0_wuT"]), lo, hi)
            ffn_down("down0", lambda f, w: a["L0_wdT"][f * P:f * P + w], lo, hi)
        for i in range(2):
            chunk(("ctxN", i), CTX, (2, D),
                  [((slice(None),), a["ctx"][2 * i:2 * i + 2].rearrange("b s d -> s b d"))],
                  dest=(ctxN[:, 0, 2 * i:2 * i + 2], ctxN[:, 1, 2 * i:2 * i + 2]), after=("down0_product", (1, TILES - 1)))
        for name, ap in (("z1", a["L1_aT"]), ("b1", a["L1_bT"]), ("k2", a["L2_wkT"]), ("m2", a["L2_wq"])):
            for i in range(2):
                chunk((name, i), P, (2, D), [((slice(None),), by_k(ap, 2 * i, 2 * i + 2))])
        for e in range(MOE):
            for name, ap in (("hid2", a["L2_w1"]), ("out2", a["L2_w2"])):
                for i in range(2):
                    chunk((name, e, i), P, (2, D), [((slice(None),), by_k(ap[e], 2 * i, 2 * i + 2))])
        tail = chunks[-4 * MOE:]
        del chunks[-4 * MOE:]
        names = {c[0]: c for c in tail}
        order = []
        for stage in [("hid2", 0)] + [st_ for e in range(MOE) for st_ in (("hid2", e + 1), ("out2", e)) if st_ != ("hid2", MOE)]:
            order += [(*stage, i) for i in range(2)]
        for n in order:
            chunk(*names[n])
        for i in range(2):
            chunk(("k3", i), P, (2, D), [((slice(None),), by_k(a["L3_wkT"], 2 * i, 2 * i + 2))])
        chunk(("v3", 0), P, (KT, KV3 * HD3), [((slice(None),), by_k(a["L3_wvT"], 0, KT))])
        for i in range(2):
            chunk(("q3", i), P, (2, D), [((slice(None),), by_k(a["L3_wqT"], 2 * i, 2 * i + 2))])
        for i in range(2):
            chunk(("o3", i), P, (2, D), [((slice(None),), by_k(a["L3_woT"], 2 * i, 2 * i + 2))])

        def nf_cols(m):
            return lambda f: nf_out[m][f][:, 0:KT * fwidth(f)].rearrange("p (k n) -> p k n", k=KT)

        for lo, hi in ((0, half_f), (half_f, FT)):
            ffn_up("up3", nf_cols(0), nf_cols(1), lo, hi)
            ffn_down("down3", lambda f, w: nf_out[2][f][0:w], lo, hi)

        base = schedule(only)
        if only is None or only == 7:
            jobs = []
            for m in range(3):
                for f in range(FT):
                    jobs += [("nf_max", m, f)] + [("nf_turn", m - 1)] * (m > 0 and f == 4)
            jobs.append(("nf_turn", 2))
            items = [(3 * f + m, m, f) for f in range(FT) for m in range(3)]
            jobs.append(("nf_load", *items[0]))
            for n, m, f in items:
                for j in range(1, NPART + 1):
                    jobs.append(("nf", n, m, f, j))
                    if j == 2 and n:
                        jobs.append(("nf_store", *items[n - 1]))
                    if j == NPART // 2 + 1 and n + 1 < len(items):
                        jobs.append(("nf_load", *items[n + 1]))
            jobs.append(("nf_store", *items[-1]))
            base = with_background(base, "scores0", BACKGROUND_END, jobs)
        steps = []
        if known:
            last = known.last_step
            free_after = {}
            slot_of, n = {}, 0
            for c_ in chunks:
                if c_[4] is None:
                    slot_of[c_[0]] = n
                    n += 1
            ring = sorted(slot_of, key=slot_of.get)
            context_at = next((at for at, s in enumerate(base) if s[0] == "pv1"), len(base))
            for i, c_ in enumerate(chunks):
                at = -1
                if c_[4] is None and slot_of[c_[0]] >= NSLOT:
                    prev = ring[slot_of[c_[0]] - NSLOT]
                    if prev not in last:
                        break
                    at = last[prev]
                if c_[5] is not None and c_[5][0] == "down0_product":
                    at = max(i2 for i2, s in enumerate(base) if s[0] == "down0") if "down0" in {s[0] for s in base} else None
                    if at is None:
                        break
                if c_[5] is not None and c_[5][0] == "nf4_stored":
                    at = max([at] + [i2 for i2, s in enumerate(base) if s[:2] == ("nf_store", c_[5][1])])
                at = max(at, max(free_after, default=-1))
                free_after.setdefault(at, []).append(i)
            free_after = spread_splits(base, [at for at, v in free_after.items() for i in v],
                                       [known.first_step.get(c_[0], 0 if c_[0] == "ctxT" else context_at) for c_ in chunks])
            n_chunks = sum(len(v) for v in free_after.values())
            load_after, split_at = {}, {i: at for at, v in free_after.items() for i in v}
            stored_at = {s[1]: at for at, s in enumerate(base) if s[0] == "nf_store"}
            for i in range(n_chunks):
                after = chunks[i][5]
                at = max(split_at[i - 2] if i >= 2 else -1, max(load_after, default=-1),
                         stored_at[after[1]] if after is not None and after[0] == "nf4_stored" else -1)
                load_after.setdefault(at, []).append(i)
            for at in range(-1, len(base)):
                steps += [base[at]] if at >= 0 else []
                loads_here, splits_here = list(load_after.get(at, [])), free_after.get(at, [])
                for j in splits_here:
                    while loads_here and loads_here[0] < j + 2:
                        steps.append(("load", loads_here.pop(0)))
                    steps.append(("split", j))
                steps += [("load", j) for j in loads_here]
        else:
            n_chunks = len(chunks)
            steps = [(kind, i) for i in range(n_chunks) for kind in ("load", "split")] + base

        slot_no, n = {}, 0
        for c_ in chunks:
            if c_[4] is None:
                slot_no[c_[0]] = n
                n += 1
        ring_names = sorted(slot_no, key=slot_no.get)

        def flat(ap, dims):
            if len(dims) == 1:
                return ap
            if len(dims) == 2:
                return ap.rearrange("p (a b) -> p a b", a=dims[0])
            return ap.rearrange("p (a b c) -> p a b c", a=dims[0], b=dims[1])

        def weight(name, part):
            _, p, dims, _, dest, _ = chunks[chunk_no[name]]
            if dest is not None:
                return dest[part]
            size = int(np.prod(dims))
            return flat(slots[0:p, slot_no[name] % NSLOT, part, 0:size], dims)

        chunk_no.clear()
        chunk_no.update({c_[0]: i for i, c_ in enumerate(chunks)})
        block = ctx.enter_context(nc.Block())

        def rows_buffer(i):
            return (nf_w, nf_a)[i // 2 % 2][:, i % 2]

        def part_no(n, j):
            return n % 3 if j == 1 else (n + 1 + j % 2) % 3

        @block.sync
        def _(sp):
            sp.dma_start(x[:, 0:TPH], a["x"][:, 0:TPH]).then_inc(*sig.mark("x_loaded0", 0, 16))
            sp.dma_start(x[:, TPH:], a["x"][:, TPH:]).then_inc(*sig.mark("x_loaded1", 0, 16))

            def load_chunk(i):
                name, p, dims, loads, dest, after = chunks[i]
                if i >= 2:
                    sp.wait_ge(*sig.when("weight_low", i - 2))
                if after is not None and after[0] == "nf4_stored":
                    for q in range(2):
                        sp.wait_ge(*sig.when(f"nf4_stored{q}", after[1] - (after[1] - q) % 2))
                size = int(np.prod(dims))
                view = flat(staging[0:p, i % 2, 0:size], dims)
                for n, (ix, src) in enumerate(loads):
                    dst = view if ix == (slice(None),) else view[:, ix[0]]
                    sp.dma_start(dst, src).then_inc(*sig.mark(f"weight_staged{i % 2}", i, 16))

            nf_src = (a["L3_w1"], a["L3_w2"])

            def nf_rows(m, f):
                w = fwidth(f) if m < 2 else P
                n = D if m < 2 or f < 10 else 6 * BLOCK
                i = m * FT + f
                if i >= 4:
                    sp.wait_ge(*sig.when("nf4_max", divmod(i - 4, FT)))
                src = nf_src[m][f * P:f * P + w] if m < 2 else a["L3_w3"][:, f * D:f * D + n]
                sp.dma_start(rows_buffer(i)[0:w, 0:n], src).then_inc(*sig.mark(f"nf4_rows{i % 4}", (m, f), 16))

            def nf_turned(m):
                for i, dst in enumerate((nf_max[m], nf_rcp[m])):
                    sp.wait_ge(*sig.when("nf4_turned", (m, i)))
                    sp.dma_start(dst, nf_t[0:88, i]).then_inc(*sig.mark(f"nf4_maxima_stored{i}", m, 16))

            def broadcast_rows(dst_tile, src, m, f):
                w = fwidth(f)
                pairs = []
                if m < 2:
                    for ph in range(2):
                        rows = src[f * 8:f * 8 + 8, 0:w].rearrange("(k two) n -> two k n", two=2)[ph]
                        dst = dst_tile[64 * ph:64 * ph + 64, 0:KT * w].rearrange("p (k n) -> p k n", k=KT)
                        pairs.append((dst, rows.partition_broadcast(64)))
                else:
                    for dr in range(4):
                        p = 0
                        while p < w:
                            c = (dr * (F // 32) + (f * P + p) // 32) // 2
                            q = p
                            while q < w and (dr * (F // 32) + (f * P + q) // 32) // 2 == c:
                                q += 32
                            pairs.append((dst_tile[p:q, dr * P:(dr + 1) * P], src[c].partition_broadcast(q - p)))
                            p = q
                return pairs

            turned_src = (a["L3_w1T"], a["L3_w2T"])

            def nf_load(n, m, f):
                w = fwidth(f)
                rows, size = (P, KT * w) if m < 2 else (w, D)
                if n == 0:
                    for i in range(2):
                        sp.wait_ge(*sig.when(f"nf4_maxima_stored{i}", 2))
                else:
                    sp.wait_ge(*sig.when("nf4_scaled", n - 1))
                if n >= 2:
                    sp.wait_ge(*sig.when(f"nf4_stored{n % 2}", n - 2))
                src = turned_src[m].rearrange("(k p) n -> p k n", p=P)[:, :, f * P:f * P + w] if m < 2 \
                    else a["L3_w3T"][f * P:f * P + w]
                dst = nf_w[0:rows, n % 2, 0:size]
                dst = dst.rearrange("p (k n) -> p k n", k=KT) if m < 2 else dst
                sp.dma_start(dst, src).then_inc(*sig.mark(f"nf4_weights{n % 2}", n, 16))
                for dst, src in broadcast_rows(nf_a[:, n % 2], nf_max[m], m, f) + broadcast_rows(nf_r[:], nf_rcp[m], m, f):
                    sp.dma_start(dst, src).then_inc(*sig.mark(f"nf4_weights{n % 2}", n, 16))

            def nf_store(n, m, f):
                w = fwidth(f)
                rows, size = (P, KT * w) if m < 2 else (w, D)
                sp.wait_ge(*sig.when("nf4_dequantised", n))
                sp.dma_start(nf_out[m][f][0:rows, 0:size], nf_w[0:rows, n % 2, 0:size])\
                    .then_inc(*sig.mark(f"nf4_stored{n % 2}", n, 16))

            for s in steps:
                if s[0] == "load":
                    load_chunk(*s[1:])
                elif s[0] == "nf_max":
                    nf_rows(*s[1:])
                elif s[0] == "nf_turn":
                    nf_turned(*s[1:])
                elif s[0] == "nf_load":
                    nf_load(*s[1:])
                elif s[0] == "nf_store":
                    nf_store(*s[1:])

        def split_source(i):
            _, p, dims, *_ = chunks[i]
            return flat(staging[0:p, i % 2, 0:int(np.prod(dims))], dims)

        @block.gpsimd
        def _(pool):
            g = nc.gpsimd
            g.memset(ident[:], 0.0).then_inc(*sig.mark("pool_const", "a"))
            pool.wait_ge(*sig.when("pool_const", "a"))
            g.affine_select(out=ident[:], in_=ident[:], compare_op=ALU.not_equal, fill=1.0, base=0,
                            pattern=[[-1, P]], channel_multiplier=1).then_inc(*sig.mark("ident_ready", 0))

            def small_loads(when, pairs):
                for w in when:
                    pool.wait_ge(*sig.when(*w))
                for name, dst, src in pairs:
                    pool.dma_start(dst, src).then_inc(*sig.mark(f"loaded_{name}", 0, 16))

            def split(i):
                pool.wait_ge(*sig.when("weight_high", i))
                _, p, dims, *_ = chunks[i]
                hi, lo = weight(chunks[i][0], 0), weight(chunks[i][0], 1)
                g.tensor_tensor(lo, split_source(i), hi.bitcast(FP32), ALU.subtract).then_inc(*sig.mark("weight_low", i))

            def nf(n, m, f, j):
                w = fwidth(f)
                rows, size = (P, KT * w) if m < 2 else (w, D)
                if j == 1:
                    return
                acc = nf_y[0:rows, part_no(n, 1), 0:size]
                pool.wait_ge(*sig.when("nf4_step", (n, j)))
                if j > 2:
                    pool.wait_ge(*sig.when("nf4_added", (n, j - 1)))
                g.tensor_tensor(acc, acc, nf_y[0:rows, part_no(n, j), 0:size], ALU.add).then_inc(*sig.mark("nf4_added", (n, j)))
                if j == NPART:
                    pool.wait_ge(*sig.when("nf4_added", (n, j)))
                    o, i1 = nf_w[0:rows, n % 2, 0:size], nf_a[0:rows, n % 2, 0:size]
                    if m == 2:
                        o, acc, i1 = o.rearrange("p (q r) -> p r q", r=4), acc.rearrange("p (r q) -> p r q", r=4), \
                            i1.rearrange("p (r q) -> p r q", r=4)
                    g.tensor_tensor(o, acc, i1, ALU.mult).then_inc(*sig.mark("nf4_dequantised", n))

            def hid2(e, c, hf):
                pool.wait_ge(*sig.when("h2_high", (e, c, hf)))
                i = (e * KT + c) * 2 + hf
                cs = slice(hf * HALF, (hf + 1) * HALF)
                g.tensor_tensor(h2[:, e % 2, 1, c, cs], hf2[:, i % 2], h2[:, e % 2, 0, c, cs].bitcast(FP32),
                                ALU.subtract).then_inc(*sig.mark("h2_low", (e, c, hf)))

            def keys3(n, b, c):
                if n == 0:
                    pool.wait_ge(*sig.when("head_mask", 0))
                pool.wait_ge(*sig.when("k3_low", c))
                if n >= 2:
                    pool.wait_ge(*sig.when("scores3_product", (n - 2, TPB - 1)))
                for part in range(2):
                    ins = g.tensor_tensor(kd3[:, n % 2, part],
                                          kr3[:, part, c, b * CTX:(b + 1) * CTX].bitcast(FP32).unsqueeze(1).broadcast_to((P, HPC, CTX)),
                                          hm3[:].unsqueeze(2).broadcast_to((P, HPC, CTX)), ALU.mult)
                ins.then_inc(*sig.mark("keys3", n))

            for s in steps:
                kind, args = s[0], s[1:]
                if kind == "split":
                    split(*args)
                elif kind == "keys3":
                    keys3(*args)
                elif kind == "nf":
                    nf(*args)
                elif kind == "hid2":
                    hid2(*args)
                elif kind == "scores1" and args == (1, 0):
                    small_loads([("down0_product", (1, TILES - 1)), ("x_done", (2, 1))],
                                [("wq1", wq1[:], a["L1_wq"]), ("keyT", keyT[:], a["L1_keysT"]),
                                 ("bq", bq[:], a["L2_bq"]), ("bk", bk[:], a["L2_bk"])])
                elif kind == "stats" and args == (5, 1):
                    pool.wait_ge(*sig.when("pv1_product", (2, B - 1, 1)))
                    pool.wait_ge(*sig.when("x_done", (5, 1)))
                    small_loads([], [("b1c", b1c[:], a["L2_b1"]),
                                     ("b2b", b2b[:], a["L2_b2"][0:2].partition_broadcast(P)),
                                     ("gwf", gwf[:, :, 0:MOE], a["L2_gw"][0:D].rearrange("(k p) n -> p k n", p=P)),
                                     ("gwr", gwr[:, 0:MOE], a["L2_gw"][D].partition_broadcast(P)),
                                     ("gbr", gbr[:, 0:MOE], a["L2_gb"].partition_broadcast(P))])
                    g.memset(gwf[:, :, MOE:4], 0.0).then_inc(*sig.mark("pool_gate", "pad"))
                    for n, t in (("vis", vis), ("txt", txt), ("one", one), ("row0", row0)):
                        g.memset(t[:], 1.0).then_inc(*sig.mark("pool_gate", n))
                    g.memset(p8[:], -1.0).then_inc(*sig.mark("pool_gate", "p8"))
                    pool.wait_ge(*sig.when("pool_gate", "row0"))
                    for n, t, base_, mult in (("visf", vis, VISION - 1, -1), ("txtf", txt, -VISION, 1), ("row0f", row0, 0, -1)):
                        g.affine_select(out=t[:], in_=t[:], compare_op=ALU.is_ge, fill=0.0, base=base_,
                                        pattern=[[0, P]], channel_multiplier=mult).then_inc(*sig.mark("pool_gate", n))
                elif kind == "out2" and args == (1, 0):
                    small_loads([("out2_added", (0, TILES - 1))], [("b2last", b2b[:, 0], a["L2_b2"][2].partition_broadcast(P))])
                elif kind == "stats" and args == (6, 1):
                    pool.wait_ge(*sig.when("out2_product", (MOE - 1, TILES - 1)))
                    pool.wait_ge(*sig.when("x_done", (6, 1)))
                    small_loads([], [("lnw", lnw[:], a["L3_lnw"])])
                    g.memset(hm3[:], 1.0).then_inc(*sig.mark("pool_head", "a"))
                    pool.wait_ge(*sig.when("pool_head", "a"))
                    g.affine_select(out=hm3[:], in_=hm3[:], compare_op=ALU.is_ge, fill=0.0, base=0,
                                    pattern=[[-HD3, HPC]], channel_multiplier=1).then_inc(*sig.mark("pool_head", "b"))
                    pool.wait_ge(*sig.when("pool_head", "b"))
                    g.affine_select(out=hm3[:], in_=hm3[:], compare_op=ALU.is_ge, fill=0.0, base=HD3 - 1,
                                    pattern=[[HD3, HPC]], channel_multiplier=-1).then_inc(*sig.mark("head_mask", 0))
                    g.memset(vd3[:].bitcast(FP32), 0.0).then_inc(*sig.mark("vd3_clear", 0))

        @block.scalar
        def _(act):
            sc = nc.scalar

            def high(stage, key, dst, src, product=None, func=ACT.Copy, **kw):
                act.wait_ge(*sig.when(*(product or (f"{stage}_product", key))))
                sc.activation(dst, src, func, **kw).then_inc(*sig.mark(f"{stage}_high", key))

            def split(i):
                name, p, dims, loads, dest, after = chunks[i]
                act.wait_ge(*sig.when(f"weight_staged{i % 2}", i))
                if dest is None and slot_no[name] >= NSLOT and known:
                    act.wait_ge(*sig.when(*known.user[("chunk", ring_names[slot_no[name] - NSLOT])]))
                if after is not None and after[0] == "down0_product":
                    act.wait_ge(*sig.when(*after))
                sc.activation(weight(name, 0), split_source(i), ACT.Copy).then_inc(*sig.mark("weight_high", i))

            def turn(layer, hf):
                for c in range(KT):
                    key = (layer, hf, c)
                    dst = xT[:, 0, c, hf * HALF:(hf + 1) * HALF]
                    if layer == 6:
                        act.wait_ge(*sig.when("loaded_lnw", 0))
                        high("turn", key, dst, psum(("turn", *key))[:], func=ACT.Identity, scale=lnw[:, c:c + 1])
                    else:
                        high("turn", key, dst, psum(("turn", *key))[:])

            def v0_(hf, i):
                p = P if i < TPH else CTX
                if hf:
                    act.wait_ge(*sig.when("pv0_product", 8 * G0 - 1))
                high("v0", (hf, i), v0[0:p, 0, i], psum(("v0", hf, i))[0:p, 0:G0 * HD0])

            def k0_(s):
                high("k0", s, k0[:, s % 2, 0, :, 0:S], psum(("k0", s))[0:HD0].rearrange("p (b n) -> p b n", b=BPH))

            def kc0_(s):
                high("kc0", s, k0[:, s % 2, 0, :, S:], psum(("kc0", s))[0:HD0, 0:BPH * CTX].rearrange("p (b n) -> p b n", b=BPH))

            def q0_(s, h):
                high("q0", (s, h), q0[:, s % 2, 0, h], psum(("q0", s, h))[0:HD0])

            def scores0(n, s, bl, h):
                act.wait_ge(*sig.when("max0", n))
                for i in range(TPB):
                    if 2 * n + i >= E0_RING:
                        act.wait_ge(*sig.when("turn0_product", (2 * n + i - E0_RING) // 2))
                    sc.activation(e0[:, (2 * n + i) % E0_RING], psum(("scores0", n, i))[:, 0:KEYS0], ACT.Exp, scale=HD0 ** -0.5,
                                  bias=mx[:, n % 4, 2 + i:3 + i], accum_out=sm[:, n % 4, i:i + 1])\
                        .then_inc(*sig.mark("exp0", (n, i)))

            def turn0(n, s, bl, h):
                act.wait_ge(*sig.when("turn0_product", n))
                if n >= 2:
                    act.wait_ge(*sig.when("pv0_product", n - 2))
                sc.activation(eT0[:, n % 2, 0, 0:2], psum(("turn0", n, 0))[:].rearrange("p (k n) -> p k n", k=2),
                              ACT.Copy).then_inc(*sig.mark("turn0_high", (n, 0)))
                sc.activation(eT0[0:CTX, n % 2, 0, 2], psum(("turn0", n, 1))[0:CTX, 0:S],
                              ACT.Copy).then_inc(*sig.mark("turn0_high", (n, 1)))

            def pv0(n, s, bl, h):
                high("pv0", n, q0[:, s % 2, 0, h, bl * S:(bl + 1) * S], psum(("pv0", n))[0:HD0, 0:S])

            def up0(f, hf):
                w, n = fwidth(f), 2 * f + hf
                act.wait_ge(*sig.when("up0_product", (f, hf, 0)))
                if n == 0:
                    act.wait_ge(*sig.when("pv0_low", 63))
                if n >= 2:
                    act.wait_ge(*sig.when("inter0", n - 2))
                sc.activation(g0[0:w, n % 2], psum(("up0", f, hf, 0))[0:w], ACT.Silu, scale=1 / 128)\
                    .then_inc(*sig.mark("silu0", n))
                act.wait_ge(*sig.when("inter0", n))
                if n >= 2:
                    act.wait_ge(*sig.when("h0_done", n - 2))
                sc.activation(f0[0:w, n % 2, 1], f0[0:w, n % 2, 0], ACT.Abs).then_inc(*sig.mark("abs0", n))
                sc.activation(f0[0:w, n % 2, 2], f0[0:w, n % 2, 0], ACT.Sign, scale=-1.0).then_inc(*sig.mark("sign0", n))

            def down0(part, t):
                if part == 0:
                    act.wait_ge(*sig.when("down0_product", (part, t)))
                    sc.activation(acc0[:, t], psum(("down0", part, t))[:], ACT.Copy).then_inc(*sig.mark("down0_part", t))
                else:
                    act.wait_ge(*sig.when("down0_sum", t))
                    sc.activation(f0[:, t % 2, 1], f0[:, t % 2, 0], ACT.Abs, scale=128.0).then_inc(*sig.mark("dabs0", t))
                    sc.activation(f0[:, t % 2, 2], f0[:, t % 2, 0], ACT.Sign, scale=-1.0).then_inc(*sig.mark("dsign0", t))

            def scores1(layer, b):
                n = (layer, b)
                act.wait_ge(*sig.when("max1", n))
                if b >= 2 or layer == 2:
                    prev = (layer, b - 2) if b >= 2 else (1, B - 2 + b)
                    act.wait_ge(*sig.when("turn1_product", prev))
                for i in range(TPB):
                    src = psum(("scores1", layer, b))[:, i * CTX:(i + 1) * CTX] if layer == 1 else s1[:, b % 2, i]
                    sc.activation(e1[:, b % 2, i], src, ACT.Exp, scale=1.0 if layer == 1 else D ** -0.5,
                                  bias=mx[:, b % 4, 2 + i:3 + i], accum_out=sm[:, b % 4, i:i + 1])\
                        .then_inc(*sig.mark("exp1", (layer, b, i)))

            def pv1(layer, b):
                if b >= 2 or layer == 2:
                    prev = (layer, b - 2, 1) if b >= 2 else (1, B - 2 + b, 1)
                    act.wait_ge(*sig.when("pv1_product", prev))
                if (layer, b) == (1, 0):
                    act.wait_ge(*sig.when("down0_product", (1, TILES - 1)))
                high("turn1", (layer, b), eT1[:, b % 2, 0], psum(("turn1", layer, b))[0:CTX, 0:S])

            def route1(t):
                act.wait_ge(*sig.when("route1_rep", t))
                for i, src in ((2, r1[:, 0, t]), (3, r1[:, 1, t])):
                    sc.activation(r1[:, i, t], src, ACT.Exp, bias=rs[:, t:t + 1]).then_inc(*sig.mark("route1_exp", (t, i)))

            def router1():
                high("router1", 0, rw[:, 0], psum(("router1",))[:, 0:KT * NE].rearrange("p (k n) -> p k n", k=KT))

            def zt1(t):
                if t >= 2:
                    act.wait_ge(*sig.when("b1_product", t - 2))
                high("zt1", t, zT[:, t % 2, 0], psum(("zt1", t))[:].rearrange("p (k n) -> p k n", k=KT))

            def k2_(c):
                act.wait_ge(*sig.when("loaded_bk", 0))
                high("k2", c, k2[:, 0, c], psum(("k2", c))[:, 0:B * CTX], func=ACT.Identity, bias=bk[:, c:c + 1])

            def m2_(c):
                high("m2", c, m2[:, 0, c], psum(("m2", c))[:, 0:B * CTX])

            def c2_():
                act.wait_ge(*sig.when("c2_product", 0))
                sc.activation(c2[:], psum(("c2",))[:, 0:B * CTX], ACT.Copy).then_inc(*sig.mark("c2_ready", 0))

            def bias2():
                act.wait_ge(*sig.when("bq_wide", 0))
                sc.activation(bqw[:, 0], bqf[:], ACT.Copy).then_inc(*sig.mark("bq_high", 0))

            def gate2(t):
                if t == 0:
                    act.wait_ge(*sig.when("pool_gate", "pad"))
                    act.wait_ge(*sig.when("loaded_gwf", 0))
                    sc.activation(gw[:, 0], gwf[:], ACT.Copy).then_inc(*sig.mark("gw_high", 0))

            def moe(part):
                if part != 1:
                    return
                act.wait_ge(*sig.when("moe_shift", 0))
                sc.activation(lg[:, :, 0:MOE], lg[:, :, 0:MOE], ACT.Exp).then_inc(*sig.mark("moe_exp", 0))

            def hid2(e, c, hf):
                i = (e * KT + c) * 2 + hf
                act.wait_ge(*sig.when("hid2_product", (e, c, hf)))
                act.wait_ge(*sig.when("loaded_b1c", 0))
                if i >= 2:
                    e_, r_ = divmod(i - 2, 2 * KT)
                    act.wait_ge(*sig.when("h2_low", (e_, r_ // 2, r_ % 2)))
                func = (ACT.Tanh, ACT.Gelu, ACT.Silu)[e]
                sc.activation(hf2[:, i % 2], psum(("hid2", e, c, hf))[:], func, bias=b1c[:, e, c:c + 1])\
                    .then_inc(*sig.mark("hid2_value", (e, c, hf)))

            def k3_(c):
                high("k3", c, kr3[:, 0, c], psum(("k3", c))[:, 0:B * CTX])

            def v3_(b):
                high("v3", b, v3[:, 0, b], psum(("v3", b))[0:CTX, 0:KV3 * HD3])

            def q3_(c, hf):
                high("q3", (c, hf), q3[:, 0, c, hf * HALF:(hf + 1) * HALF], psum(("q3", c, hf))[:])

            def scores3(n, b, c):
                for i in range(TPB):
                    act.wait_ge(*sig.when("shift3", (n, i)))
                    sc.activation(e3[:, n % 2, i], e3[:, n % 2, i], ACT.Exp, scale=HD3 ** -0.5)\
                        .then_inc(*sig.mark("exp3", (n, i)))

            def turn3(n, b, c):
                for i in range(2):
                    act.wait_ge(*sig.when("turn3_product", (n, i)))
                    if n >= 1:
                        act.wait_ge(*sig.when("pv3_product", n - 1))
                    sc.activation(eT3[:, 0, 2 * i:2 * i + 2], psum(("turn3", n, i))[:].rearrange("p (k n) -> p k n", k=2),
                                  ACT.Copy).then_inc(*sig.mark("turn3_high", (n, i)))

            def pv3(n, b, c):
                high("pv3", n, q3[:, 0, c, b * S:(b + 1) * S], psum(("pv3", n))[:, 0:S])

            def up3(f, hf):
                w, n = fwidth(f), 2 * f + hf
                act.wait_ge(*sig.when("up3_product", (f, hf, 0)))
                if n == 0:
                    act.wait_ge(*sig.when("pv3_low", 15))
                    act.wait_ge(*sig.when("nf4_stored0", 3 * FT - 1))
                if n >= 3:
                    act.wait_ge(*sig.when("h3_low", n - 3))
                sc.activation(g3[0:w, n % 3], psum(("up3", f, hf, 0))[0:w], ACT.Silu).then_inc(*sig.mark("silu3", n))

            def nf_turn(m):
                for i in range(2):
                    act.wait_ge(*sig.when("nf4_turn_product", m))
                    if m:
                        act.wait_ge(*sig.when(f"nf4_maxima_stored{i}", m - 1))
                    elif i == 0:
                        act.wait_ge(*sig.when("nf4_max", (0, 0)))
                    sc.activation(nf_t[0:88, i], psum(("nf_turn", m))[0:88, i * P:(i + 1) * P], ACT.Copy)\
                        .then_inc(*sig.mark("nf4_turned", (m, i)))

            handlers = {"split": split, "turn": turn, "v0": v0_, "k0": k0_, "kc0": kc0_, "q0": q0_, "scores0": scores0,
                        "turn0": turn0, "pv0": pv0, "up0": up0, "down0": down0, "scores1": scores1, "pv1": pv1, "bias2": bias2,
                        "route1": route1, "router1": router1, "zt1": zt1, "k2": k2_, "m2": m2_, "c2": c2_,
                        "gate2": gate2, "moe": moe, "hid2": hid2, "k3": k3_, "v3": v3_, "q3": q3_,
                        "scores3": scores3, "turn3": turn3, "pv3": pv3, "up3": up3, "nf_turn": nf_turn}
            for s in steps:
                if s[0] in handlers:
                    handlers[s[0]](*s[1:])

        @block.vector
        def _(dve):
            v = nc.vector
            links = [0]

            def link(ins):
                links[0] += 1
                ins.then_inc(sig.sem("vector_chain"), 1)
                dve.wait_ge(sig.sem("vector_chain"), links[0])

            def low(stage, key, dst, src, hi):
                dve.wait_ge(*sig.when(f"{stage}_high", key))
                v.tensor_tensor(dst, src, hi.bitcast(FP32), ALU.subtract).then_inc(*sig.mark(f"{stage}_low", key))

            def rsqrt(y, t, tmp, scale=None):
                ib = y.bitcast(INT32)
                link(v.tensor_scalar(ib, t.bitcast(INT32), 1, None, ALU.logical_shift_right))
                link(v.tensor_scalar(ib, ib, -1.0, 1597463007.0, ALU.mult, ALU.add))
                link(v.tensor_scalar(tmp[0], t, -0.5, None, ALU.mult))
                for _ in range(4):
                    link(v.tensor_tensor(tmp[1], y, y, ALU.mult))
                    link(v.tensor_tensor(tmp[1], tmp[1], tmp[0], ALU.mult))
                    link(v.scalar_tensor_tensor(y, tmp[1], 1.5, y, ALU.add, ALU.mult))

            def stats(layer, hf):
                ts = range(hf * TPH, (hf + 1) * TPH)
                sl = slice(hf * TPH, (hf + 1) * TPH)
                if layer == 0:
                    dve.wait_ge(*sig.when(f"x_loaded{hf}", 0))
                else:
                    dve.wait_ge(*sig.when("x_done", (layer, hf)))
                for t in ts:
                    ins = v.bn_stats(st[:, t], x[:, t])
                link(ins)
                for t in ts:
                    ins = v.bn_aggr(mv[:, t], st[:, t])
                link(ins)
                link(v.tensor_scalar(rt[:, 0, sl], mv[:, sl, 1], LN_EPS, None, ALU.add))
                rsqrt(rs[:, sl], rt[:, 0, sl], (rt[:, 1, sl], rt[:, 2, sl]))
                if layer == 6:
                    link(v.tensor_tensor(rt[:, 0, sl], rs[:, sl], rs[:, sl], ALU.mult))
                    link(v.tensor_tensor(rt[:, 0, sl], rt[:, 0, sl], mv[:, sl, 1], ALU.mult))
                    link(v.tensor_scalar(rt[:, 0, sl], rt[:, 0, sl], LN_EPS, None, ALU.add))
                    rsqrt(rt[:, 3, sl], rt[:, 0, sl], (rt[:, 1, sl], rt[:, 2, sl]))
                    link(v.tensor_tensor(rs[:, sl], rs[:, sl], rt[:, 3, sl], ALU.mult))
                if layer or hf:
                    prev = (layer, 0, KT - 1) if hf else (layer - 1, 1, KT - 1)
                    dve.wait_ge(*sig.when("turn_product", prev))
                for t in ts:
                    v.tensor_scalar(xn[:, t % TPH], x[:, t], mv[:, t, 0:1], rs[:, t:t + 1], ALU.subtract, ALU.mult)\
                        .then_inc(*sig.mark("normalised", (layer, t)))
                if layer == 5:
                    dve.wait_ge(*sig.when("normalised", (layer, ts[-1])))
                    v.tensor_reduce(ab[:, sl], xn[:], AX.X, ALU.add, apply_absolute_value=True)\
                        .then_inc(*sig.mark("strength", hf))

            def turn(layer, hf):
                for c in range(KT):
                    key = (layer, hf, c)
                    cs = slice(hf * HALF, (hf + 1) * HALF)
                    if layer == 6:
                        dve.wait_ge(*sig.when("turn_high", key))
                        v.scalar_tensor_tensor(xT[:, 1, c, cs], psum(("turn", *key))[:], lnw[:, c:c + 1],
                                               xT[:, 0, c, cs].bitcast(FP32), ALU.mult, ALU.subtract)\
                            .then_inc(*sig.mark("turn_low", key))
                    else:
                        low("turn", key, xT[:, 1, c, cs], psum(("turn", *key))[:], xT[:, 0, c, cs])

            def v0_(hf, i):
                p = P if i < TPH else CTX
                low("v0", (hf, i), v0[0:p, 1, i], psum(("v0", hf, i))[0:p, 0:G0 * HD0], v0[0:p, 0, i])

            def k0_(s):
                low("k0", s, k0[:, s % 2, 1, :, 0:S], psum(("k0", s))[0:HD0].rearrange("p (b n) -> p b n", b=BPH),
                    k0[:, s % 2, 0, :, 0:S])

            def kc0_(s):
                low("kc0", s, k0[:, s % 2, 1, :, S:],
                    psum(("kc0", s))[0:HD0, 0:BPH * CTX].rearrange("p (b n) -> p b n", b=BPH), k0[:, s % 2, 0, :, S:])

            def q0_(s, h):
                low("q0", (s, h), q0[:, s % 2, 1, h], psum(("q0", s, h))[0:HD0], q0[:, s % 2, 0, h])

            def scores0(n, s, bl, h):
                for i in range(TPB):
                    dve.wait_ge(*sig.when("scores0_product", (n, i)))
                    ins = v.tensor_reduce(mx[:, n % 4, i:i + 1], psum(("scores0", n, i))[:, 0:KEYS0], AX.X, ALU.max,
                                          negate=True)
                link(ins)
                v.tensor_scalar(mx[:, n % 4, 2:4], mx[:, n % 4, 0:2], HD0 ** -0.5, None, ALU.mult)\
                    .then_inc(*sig.mark("max0", n))

            def scale0(n):
                dve.wait_ge(*sig.when("exp0", (n, TPB - 1)))
                link(v.reciprocal(sm[:, n % 4, 2:4], sm[:, n % 4, 0:2]))
                for i in range(TPB):
                    v.tensor_scalar(e0[:, (2 * n + i) % E0_RING], e0[:, (2 * n + i) % E0_RING], sm[:, n % 4, 2 + i:3 + i], None, ALU.mult)\
                        .then_inc(*sig.mark("probs0", (n, i)))

            def turn0(n, s, bl, h):
                dve.wait_ge(*sig.when("turn0_high", (n, 0)))
                v.tensor_tensor(eT0[:, n % 2, 1, 0:2], psum(("turn0", n, 0))[:].rearrange("p (k n) -> p k n", k=2),
                                eT0[:, n % 2, 0, 0:2].bitcast(FP32), ALU.subtract).then_inc(*sig.mark("turn0_low", (n, 0)))
                dve.wait_ge(*sig.when("turn0_high", (n, 1)))
                v.tensor_tensor(eT0[0:CTX, n % 2, 1, 2], psum(("turn0", n, 1))[0:CTX, 0:S],
                                eT0[0:CTX, n % 2, 0, 2].bitcast(FP32), ALU.subtract).then_inc(*sig.mark("turn0_low", (n, 1)))

            def pv0(n, s, bl, h):
                cs = slice(bl * S, (bl + 1) * S)
                low("pv0", n, q0[:, s % 2, 1, h, cs], psum(("pv0", n))[0:HD0, 0:S], q0[:, s % 2, 0, h, cs])

            def add_to_x(stage, key, t, src, name=None, mark=None, scale=None):
                dve.wait_ge(*sig.when(f"{stage}_product", key))
                if mark is None:
                    mark = (f"{stage}_added", key)
                if scale is None:
                    v.tensor_tensor(x[:, t], src, x[:, t], ALU.add).then_inc(*sig.mark(*mark))
                else:
                    v.scalar_tensor_tensor(x[:, t], src, scale, x[:, t], ALU.mult, ALU.add).then_inc(*sig.mark(*mark))

            def o0(s, i):
                t = (s // G0) * TPH + i
                if s % G0:
                    dve.wait_ge(*sig.when("o0_added", (s - 1, i)))
                add_to_x("o0", (s, i), t, psum(("o0", s, i))[:])
                if s % G0 == G0 - 1 and i == TPH - 1:
                    done(1, s // G0, "o0_added", (s, i))

            def done(layer, hf, name, key):
                dve.wait_ge(*sig.when(name, key))
                v.tensor_copy(rt[0:1, 3, 0:1], x[0:1, hf * TPH, 0:1]).then_inc(*sig.mark("x_done", (layer, hf)))

            def cut(n, p):
                f = f0[0:p, n % 2]
                link(v.tensor_scalar(f[:, 3], f[:, 1], ROUND, ROUND, ALU.add, ALU.subtract))
                link(v.tensor_tensor(f[:, 4], f[:, 1], f[:, 3], ALU.subtract))
                link(v.scalar_tensor_tensor(f[:, 4], f[:, 4], 0.0, f[:, 3], ALU.is_lt, ALU.subtract))
                link(v.tensor_tensor(f[:, 3], f[:, 4], f[:, 2], ALU.mult))
                return f[:, 3]

            def finish_up0(n):
                f, hf = divmod(n, 2)
                w = fwidth(f)
                dve.wait_ge(*sig.when("sign0", n))
                dve.wait_ge(*sig.when("abs0", n))
                if f >= half_f:
                    dve.wait_ge(*sig.when("down0_product", (0, TILES - 1)))
                v.tensor_scalar(h0[0:w, f % half_f, hf * HALF:(hf + 1) * HALF], cut(n, w), -128.0, 127.0, ALU.max, ALU.min)\
                    .then_inc(*sig.mark("h0_done", n))

            def up0(f, hf):
                w, n = fwidth(f), 2 * f + hf
                dve.wait_ge(*sig.when("silu0", n))
                dve.wait_ge(*sig.when("up0_product", (f, hf, 1)))
                if n >= 2:
                    dve.wait_ge(*sig.when("sign0", n - 2))
                if n == 0:
                    dve.wait_ge(*sig.when("pv0_product", 63))
                v.tensor_tensor(f0[0:w, n % 2, 0], psum(("up0", f, hf, 1))[0:w], g0[0:w, n % 2], ALU.mult)\
                    .then_inc(*sig.mark("inter0", n))
                if n % (2 * half_f):
                    finish_up0(n - 1)
                if n in (2 * half_f - 1, 2 * FT - 1):
                    finish_up0(n)

            def finish_down0(t):
                dve.wait_ge(*sig.when("dabs0", t))
                dve.wait_ge(*sig.when("dsign0", t))
                link(v.tensor_scalar(f0[:, t % 2, 0], cut(t, P), -128.0, 127.0, ALU.max, ALU.min))
                v.tensor_tensor(x[:, t], x[:, t], f0[:, t % 2, 0], ALU.add).then_inc(*sig.mark("x_done0", t))

            def down0(part, t):
                if part == 0:
                    return
                dve.wait_ge(*sig.when("down0_product", (part, t)))
                dve.wait_ge(*sig.when("down0_part", t))
                if t >= 2:
                    dve.wait_ge(*sig.when("x_done0", t - 2))
                elif t == 0:
                    dve.wait_ge(*sig.when("h0_done", 2 * FT - 1))
                    dve.wait_ge(*sig.when("sign0", 2 * FT - 1))
                v.tensor_tensor(f0[:, t % 2, 0], psum(("down0", part, t))[:], acc0[:, t], ALU.add)\
                    .then_inc(*sig.mark("down0_sum", t))
                if t % TPH:
                    finish_down0(t - 1)
                if t % TPH == TPH - 1:
                    finish_down0(t)
                    done(2, t // TPH, "x_done0", t)

            def scores1(layer, b):
                dve.wait_ge(*sig.when("scores1_product", (layer, b)))
                src = psum(("scores1", layer, b))[:, 0:TPB * CTX].rearrange("p (i n) -> p i n", i=TPB)
                if layer == 2:
                    dve.wait_ge(*sig.when("c2_ready", 0))
                    if b >= 2:
                        dve.wait_ge(*sig.when("exp1", (layer, b - 2, TPB - 1)))
                    for i in range(TPB):
                        ins = v.tensor_tensor(s1[:, b % 2, i], src[:, i], c2[:, b * CTX:(b + 1) * CTX], ALU.add)
                    ins.then_inc(*sig.mark("biased2", b))
                    dve.wait_ge(*sig.when("biased2", b))
                    src = s1[:, b % 2]
                link(v.tensor_reduce(mx[:, b % 4, 0:2], src, AX.X, ALU.max, negate=True))
                v.tensor_scalar(mx[:, b % 4, 2:4], mx[:, b % 4, 0:2], 1.0 if layer == 1 else D ** -0.5, None, ALU.mult)\
                    .then_inc(*sig.mark("max1", (layer, b)))
                dve.wait_ge(*sig.when("exp1", (layer, b, TPB - 1)))
                link(v.reciprocal(sm[:, b % 4, 2:4], sm[:, b % 4, 0:2]))
                for i in range(TPB):
                    v.tensor_scalar(e1[:, b % 2, i], e1[:, b % 2, i], sm[:, b % 4, 2 + i:3 + i], None, ALU.mult)\
                        .then_inc(*sig.mark("probs1", (layer, b, i)))

            def pv1(layer, b):
                low("turn1", (layer, b), eT1[:, b % 2, 1], psum(("turn1", layer, b))[0:CTX, 0:S], eT1[:, b % 2, 0])
                for i in range(TPB):
                    add_to_x("pv1", (layer, b, i), TPB * b + i, psum(("pv1", layer, b, i))[:])
                if b % BPH == BPH - 1:
                    done(3 if layer == 1 else 5, b // BPH, "pv1_added", (layer, b, 1))

            def router1():
                low("router1", 0, rw[:, 1], psum(("router1",))[:, 0:KT * NE].rearrange("p (k n) -> p k n", k=KT), rw[:, 0])

            def route1(t):
                dve.wait_ge(*sig.when("route1_product", t))
                ss = r1[:, 0, t]
                link(v.tensor_copy(ss, psum(("route1", t))[:, 0:NE]))
                link(v.max(top8[:, 0, t], ss))
                link(v.match_replace(r1[:, 1, t], top8[:, 0, t], ss, -1e30))
                link(v.max(top8[:, 1, t], r1[:, 1, t]))
                link(v.match_replace(r1[:, 1, t], top8[:, 1, t], r1[:, 1, t], -1e30))
                v.tensor_scalar(rs[:, t:t + 1], top8[:, 0, t, 0:1], -1.0, None, ALU.mult)\
                    .then_inc(*sig.mark("route1_rep", t))
                dve.wait_ge(*sig.when("route1_exp", (t, 3)))
                link(v.tensor_tensor(r1[:, 0, t], r1[:, 2, t], r1[:, 3, t], ALU.subtract))
                link(v.tensor_reduce(rt[:, 1, t:t + 1], r1[:, 0, t], AX.X, ALU.add))
                link(v.reciprocal(rt[:, 2, t:t + 1], rt[:, 1, t:t + 1]))
                v.tensor_scalar(r1[:, 1, t], r1[:, 0, t], rt[:, 2, t:t + 1], None, ALU.mult)\
                    .then_inc(*sig.mark("gate1", t))

            def z1(t):
                pass

            def zt1(t):
                dve.wait_ge(*sig.when("z1_product", t))
                dve.wait_ge(*sig.when("gate1", t))
                if t >= 2:
                    dve.wait_ge(*sig.when("zt1_product", t - 2))
                v.tensor_tensor(zg[:, t % 2].rearrange("p (e r) -> p e r", e=NE),
                                psum(("z1", t))[:].rearrange("p (e r) -> p e r", e=NE),
                                r1[:, 1, t].unsqueeze(2).broadcast_to((P, NE, RANK)), ALU.mult)\
                    .then_inc(*sig.mark("gated1", t))
                low("zt1", t, zT[:, t % 2, 1], psum(("zt1", t))[:].rearrange("p (k n) -> p k n", k=KT), zT[:, t % 2, 0])

            def b1(t):
                add_to_x("b1", t, t, psum(("b1", t))[:], scale=2.0)
                if t % TPH == TPH - 1:
                    done(4, t // TPH, "b1_added", t)

            def k2_(c):
                dve.wait_ge(*sig.when("k2_high", c))
                v.scalar_tensor_tensor(k2[:, 1, c], psum(("k2", c))[:, 0:B * CTX], bk[:, c:c + 1],
                                       k2[:, 0, c].bitcast(FP32), ALU.add, ALU.subtract).then_inc(*sig.mark("k2_low", c))

            def m2_(c):
                low("m2", c, m2[:, 1, c], psum(("m2", c))[:, 0:B * CTX], m2[:, 0, c])

            def bias2():
                v.memset(bqf[:], 1.0).then_inc(*sig.mark("ones_ready", 0))
                dve.wait_ge(*sig.when("loaded_bq", 0))
                dve.wait_ge(*sig.when("ones_ready", 0))
                for c in range(KT):
                    ins = v.tensor_scalar(bqf[:, c], bqf[:, c], bq[:, c:c + 1], None, ALU.mult)
                ins.then_inc(*sig.mark("bq_wide", 0))
                dve.wait_ge(*sig.when("bq_high", 0))
                v.tensor_tensor(bqw[:, 1], bqf[:], bqw[:, 0].bitcast(FP32), ALU.subtract).then_inc(*sig.mark("bq_low", 0))

            def gate2(t):
                if t == 0:
                    dve.wait_ge(*sig.when("gw_high", 0))
                    v.tensor_tensor(gw[:, 1], gwf[:], gw[:, 0].bitcast(FP32), ALU.subtract).then_inc(*sig.mark("gw_low", 0))
                dve.wait_ge(*sig.when("gate2_product", t))
                v.tensor_copy(lg[:, t, 0:MOE], psum(("gate2", t))[:, 0:MOE]).then_inc(*sig.mark("logits2", t))

            def moe0():
                dve.wait_ge(*sig.when("strength_product", 0))
                pb = psum(("strength",))
                dve.wait_ge(*sig.when("logits2", TILES - 1))
                link(v.tensor_copy(gt[:, 0:3, 0:B], pb[:, 0:3 * B].rearrange("p (a b) -> p a b", a=3)))
                link(v.tensor_tensor(ra[:, 0, 0:B], gt[:, 1, 0:B], gt[:, 2, 0:B], ALU.add))
                link(v.tensor_scalar(ra[:, 0, 0:B], ra[:, 0, 0:B], 1.0 / ((S - VISION) * D), None, ALU.mult))
                link(v.tensor_scalar(ra[:, 1, 0:B], gt[:, 0, 0:B], 1.0 / (VISION * D), 1e-8, ALU.mult, ALU.add))
                link(v.reciprocal(ra[:, 2, 0:B], ra[:, 1, 0:B]))
                ratio = ra[:, 3, :].rearrange("p (b i) -> p b i", i=TPB)
                for i in range(TPB):
                    ins = v.tensor_tensor(ratio[:, :, i], ra[:, 0, 0:B], ra[:, 2, 0:B], ALU.mult)
                link(ins)
                dve.wait_ge(*sig.when("loaded_gwr", 0))
                dve.wait_ge(*sig.when("loaded_gbr", 0))
                for e in range(MOE):
                    link(v.scalar_tensor_tensor(lg[:, :, e], ra[:, 3], gwr[:, e:e + 1], lg[:, :, e], ALU.mult, ALU.add))
                    link(v.tensor_scalar(lg[:, :, e], lg[:, :, e], gbr[:, e:e + 1], None, ALU.add))
                link(v.tensor_reduce(gt[:, 0], lg[:, :, 0:MOE], AX.X, ALU.max))
                v.tensor_tensor(lg[:, :, 0:MOE], lg[:, :, 0:MOE], gt[:, 0].unsqueeze(2).broadcast_to((P, TILES, MOE)),
                                ALU.subtract).then_inc(*sig.mark("moe_shift", 0))

            def moe1():
                dve.wait_ge(*sig.when("moe_exp", 0))
                link(v.tensor_reduce(gt[:, 1], lg[:, :, 0:MOE], AX.X, ALU.add))
                link(v.reciprocal(gt[:, 2], gt[:, 1]))
                dve.wait_ge(*sig.when("pool_gate", "p8"))
                link(v.tensor_tensor(p8[:, :, 0:MOE], lg[:, :, 0:MOE], gt[:, 2].unsqueeze(2).broadcast_to((P, TILES, MOE)),
                                     ALU.mult))
                for t in range(TILES):
                    ins = v.max(t8[:, t], p8[:, t])
                link(ins)
                link(v.tensor_tensor(gt[:, 3], t8[:, :, 0], t8[:, :, 1], ALU.add))
                link(v.tensor_scalar(gt[:, 3], gt[:, 3], 1e-8, None, ALU.add))
                link(v.reciprocal(gt[:, 4], gt[:, 3]))
                link(v.tensor_tensor(gt[:, 5], t8[:, :, 0], gt[:, 4], ALU.mult))
                link(v.tensor_tensor(gt[:, 6], t8[:, :, 1], gt[:, 4], ALU.mult))

            def moe2():
                A_, B_, C_ = (p8[:, :, e] for e in range(MOE))
                link(v.tensor_tensor(gt[:, 7], A_, B_, ALU.is_ge))
                link(v.tensor_tensor(gt[:, 8], A_, C_, ALU.is_ge))
                link(v.tensor_tensor(gt[:, 9], B_, C_, ALU.is_ge))
                link(v.tensor_scalar(gt[:, 10], gt[:, 7], -1.0, 1.0, ALU.mult, ALU.add))
                link(v.tensor_scalar(gt[:, 11], gt[:, 9], -1.0, 1.0, ALU.mult, ALU.add))
                link(v.tensor_scalar(gt[:, 4], gt[:, 8], -1.0, 1.0, ALU.mult, ALU.add))
                for i, e, p_, q_ in ((0, 0, 7, 8), (0, 1, 10, 9), (0, 2, 4, 11), (1, 2, 8, 9), (1, 1, 7, 11), (1, 0, 10, 4)):
                    link(v.tensor_tensor(fl[:, i, e], gt[:, p_], gt[:, q_], ALU.mult))
                link(v.tensor_tensor(fl[:, 1], fl[:, 0], fl[:, 1], ALU.add))
                v.tensor_scalar(fl[:, 1], fl[:, 1], -1.0, 1.0, ALU.mult, ALU.add).then_inc(*sig.mark("choice2", 0))

            def moe3():
                dve.wait_ge(*sig.when("choice_product", 0))
                src = psum(("choice",))[:, 0:2 * MOE * TILES].rearrange("p (a b i) -> p a b i", a=2 * MOE, i=TPB)
                fbv = fb[:].rearrange("p c e t -> p (c e) t").rearrange("p a (b i) -> p a b i", i=TPB)
                for i in range(TPB):
                    ins = v.tensor_copy(fbv[:, :, :, i], src[:, :, :, 0])
                ins.then_inc(*sig.mark("choice_taken", 0))
                dve.wait_ge(*sig.when("choice_taken", 0))
                for e in range(MOE):
                    link(v.tensor_tensor(cf[:, e], fb[:, 0, e], gt[:, 5], ALU.mult))
                    link(v.tensor_tensor(gt[:, 3], fb[:, 1, e], gt[:, 6], ALU.mult))
                    link(v.tensor_tensor(cf[:, e], cf[:, e], gt[:, 3], ALU.add))

            def moe(part):
                (moe0, moe1, moe2, moe3)[part]()

            def hid2(e, c, hf):
                i = (e * KT + c) * 2 + hf
                dve.wait_ge(*sig.when("hid2_value", (e, c, hf)))
                if e >= 2:
                    dve.wait_ge(*sig.when("out2_product", (e - 2, TILES - 1)))
                v.tensor_copy(h2[:, e % 2, 0, c, hf * HALF:(hf + 1) * HALF], hf2[:, i % 2])\
                    .then_inc(*sig.mark("h2_high", (e, c, hf)))

            def out2(e, t):
                dve.wait_ge(*sig.when("out2_product", (e, t)))
                dve.wait_ge(*sig.when("loaded_b2last" if e == MOE - 1 else "loaded_b2b", 0))
                if (e, t) != (0, 0):
                    dve.wait_ge(*sig.when("out2_added", (e, t - 1) if t else (e - 1, TILES - 1)))
                link(v.tensor_tensor(y2[:], psum(("out2", e, t))[:], b2b[:, e % 2], ALU.add))
                v.scalar_tensor_tensor(x[:, t], y2[:], cf[:, e, t:t + 1], x[:, t], ALU.mult, ALU.add)\
                    .then_inc(*sig.mark("out2_added", (e, t)))
                if e == MOE - 1 and t % TPH == TPH - 1:
                    done(6, t // TPH, "out2_added", (e, t))

            def k3_(c):
                low("k3", c, kr3[:, 1, c], psum(("k3", c))[:, 0:B * CTX], kr3[:, 0, c])

            def v3_(b):
                low("v3", b, v3[:, 1, b], psum(("v3", b))[0:CTX, 0:KV3 * HD3], v3[:, 0, b])

            def q3_(c, hf):
                cs = slice(hf * HALF, (hf + 1) * HALF)
                low("q3", (c, hf), q3[:, 1, c, cs], psum(("q3", c, hf))[:], q3[:, 0, c, cs])

            def values3(n, b, c):
                if n >= 2:
                    dve.wait_ge(*sig.when("pv3_product", n - 2))
                dve.wait_ge(*sig.when("vd3_clear", 0))
                dve.wait_ge(*sig.when("v3_low", b))
                groups = HPC // REP3
                for part in range(2):
                    src = v3[:, part, b, c * groups * HD3:(c + 1) * groups * HD3].bitcast(FP32)\
                        .rearrange("p (u d) -> p u d", d=HD3).unsqueeze(2).broadcast_to((CTX, groups, PAIRS // groups, HD3))
                    for j in range(2):
                        blocks = vd3[CTX * j:CTX * (j + 1), n % 2, part].rearrange("p q (a d) -> p (q a) d", d=HD3)
                        dst = blocks[:, j::HPC + 2].rearrange("p (u w) d -> p u w d", u=groups)
                        ins = v.tensor_copy(dst, src)
                ins.then_inc(*sig.mark("values3", n))

            def scores3(n, b, c):
                for i in range(TPB):
                    dve.wait_ge(*sig.when("scores3_product", (n, i)))
                    src = psum(("scores3", n, i))[:].rearrange("p (h k) -> p h k", h=HPC)
                    link(v.tensor_reduce(mx[:, n % 4, i * HPC:(i + 1) * HPC], src, AX.X, ALU.max))
                    if n >= 2:
                        dve.wait_ge(*sig.when("turn3_product", (n - 2, 1)))
                    v.tensor_tensor(e3[:, n % 2, i].rearrange("p (h k) -> p h k", h=HPC), src,
                                    mx[:, n % 4, i * HPC:(i + 1) * HPC].unsqueeze(2).broadcast_to((P, HPC, CTX)),
                                    ALU.subtract).then_inc(*sig.mark("shift3", (n, i)))

            def scale3(n):
                for i in range(TPB):
                    dve.wait_ge(*sig.when("exp3", (n, i)))
                    e = e3[:, n % 2, i].rearrange("p (h k) -> p h k", h=HPC)
                    hs = slice(i * HPC, (i + 1) * HPC)
                    link(v.tensor_reduce(sm[:, n % 4, hs], e, AX.X, ALU.add))
                    link(v.reciprocal(mx[:, n % 4, hs], sm[:, n % 4, hs]))
                    v.tensor_tensor(e, e, mx[:, n % 4, hs].unsqueeze(2).broadcast_to((P, HPC, CTX)), ALU.mult)\
                        .then_inc(*sig.mark("probs3", (n, i)))

            def turn3(n, b, c):
                for i in range(2):
                    dve.wait_ge(*sig.when("turn3_high", (n, i)))
                    v.tensor_tensor(eT3[:, 1, 2 * i:2 * i + 2], psum(("turn3", n, i))[:].rearrange("p (k n) -> p k n", k=2),
                                    eT3[:, 0, 2 * i:2 * i + 2].bitcast(FP32), ALU.subtract)\
                        .then_inc(*sig.mark("turn3_low", (n, i)))

            def pv3(n, b, c):
                cs = slice(b * S, (b + 1) * S)
                low("pv3", n, q3[:, 1, c, cs], psum(("pv3", n))[:, 0:S], q3[:, 0, c, cs])

            def o3(t):
                add_to_x("o3", t, t, psum(("o3", t))[:])
                if t % TPH == TPH - 1:
                    done(7, t // TPH, "o3_added", t)

            def up3(f, hf):
                w, n = fwidth(f), 2 * f + hf
                cs = slice(hf * HALF, (hf + 1) * HALF)
                fi = f % half_f
                dve.wait_ge(*sig.when("silu3", n))
                dve.wait_ge(*sig.when("up3_product", (f, hf, 1)))
                if f >= half_f:
                    dve.wait_ge(*sig.when("down3_product", (0, TILES - 1)))
                if n == 0:
                    dve.wait_ge(*sig.when("o3_product", TILES - 1))
                link(v.tensor_tensor(g3[0:w, n % 3], psum(("up3", f, hf, 1))[0:w], g3[0:w, n % 3], ALU.mult))
                link(v.tensor_copy(h3[0:w, 0, fi, cs], g3[0:w, n % 3]))
                v.tensor_tensor(h3[0:w, 1, fi, cs], g3[0:w, n % 3], h3[0:w, 0, fi, cs].bitcast(FP32), ALU.subtract)\
                    .then_inc(*sig.mark("h3_low", n))

            def down3(part, t):
                if part:
                    dve.wait_ge(*sig.when("down3_added", (0, t)))
                add_to_x("down3", (part, t), t, psum(("down3", part, t))[:])

            def nf_max_(m, f):
                w = fwidth(f) if m < 2 else P
                n = D if m < 2 or f < 10 else 6 * BLOCK
                i = m * FT + f
                dve.wait_ge(*sig.when(f"nf4_rows{i % 4}", (m, f)))
                if (m, f) == (0, 0):
                    link(v.memset(nf_m[:], 0.0))
                v.tensor_reduce(nf_m[0:w, 0, f * 8:f * 8 + n // BLOCK], rows_buffer(i)[0:w, 0:n].rearrange("p (b k) -> p b k", k=BLOCK),
                                AX.X, ALU.max, apply_absolute_value=True).then_inc(*sig.mark("nf4_max", (m, f)))
                if f == FT - 1:
                    dve.wait_ge(*sig.when("nf4_max", (m, f)))
                    c = 88 if m < 2 else 86
                    if m:
                        dve.wait_ge(*sig.when("nf4_turn_product", m - 1))
                    link(v.tensor_copy(nf_m[:, 1, 0:88], nf_m[:, 0, 0:88]))
                    link(v.tensor_scalar(nf_m[:, 2, 0:88], nf_m[:, 1, 0:88], TINY, None, ALU.max))
                    v.reciprocal(nf_m[:, 2, 0:88], nf_m[:, 2, 0:88]).then_inc(*sig.mark("nf4_rcp", m))

            def nf(n, m, f, j):
                w = fwidth(f)
                rows, size = (P, KT * w) if m < 2 else (w, D)
                w_ = nf_w[0:rows, n % 2, 0:size]
                if j == 1:
                    dve.wait_ge(*sig.when(f"nf4_weights{n % 2}", n))
                    v.tensor_tensor(w_, w_, nf_r[0:rows, 0:size], ALU.mult).then_inc(*sig.mark("nf4_scaled", n))
                    dve.wait_ge(*sig.when("nf4_scaled", n))
                part = nf_y[0:rows, part_no(n, j), 0:size]
                if j >= 4:
                    dve.wait_ge(*sig.when("nf4_added", (n, j - 2)))
                elif n and j == 3:
                    dve.wait_ge(*sig.when("nf4_dequantised", n - 1))
                elif n:
                    dve.wait_ge(*sig.when("nf4_added", (n - 1, NPART - NPART % 2 if j == 1 else NPART - 1 + NPART % 2)))
                at, numbers = PARTS[j - 1]
                if j == 1:
                    link(v.tensor_scalar(part, w_, float(BOUNDS[0]), numbers[0], ALU.is_gt, ALU.mult))
                    ins = v.tensor_scalar(part, part, float(CODE[0]), None, ALU.add)
                elif len(numbers) == 1:
                    ins = v.tensor_scalar(part, w_, float(BOUNDS[at]), numbers[0], ALU.is_gt, ALU.mult)
                else:
                    link(v.tensor_scalar(part, w_, float(BOUNDS[at + 1]), numbers[1], ALU.is_gt, ALU.mult))
                    link(v.scalar_tensor_tensor(part, w_, float(BOUNDS[at]), part, ALU.is_gt, ALU.add))
                    ins = v.tensor_scalar(part, part, numbers[0], None, ALU.mult)
                ins.then_inc(*sig.mark("nf4_step", (n, j)))

            handlers = {"stats": stats, "turn": turn, "v0": v0_, "k0": k0_, "kc0": kc0_, "q0": q0_, "scores0": scores0,
                        "turn0": turn0, "scale0": scale0, "scale3": scale3, "pv0": pv0, "o0": o0, "up0": up0, "down0": down0, "scores1": scores1,
                        "pv1": pv1, "router1": router1, "route1": route1, "z1": z1, "zt1": zt1, "b1": b1, "k2": k2_,
                        "m2": m2_, "bias2": bias2, "gate2": gate2, "moe": moe, "hid2": hid2, "out2": out2, "k3": k3_,
                        "v3": v3_, "q3": q3_, "values3": values3, "scores3": scores3, "turn3": turn3,
                        "pv3": pv3, "o3": o3, "up3": up3,
                        "down3": down3, "nf_max": nf_max_, "nf": nf}
            for s in steps:
                if s[0] in handlers:
                    handlers[s[0]](*s[1:])

        @block.tensor
        def _(pe):
            mm = nc.tensor.matmul
            here = [0]

            def claim(key, *freed_by):
                n, ended = sig.next_bank(key, *freed_by)
                for event in ended:
                    pe.wait_ge(*sig.when(*event))
                return banks[n]

            def need(name, user):
                if known:
                    pe.wait_ge(*sig.when("weight_low", chunk_no[name]))
                sig.user["chunk", name] = user
                sig.last_step[name] = here[0]
                sig.first_step.setdefault(name, here[0])
                return weight(name, 0), weight(name, 1)

            def product(dst, pairs):
                passes = []
                for l_, r_ in pairs:
                    if len(r_) == 1:
                        passes += [(l_[1], r_[0]), (l_[0], r_[0])]
                    elif len(l_) == 1:
                        passes += [(l_[0], r_[1]), (l_[0], r_[0])]
                    else:
                        passes += [(l_[1], r_[0]), (l_[0], r_[1]), (l_[0], r_[0])]
                for i, (l_, r_) in enumerate(passes):
                    ins = mm(dst, l_, r_, start=i == 0, stop=i == len(passes) - 1)
                return ins

            def cols(parts, *ix):
                return [p[ix] for p in parts]

            def xt(k, c0, c1):
                return [xT[:, p, k, c0:c1] for p in range(2)]

            ALL = slice(None)

            def xt_ready(hf):
                pe.wait_ge(*sig.when("turn_low", (layer_of[hf], hf, KT - 1)))

            layer_of = {}

            def turn(layer, hf):
                layer_of[hf] = layer
                pe.wait_ge(*sig.when("ident_ready", 0))
                for c in range(KT):
                    key = (layer, hf, c)
                    bank = claim(("turn", *key), ("turn_low", key))
                    for i in range(TPH):
                        pe.wait_ge(*sig.when("normalised", (layer, hf * TPH + i)))
                        ins = nc.tensor.transpose(bank[:, i * P:(i + 1) * P], xn[:, i, c * P:(c + 1) * P], ident[:])
                    ins.then_inc(*sig.mark("turn_product", key))

            def v0_(hf, i):
                user = ("v0_product", (hf, i))
                w = [need(("v0", hf, j), user) for j in range(2)]
                p = P if i < TPH else CTX
                t, b = hf * TPH + i, hf * BPH + i - TPH
                xt_ready(hf)
                if (hf, i) == (0, TPH) and known:
                    pe.wait_ge(*sig.when("weight_low", chunk_no["ctxT"]))
                bank = claim(("v0", hf, i), ("v0_low", (hf, i)))
                pairs = []
                for k in range(KT):
                    l_ = xt(k, t * P, (t + 1) * P) if i < TPH else [ctxT[:, q, k, b * CTX:(b + 1) * CTX] for q in range(2)]
                    pairs.append((l_, [w[k // 2][q][:, k % 2] for q in range(2)]))
                product(bank[0:p, 0:G0 * HD0], pairs).then_inc(*sig.mark(*user))

            def qk(s, user, c0, c1, moving, dst):
                w = [need(("qk0", s, i), user) for i in range(2)]
                pairs = [([w[k // 2][q][:, k % 2, c0:c1] for q in range(2)], moving(k)) for k in range(KT)]
                product(dst, pairs).then_inc(*sig.mark(*user))

            def k0_(s):
                hf = s // G0
                xt_ready(hf)
                bank = claim(("k0", s), ("k0_low", s))
                qk(s, ("k0_product", s), HPG * HD0, (HPG + 1) * HD0, lambda k: xt(k, hf * HALF, (hf + 1) * HALF), bank[0:HD0])

            def kc0_(s):
                hf = s // G0
                bank = claim(("kc0", s), ("kc0_low", s))
                n = BPH * CTX
                qk(s, ("kc0_product", s), HPG * HD0, (HPG + 1) * HD0,
                   lambda k: [ctxT[:, q, k, hf * n:(hf + 1) * n] for q in range(2)], bank[0:HD0, 0:n])

            def q0_(s, h):
                hf = s // G0
                bank = claim(("q0", s, h), ("q0_low", (s, h)))
                qk(s, ("q0_product", (s, h)), h * HD0, (h + 1) * HD0, lambda k: xt(k, hf * HALF, (hf + 1) * HALF), bank[0:HD0])

            def scores0(n, s, bl, h):
                pe.wait_ge(*sig.when("q0_low", (s, h)))
                pe.wait_ge(*sig.when("k0_low", s))
                pe.wait_ge(*sig.when("kc0_low", s))
                for i in range(TPB):
                    bank = claim(("scores0", n, i), ("exp0", (n, i)))
                    l_ = [q0[:, s % 2, p, h, bl * S + i * P:bl * S + (i + 1) * P] for p in range(2)]
                    product(bank[:, 0:KEYS0], [(l_, [k0[:, s % 2, p, bl] for p in range(2)])])\
                        .then_inc(*sig.mark("scores0_product", (n, i)))

            def turn0(n, s, bl, h):
                b0 = claim(("turn0", n, 0), ("turn0_low", (n, 0)))
                b1_ = claim(("turn0", n, 1), ("turn0_low", (n, 1)))
                for i in range(TPB):
                    pe.wait_ge(*sig.when("probs0", (n, i)))
                    for k in range(2):
                        nc.tensor.transpose(b0[:, (2 * k + i) * P:(2 * k + i + 1) * P], e0[:, (2 * n + i) % E0_RING, k * P:(k + 1) * P], ident[:])
                    ins = nc.tensor.transpose(b1_[0:CTX, i * P:(i + 1) * P], e0[:, (2 * n + i) % E0_RING, S:KEYS0], ident[:])
                ins.then_inc(*sig.mark("turn0_product", n))

            def pv0(n, s, bl, h):
                g, hf = s % G0, s // G0
                pe.wait_ge(*sig.when("v0_low", (hf, TPH + BPH - 1)))
                pe.wait_ge(*sig.when("turn0_low", (n, 1)))
                bank = claim(("pv0", n), ("pv0_low", n))
                pairs = []
                for k, (t, p) in enumerate(((TPB * bl, P), (TPB * bl + 1, P), (TPH + bl, CTX))):
                    pairs.append(([v0[0:p, q, t, g * HD0:(g + 1) * HD0] for q in range(2)],
                                  [eT0[0:p, n % 2, q, k] for q in range(2)]))
                product(bank[0:HD0, 0:S], pairs).then_inc(*sig.mark("pv0_product", n))

            def o0(s, i):
                user = ("o0_product", (s, i))
                w = [need(("o0", s, j), user) for j in range(2)]
                pe.wait_ge(*sig.when("pv0_low", 8 * s + 7))
                bank = claim(("o0", s, i), ("o0_added", (s, i)))
                pairs = [([q0[:, s % 2, p, h, i * P:(i + 1) * P] for p in range(2)], [w[h // 2][p][:, h % 2] for p in range(2)])
                         for h in range(HPG)]
                product(bank[:], pairs).then_inc(*sig.mark(*user))

            def up(stage, f, hf, freed_by):
                w = fwidth(f)
                xt_ready(hf)
                for m in range(2):
                    user = (f"{stage}_product", (f, hf, m))
                    parts = need((stage, f), user)
                    bank = claim((stage, f, hf, m), freed_by[m])
                    pairs = [([q[:, m, k] for q in parts], xt(k, hf * HALF, (hf + 1) * HALF)) for k in range(KT)]
                    product(bank[0:w], pairs).then_inc(*sig.mark(*user))

            def down_chunk(stage, f, lo, user):
                first = lo + (f - lo) // 2 * 2
                if (stage, first) in chunk_no and f != first and (stage, f) not in chunk_no:
                    parts = need((stage, first), user)
                    return [q[0:fwidth(f), 1] for q in parts]
                parts = need((stage, f), user)
                return [q[0:fwidth(f), 0] for q in parts]

            def down0(part, t):
                user = ("down0_product", (part, t))
                lo, hi = (0, half_f) if part == 0 else (half_f, FT)
                pe.wait_ge(*sig.when("h0_done", 2 * hi - 1))
                bank = claim(("down0", part, t), ("down0_sum" if part else "down0_part", t))
                pairs = [([h0[0:fwidth(f), f % half_f, t * P:(t + 1) * P]], down_chunk("down0", f, lo, user))
                         for f in range(lo, hi)]
                product(bank[:], pairs).then_inc(*sig.mark(*user))

            def scores1(layer, b):
                if layer == 1:
                    keys = ctxT
                else:
                    keys = m2
                    pe.wait_ge(*sig.when("m2_low", KT - 1))
                xt_ready(b // BPH)
                reader = ("exp1", (layer, b, TPB - 1)) if layer == 1 else ("biased2", b)
                bank = claim(("scores1", layer, b), reader)
                for i in range(TPB):
                    t = TPB * b + i
                    pairs = [(xt(k, t * P, (t + 1) * P), [keys[:, q, k, b * CTX:(b + 1) * CTX] for q in range(2)])
                             for k in range(KT)]
                    ins = product(bank[:, i * CTX:(i + 1) * CTX], pairs)
                ins.then_inc(*sig.mark("scores1_product", (layer, b)))

            def pv1(layer, b):
                bank = claim(("turn1", layer, b), ("turn1_low", (layer, b)))
                for i in range(TPB):
                    pe.wait_ge(*sig.when("probs1", (layer, b, i)))
                    ins = nc.tensor.transpose(bank[0:CTX, i * P:(i + 1) * P], e1[:, b % 2, i], ident[:])
                ins.then_inc(*sig.mark("turn1_product", (layer, b)))
                pe.wait_ge(*sig.when("turn1_low", (layer, b)))
                if known:
                    pe.wait_ge(*sig.when("weight_low", chunk_no["ctxN", 1]))
                for i in range(TPB):
                    bank = claim(("pv1", layer, b, i), ("pv1_added", (layer, b, i)))
                    product(bank[:], [([eT1[:, b % 2, q, i * P:(i + 1) * P] for q in range(2)],
                                       [ctxN[:, q, b] for q in range(2)])])\
                        .then_inc(*sig.mark("pv1_product", (layer, b, i)))

            def router1():
                pe.wait_ge(*sig.when("loaded_wq1", 0))
                pe.wait_ge(*sig.when("loaded_keyT", 0))
                bank = claim(("router1",), ("router1_low", 0))
                for k in range(KT):
                    ins = mm(bank[:, k * NE:(k + 1) * NE], wq1[:, k * P:(k + 1) * P], keyT[:], start=True, stop=True)
                ins.then_inc(*sig.mark("router1_product", 0))

            def route1(t):
                pe.wait_ge(*sig.when("router1_low", 0))
                xt_ready(t // TPH)
                bank = claim(("route1", t), ("route1_rep", t))
                pairs = [(xt(k, t * P, (t + 1) * P), [rw[:, q, k] for q in range(2)]) for k in range(KT)]
                product(bank[:, 0:NE], pairs).then_inc(*sig.mark("route1_product", t))

            def z1(t):
                user = ("z1_product", t)
                w = [need(("z1", i), user) for i in range(2)]
                xt_ready(t // TPH)
                bank = claim(("z1", t), ("gated1", t))
                pairs = [(xt(k, t * P, (t + 1) * P), [w[k // 2][q][:, k % 2] for q in range(2)]) for k in range(KT)]
                product(bank[:], pairs).then_inc(*sig.mark(*user))

            def zt1(t):
                pe.wait_ge(*sig.when("gated1", t))
                bank = claim(("zt1", t), ("zt1_low", t))
                for c in range(KT):
                    ins = nc.tensor.transpose(bank[:, c * P:(c + 1) * P], zg[:, t % 2, c * P:(c + 1) * P], ident[:])
                ins.then_inc(*sig.mark("zt1_product", t))

            def b1(t):
                user = ("b1_product", t)
                w = [need(("b1", i), user) for i in range(2)]
                pe.wait_ge(*sig.when("zt1_low", t))
                bank = claim(("b1", t), ("b1_added", t))
                pairs = [([zT[:, t % 2, q, k] for q in range(2)], [w[k // 2][q][:, k % 2] for q in range(2)]) for k in range(KT)]
                product(bank[:], pairs).then_inc(*sig.mark(*user))

            def ctx_product(stage, c, moving, freed_by):
                user = (f"{stage}_product", c)
                w = [need((stage, i), user) for i in range(2)]
                if stage == "m2":
                    pe.wait_ge(*sig.when("k2_low", KT - 1))
                bank = claim((stage, c), freed_by)
                pairs = [([w[k // 2][q][:, k % 2, c * P:(c + 1) * P] for q in range(2)], [moving[:, q, k] for q in range(2)])
                         for k in range(KT)]
                product(bank[:, 0:B * CTX], pairs).then_inc(*sig.mark(*user))

            def c2_():
                pe.wait_ge(*sig.when("bq_low", 0))
                bank = claim(("c2",), ("c2_ready", 0))
                pairs = [([bqw[:, q, k] for q in range(2)], [k2[:, q, k] for q in range(2)]) for k in range(KT)]
                product(bank[:, 0:B * CTX], pairs).then_inc(*sig.mark("c2_product", 0))

            def gate2(t):
                pe.wait_ge(*sig.when("gw_low", 0))
                xt_ready(t // TPH)
                bank = claim(("gate2", t), ("logits2", t))
                pairs = [(xt(k, t * P, (t + 1) * P), [gw[:, q, k] for q in range(2)]) for k in range(KT)]
                product(bank[:, 0:4], pairs).then_inc(*sig.mark("gate2_product", t))

            def moe(part):
                if part == 3:
                    pe.wait_ge(*sig.when("choice2", 0))
                    bank = claim(("choice",), ("choice_taken", 0))
                    mm(bank[:, 0:2 * MOE * TILES], row0[:], fl[:].rearrange("p c e t -> p (c e t)"), start=True, stop=True)\
                        .then_inc(*sig.mark("choice_product", 0))
                if part:
                    return
                pe.wait_ge(*sig.when("strength", 1))
                pe.wait_ge(*sig.when("pool_gate", "row0f"))
                bank = claim(("strength",), ("moe_shift", 0))
                even = ab[:].rearrange("p (b i) -> p i b", i=TPB)
                for i, (mask, src) in enumerate(((vis, even[:, 0]), (txt, even[:, 0]), (one, even[:, 1]))):
                    ins = mm(bank[:, i * B:(i + 1) * B], mask[:], src, start=True, stop=True)
                ins.then_inc(*sig.mark("strength_product", 0))

            def hid2(e, c, hf):
                user = ("hid2_product", (e, c, hf))
                w = [need(("hid2", e, i), user) for i in range(2)]
                xt_ready(hf)
                bank = claim(("hid2", e, c, hf), ("hid2_value", (e, c, hf)))
                pairs = [([w[k // 2][q][:, k % 2, c * P:(c + 1) * P] for q in range(2)], xt(k, hf * HALF, (hf + 1) * HALF))
                         for k in range(KT)]
                product(bank[:], pairs).then_inc(*sig.mark(*user))

            def out2(e, t):
                user = ("out2_product", (e, t))
                w = [need(("out2", e, i), user) for i in range(2)]
                pe.wait_ge(*sig.when("h2_low", (e, KT - 1, t // TPH)))
                bank = claim(("out2", e, t), ("out2_added", (e, t)))
                pairs = [([h2[:, e % 2, q, k, t * P:(t + 1) * P] for q in range(2)], [w[k // 2][q][:, k % 2] for q in range(2)])
                         for k in range(KT)]
                product(bank[:], pairs).then_inc(*sig.mark(*user))

            def v3_(b):
                user = ("v3_product", b)
                w = need(("v3", 0), user)
                bank = claim(("v3", b), ("v3_low", b))
                pairs = []
                for k in range(KT):
                    pairs.append(([ctxT[:, q, k, b * CTX:(b + 1) * CTX] for q in range(2)], [w[q][:, k] for q in range(2)]))
                product(bank[0:CTX, 0:KV3 * HD3], pairs).then_inc(*sig.mark(*user))

            def q3_(c, hf):
                user = ("q3_product", (c, hf))
                w = [need(("q3", i), user) for i in range(2)]
                xt_ready(hf)
                bank = claim(("q3", c, hf), ("q3_low", (c, hf)))
                pairs = [([w[k // 2][q][:, k % 2, c * P:(c + 1) * P] for q in range(2)], xt(k, hf * HALF, (hf + 1) * HALF))
                         for k in range(KT)]
                product(bank[:], pairs).then_inc(*sig.mark(*user))

            def scores3(n, b, c):
                pe.wait_ge(*sig.when("q3_low", (c, b // BPH)))
                pe.wait_ge(*sig.when("keys3", n))
                for i in range(TPB):
                    t = TPB * b + i
                    bank = claim(("scores3", n, i), ("shift3", (n, i)))
                    product(bank[:], [([q3[:, q, c, t * P:(t + 1) * P] for q in range(2)],
                                       [kd3[:, n % 2, q].rearrange("p h k -> p (h k)") for q in range(2)])])\
                        .then_inc(*sig.mark("scores3_product", (n, i)))

            def turn3(n, b, c):
                for j in range(2):
                    bank = claim(("turn3", n, j), ("turn3_low", (n, j)))
                    for i in range(TPB):
                        pe.wait_ge(*sig.when("probs3", (n, i)))
                        for p in range(2):
                            ins = nc.tensor.transpose(bank[:, (2 * p + i) * P:(2 * p + i + 1) * P],
                                                      e3[:, n % 2, i, (2 * j + p) * P:(2 * j + p + 1) * P], ident[:])
                    ins.then_inc(*sig.mark("turn3_product", (n, j)))

            def pv3(n, b, c):
                pe.wait_ge(*sig.when("turn3_low", (n, 1)))
                pe.wait_ge(*sig.when("values3", n))
                bank = claim(("pv3", n), ("pv3_low", n))
                pairs = [([vd3[:, n % 2, q, p] for q in range(2)], [eT3[:, q, p] for q in range(2)]) for p in range(PAIRS)]
                product(bank[:, 0:S], pairs).then_inc(*sig.mark("pv3_product", n))

            def o3(t):
                user = ("o3_product", t)
                w = [need(("o3", i), user) for i in range(2)]
                pe.wait_ge(*sig.when("pv3_low", (t // TPB) * KT + KT - 1))
                bank = claim(("o3", t), ("o3_added", t))
                pairs = [([q3[:, q, k, t * P:(t + 1) * P] for q in range(2)], [w[k // 2][q][:, k % 2] for q in range(2)])
                         for k in range(KT)]
                product(bank[:], pairs).then_inc(*sig.mark(*user))

            def down3(part, t):
                user = ("down3_product", (part, t))
                lo, hi = (0, half_f) if part == 0 else (half_f, FT)
                pe.wait_ge(*sig.when("h3_low", 2 * hi - 1))
                bank = claim(("down3", part, t), ("down3_added", (part, t)))
                pairs = [([h3[0:fwidth(f), q, f % half_f, t * P:(t + 1) * P] for q in range(2)], down_chunk("down3", f, lo, user))
                         for f in range(lo, hi)]
                product(bank[:], pairs).then_inc(*sig.mark(*user))

            def nf_turn(m):
                pe.wait_ge(*sig.when("nf4_rcp", m))
                bank = claim(("nf_turn", m), ("nf4_turned", (m, 1)))
                for i in range(2):
                    ins = nc.tensor.transpose(bank[0:88, i * P:(i + 1) * P], nf_m[:, 1 + i], ident[:])
                ins.then_inc(*sig.mark("nf4_turn_product", m))

            handlers = {"turn": turn, "v0": v0_, "k0": k0_, "kc0": kc0_, "q0": q0_, "scores0": scores0, "turn0": turn0,
                        "pv0": pv0, "o0": o0, "down0": down0, "scores1": scores1, "pv1": pv1, "router1": router1,
                        "route1": route1, "z1": z1, "zt1": zt1, "b1": b1, "c2": c2_, "gate2": gate2, "moe": moe,
                        "hid2": hid2, "out2": out2, "v3": v3_, "q3": q3_, "scores3": scores3, "turn3": turn3,
                        "pv3": pv3, "o3": o3, "down3": down3, "nf_turn": nf_turn,
                        "up0": lambda f, hf: up("up0", f, hf, (("silu0", 2 * f + hf), ("inter0", 2 * f + hf))),
                        "up3": lambda f, hf: up("up3", f, hf, (("silu3", 2 * f + hf), ("h3_low", 2 * f + hf))),
                        "k2": lambda c: ctx_product("k2", c, ctxT, ("k2_low", c)),
                        "m2": lambda c: ctx_product("m2", c, k2, ("m2_low", c)),
                        "k3": lambda c: ctx_product("k3", c, ctxT, ("k3_low", c))}
            base_at = -1
            for s in steps:
                if s[0] in ("load", "split"):
                    continue
                base_at += 1
                here[0] = base_at
                if s[0] in handlers:
                    handlers[s[0]](*s[1:])

        @block.sync
        def _(sp):
            layer = {None: 8}.get(only, only)
            for hf in range(2):
                if layer == 8:
                    sp.wait_ge(*sig.when("down3_added", (1, (hf + 1) * TPH - 1)))
                else:
                    sp.wait_ge(*sig.when("x_done", (layer, hf)))
                sp.dma_start(out[:, hf * TPH:(hf + 1) * TPH], x[:, hf * TPH:(hf + 1) * TPH]).then_inc(*sig.mark("stored", hf, 16))
            sp.wait_ge(sig.sem("stored"), 32)
        return sig


def lay_out(i):
    t = np.ascontiguousarray
    d = {k: np.asarray(v) for k, v in i.items()}
    wq, wk = d["L0_xattn_Wq"], d["L0_xattn_Wk"]
    rows = [((c * HPC + h) // REP3) * HD3 + j for c in range(KT) for h in range(HPC) for j in range(HD3)]
    return {
        "x": d["x"].reshape(TILES, P, D),
        "ctx": d["ctx_4096"],
        "ctxT": t(d["ctx_4096"].reshape(B * CTX, D).T),
        "L0_wqkT": t(np.stack([np.concatenate([wq[g * HPG * HD0:(g + 1) * HPG * HD0], wk[g * HD0:(g + 1) * HD0]]).T
                               for g in range(G0)])),
        "L0_wvT": t(d["L0_xattn_Wv"].T),
        "L0_woT": t(d["L0_xattn_Wo"].T),
        "L0_wgT": t(d["L0_ffn_w_gate"].T), "L0_wuT": t(d["L0_ffn_w_up"].T), "L0_wdT": t(d["L0_ffn_w_down"].T),
        "L1_aT": t(d["L1_ffn_A_w"].T), "L1_bT": t(d["L1_ffn_B_w"].T),
        "L1_wq": d["L1_ffn_Wq_w"], "L1_keysT": t(d["L1_ffn_keys"].T),
        "L2_wkT": t(d["L2_xattn_Wk"].T), "L2_wq": d["L2_xattn_Wq"],
        "L2_bq": t(d["L2_xattn_bq"].reshape(KT, P).T), "L2_bk": t(d["L2_xattn_bk"].reshape(KT, P).T),
        "L2_gw": d["L2_ffn_gate_w"], "L2_gb": d["L2_ffn_gate_b"],
        "L2_w1": d["L2_ffn_w1"], "L2_w2": d["L2_ffn_w2"],
        "L2_b1": t(d["L2_ffn_b1"].reshape(MOE, KT, P).transpose(2, 0, 1)), "L2_b2": d["L2_ffn_b2"],
        "L3_wqT": t(d["L3_xattn_wq"].T), "L3_wkT": t(d["L3_xattn_wk"][rows].T), "L3_wvT": t(d["L3_xattn_wv"].T),
        "L3_woT": t(d["L3_xattn_wo"].T), "L3_lnw": t(d["L3_xattn_ln_w"].reshape(KT, P).T),
        "L3_w1": d["L3_ffn_w1"], "L3_w2": d["L3_ffn_w2"], "L3_w3": d["L3_ffn_w3"].reshape(P, F * D // P),
        "L3_w1T": t(d["L3_ffn_w1"].T), "L3_w2T": t(d["L3_ffn_w2"].T),
        "L3_w3T": t(d["L3_ffn_w3"].reshape(P, 4, F).transpose(2, 1, 0).reshape(F, D)),
    }


def write_program(nc, shapes, known, only=None):
    aps = {n: nc.dram_tensor(f"in_{n}", shape, FP32, kind="ExternalInput").ap() for n, shape in shapes.items()}
    aps["x"] = aps["x"].rearrange("t p d -> p t d")
    out = nc.dram_tensor("out_x", (TILES, P, D), FP32, kind="ExternalOutput").ap()
    return build(nc, aps, out.rearrange("t p d -> p t d"), known, only)


def kernel(**inputs):
    import concourse.bacc as _bacc
    from concourse.bass_utils import run_bass_kernel_spmd as _run

    arrays = lay_out(inputs)
    shapes = {n: v.shape for n, v in arrays.items()}
    counts = None
    for _ in range(2):
        nc = _bacc.Bacc("TRN2", target_bir_lowering=False, num_devices=1)
        counts = write_program(nc, shapes, counts)
    r = _run(nc, [{f"in_{n}": v for n, v in arrays.items()}], core_ids=[0])
    return np.asarray(r.results[0]["out_x"]).reshape(B, S, D)
```
